# Optimizing a Trainium2 kernel written in Bass

```python
import numpy as np
import jax
import jax.numpy as jnp

def _softmax(x, axis=-1):
    return jax.nn.softmax(x, axis=axis)

def _gelu(x):
    return jax.nn.gelu(x, approximate=True)

def _silu(x):
    return jax.nn.silu(x)

def _sigmoid(x):
    return jax.nn.sigmoid(x)

def _layernorm(x, axis=-1, eps=1e-05):
    m = jnp.mean(x, axis=axis, keepdims=True)
    v = jnp.var(x, axis=axis, keepdims=True)
    return (x - m) / jnp.sqrt(v + eps)

def _scatter_add(tgt, idx, src, axis=0):
    return tgt.at[idx].add(src)

def _segment_sum(src, seg, n):
    return jax.ops.segment_sum(src, seg, n)
kernel_name = 'mk_gnn_resnorm_d4_gnn_r32_471653'

def setup_inputs(seed: int=0):
    np.random.seed(seed)
    _w = jnp.asarray

    def _rec_inputs():
        import jax
        import jax.numpy as jnp
        _gk = jax.random.key(seed)
        x = -0.0002117 + 1 * jax.random.normal(jax.random.fold_in(_gk, 1), (3125, 256), jnp.float32)
        _s = jax.random.randint(jax.random.fold_in(_gk, 2), (25000,), 0, 3125, jnp.int32)
        _d = jax.random.randint(jax.random.fold_in(_gk, 3), (25000,), 0, 3125, jnp.int32)
        _loop = jnp.arange(3125, dtype=jnp.int32)
        src = jnp.concatenate([_s, _d, _loop])
        dst = jnp.concatenate([_d, _s, _loop])
        _o = jnp.argsort(dst, stable=True)
        src = src[_o]
        dst = dst[_o]
        edge_weight = jax.random.uniform(jax.random.fold_in(_gk, 13), (53125,), jnp.float32, 0.0, 0.999998)
        return (x, src, dst, edge_weight)
    x, src, dst, edge_weight = _rec_inputs()

    def _L0_gnn_setup():
        import jax, jax.numpy as jnp
        import numpy as np
        N, D, E = (3125, 256, 312500)
        H = 2 * D
        EPS = 0.0
        key = jax.random.key(seed)
        k1, k2, k3, k4, k5, k6, k7 = jax.random.split(key, 7)
        x = jax.random.normal(k1, (N, D), dtype=jnp.float32)
        edge_index = jax.random.randint(k2, (2, E), 0, N, dtype=jnp.int64)
        edge_weight = jax.random.uniform(k3, (E,), dtype=jnp.float32)
        s1 = 1.0 / np.sqrt(D)
        s2 = 1.0 / np.sqrt(H)
        W1 = jax.random.uniform(k4, (D, H), dtype=jnp.float32, minval=-s1, maxval=s1)
        b1 = jax.random.uniform(k5, (H,), dtype=jnp.float32, minval=-s1, maxval=s1)
        W2 = jax.random.uniform(k6, (H, D), dtype=jnp.float32, minval=-s2, maxval=s2)
        b2 = jax.random.uniform(k7, (D,), dtype=jnp.float32, minval=-s2, maxval=s2)
        return {'x': x, 'edge_index': edge_index, 'edge_weight': edge_weight, 'W1': W1, 'b1': b1, 'W2': W2, 'b2': b2}
    _L0_gnn_all = _L0_gnn_setup()
    _L0_gnn_in = {k: v for k, v in _L0_gnn_all.items() if k in ('W1', 'b1', 'W2', 'b2')}
    del _L0_gnn_all

    def _L1_gnn_setup():
        import jax, jax.numpy as jnp
        import numpy as np
        N_NODES = 3125
        N_EDGES = 50000
        IN_C, HID_C, OUT_C = (256, 128, 256)
        key = jax.random.key(seed)
        ks = jax.random.split(key, 8)
        x = jax.random.normal(ks[0], (N_NODES, IN_C), dtype=jnp.float32)
        src = jax.random.randint(ks[1], (N_EDGES,), 0, N_NODES, dtype=jnp.int64)
        dst = jnp.sort(jax.random.randint(ks[2], (N_EDGES,), 0, N_NODES, dtype=jnp.int64))
        W_conv = jax.random.normal(ks[3], (IN_C, HID_C), dtype=jnp.float32) * (2.0 / (IN_C + HID_C)) ** 0.5
        b_conv = jnp.zeros((HID_C,), dtype=jnp.float32)
        W1 = jax.random.normal(ks[4], (HID_C, HID_C), dtype=jnp.float32) * (2.0 / (2 * HID_C)) ** 0.5
        b1 = jax.random.uniform(ks[5], (HID_C,), dtype=jnp.float32, minval=-1.0, maxval=1.0) / np.sqrt(HID_C)
        W2 = jax.random.normal(ks[6], (OUT_C, HID_C), dtype=jnp.float32) * (2.0 / (HID_C + OUT_C)) ** 0.5
        b2 = jax.random.uniform(ks[7], (OUT_C,), dtype=jnp.float32, minval=-1.0, maxval=1.0) / np.sqrt(OUT_C)
        return {'x': x, 'src': src, 'dst': dst, 'W_conv': W_conv, 'b_conv': b_conv, 'W1': W1, 'b1': b1, 'W2': W2, 'b2': b2}
    _L1_gnn_all = _L1_gnn_setup()
    _L1_gnn_in = {k: v for k, v in _L1_gnn_all.items() if k in ('W_conv', 'b_conv', 'W1', 'b1', 'W2', 'b2')}
    del _L1_gnn_all

    def _L2_gnn_setup():
        import jax, jax.numpy as jnp
        import numpy as np
        N_NODES = 10000
        N_EDGES = 10000
        D = 256
        AVG_D = 3.4965
        EPS = 1e-05

        def _pna_forward(h, src_idx, dst_idx, pre_W, pre_b, post_W, post_b, mix_W, mix_b):
            n = h.shape[0]
            z = jnp.concatenate([h[src_idx], h[dst_idx]], axis=1)
            m = jax.nn.relu(z @ pre_W + pre_b)
            deg = jax.ops.segment_sum(jnp.ones((m.shape[0],), dtype=m.dtype), dst_idx, num_segments=n)
            deg_safe = jnp.maximum(deg, 1.0)[:, None]
            s = jax.ops.segment_sum(m, dst_idx, num_segments=n)
            mean = s / deg_safe
            sq_mean = jax.ops.segment_sum(m * m, dst_idx, num_segments=n) / deg_safe
            std = jnp.sqrt(jax.nn.relu(sq_mean - mean * mean) + EPS)
            has = (deg > 0)[:, None]
            mx = jnp.where(has, jax.ops.segment_max(m, dst_idx, num_segments=n), 0.0)
            mn = jnp.where(has, jax.ops.segment_min(m, dst_idx, num_segments=n), 0.0)
            agg = jnp.concatenate([mean, mx, mn, std], axis=1)
            logD = jnp.log(deg + 1.0)
            amp = (logD / AVG_D)[:, None]
            att = (AVG_D / jnp.maximum(logD, EPS))[:, None]
            scaled = jnp.concatenate([agg, agg * amp, agg * att], axis=1)
            h_cat = jnp.concatenate([h, scaled], axis=1)
            h_t = jax.nn.relu(h_cat @ post_W + post_b)
            out = jax.nn.relu(h_t @ mix_W + mix_b)
            return out
        key = jax.random.key(seed)
        ks = jax.random.split(key, 8)
        h = jax.random.normal(ks[0], (N_NODES, D), dtype=jnp.float32)
        src_idx = jax.random.randint(ks[1], (N_EDGES,), 0, N_NODES)
        dst_idx = jax.random.randint(ks[2], (N_EDGES,), 0, N_NODES)
        pre_W = jax.random.normal(ks[3], (2 * D, D), dtype=jnp.float32) * 0.02
        pre_b = jnp.zeros((D,), dtype=jnp.float32)
        post_W = jax.random.normal(ks[4], (13 * D, D), dtype=jnp.float32) * 0.02
        post_b = jnp.zeros((D,), dtype=jnp.float32)
        mix_W = jax.random.normal(ks[5], (D, D), dtype=jnp.float32) * 0.02
        mix_b = jnp.zeros((D,), dtype=jnp.float32)
        return {'h': h, 'src_idx': src_idx, 'dst_idx': dst_idx, 'pre_W': pre_W, 'pre_b': pre_b, 'post_W': post_W, 'post_b': post_b, 'mix_W': mix_W, 'mix_b': mix_b}
    _L2_gnn_all = _L2_gnn_setup()
    _L2_gnn_in = {k: v for k, v in _L2_gnn_all.items() if k in ('pre_W', 'pre_b', 'post_W', 'post_b', 'mix_W', 'mix_b')}
    del _L2_gnn_all

    def _L3_gnn_setup():
        import jax, jax.numpy as jnp
        import numpy as np
        N_NODES = 3125
        N_EDGES = 100000
        D_IN = 256
        D_OUT = 256
        key = jax.random.key(seed)
        k1, k2, k3, k4, k5, k6 = jax.random.split(key, 6)
        X = jax.random.normal(k1, (N_NODES, D_IN), dtype=jnp.float32)
        edge_src = jax.random.randint(k2, (N_EDGES,), 0, N_NODES, dtype=jnp.int32)
        edge_dst = jax.random.randint(k3, (N_EDGES,), 0, N_NODES, dtype=jnp.int32)
        edge_vals = jax.random.uniform(k4, (N_EDGES,), dtype=jnp.float32)
        W = jax.random.normal(k5, (D_IN, D_OUT), dtype=jnp.float32) * (1.0 / np.sqrt(D_IN))
        b = jax.random.normal(k6, (D_OUT,), dtype=jnp.float32) * 0.01
        return {'X': X, 'edge_src': edge_src, 'edge_dst': edge_dst, 'edge_vals': edge_vals, 'W': W, 'b': b}
    _L3_gnn_all = _L3_gnn_setup()
    _L3_gnn_in = {k: v for k, v in _L3_gnn_all.items() if k in ('W', 'b')}
    del _L3_gnn_all
    return {'x': x, 'src': src, 'dst': dst, 'edge_weight': edge_weight, 'L0_gnn_W1': _L0_gnn_in['W1'], 'L0_gnn_b1': _L0_gnn_in['b1'], 'L0_gnn_W2': _L0_gnn_in['W2'], 'L0_gnn_b2': _L0_gnn_in['b2'], 'L1_gnn_W_conv': _L1_gnn_in['W_conv'], 'L1_gnn_b_conv': _L1_gnn_in['b_conv'], 'L1_gnn_W1': _L1_gnn_in['W1'], 'L1_gnn_b1': _L1_gnn_in['b1'], 'L1_gnn_W2': _L1_gnn_in['W2'], 'L1_gnn_b2': _L1_gnn_in['b2'], 'L2_gnn_pre_W': _L2_gnn_in['pre_W'], 'L2_gnn_pre_b': _L2_gnn_in['pre_b'], 'L2_gnn_post_W': _L2_gnn_in['post_W'], 'L2_gnn_post_b': _L2_gnn_in['post_b'], 'L2_gnn_mix_W': _L2_gnn_in['mix_W'], 'L2_gnn_mix_b': _L2_gnn_in['mix_b'], 'L3_gnn_W': _L3_gnn_in['W'], 'L3_gnn_b': _L3_gnn_in['b']}

def reference(x, src, dst, edge_weight, L0_gnn_W1, L0_gnn_b1, L0_gnn_W2, L0_gnn_b2, L1_gnn_W_conv, L1_gnn_b_conv, L1_gnn_W1, L1_gnn_b1, L1_gnn_W2, L1_gnn_b2, L2_gnn_pre_W, L2_gnn_pre_b, L2_gnn_post_W, L2_gnn_post_b, L2_gnn_mix_W, L2_gnn_mix_b, L3_gnn_W, L3_gnn_b):
    import jax
    import jax.numpy as jnp

    def _L0_gnn_ref(x, edge_index, edge_weight, W1, b1, W2, b2):
        import jax, jax.numpy as jnp
        import numpy as np
        N, D, E = (3125, 256, 312500)
        H = 2 * D
        EPS = 0.0
        row, col = (edge_index[0], edge_index[1])
        messages = x[col] * edge_weight[:, None]
        agg = jax.ops.segment_sum(messages, row, num_segments=N)
        h = (1.0 + EPS) * x + agg
        h = jax.nn.relu(h @ W1 + b1)
        out = h @ W2 + b2
        return out

    def _L1_gnn_ref(x, src, dst, W_conv, b_conv, W1, b1, W2, b2):
        import jax, jax.numpy as jnp
        import numpy as np
        N_NODES = 3125
        N_EDGES = 50000
        IN_C, HID_C, OUT_C = (256, 128, 256)
        N = x.shape[0]
        ones = jnp.ones(src.shape[0], dtype=x.dtype)
        out_deg = jnp.clip(jax.ops.segment_sum(ones, src, num_segments=N), 1.0)
        in_deg = jnp.clip(jax.ops.segment_sum(ones, dst, num_segments=N), 1.0)
        h = x * jax.lax.rsqrt(out_deg)[:, None]
        h = h @ W_conv
        m = jax.ops.segment_sum(h[src], dst, num_segments=N, indices_are_sorted=True)
        h = m * jax.lax.rsqrt(in_deg)[:, None] + b_conv
        h = jax.nn.relu(h)
        h = jax.nn.relu(h @ W1.T + b1)
        return h @ W2.T + b2

    def _L2_gnn_ref(h, src_idx, dst_idx, pre_W, pre_b, post_W, post_b, mix_W, mix_b):
        import jax, jax.numpy as jnp
        import numpy as np
        N_NODES = 10000
        N_EDGES = 10000
        D = 256
        AVG_D = 3.4965
        EPS = 1e-05

        def _pna_forward(h, src_idx, dst_idx, pre_W, pre_b, post_W, post_b, mix_W, mix_b):
            n = h.shape[0]
            z = jnp.concatenate([h[src_idx], h[dst_idx]], axis=1)
            m = jax.nn.relu(z @ pre_W + pre_b)
            deg = jax.ops.segment_sum(jnp.ones((m.shape[0],), dtype=m.dtype), dst_idx, num_segments=n)
            deg_safe = jnp.maximum(deg, 1.0)[:, None]
            s = jax.ops.segment_sum(m, dst_idx, num_segments=n)
            mean = s / deg_safe
            sq_mean = jax.ops.segment_sum(m * m, dst_idx, num_segments=n) / deg_safe
            std = jnp.sqrt(jax.nn.relu(sq_mean - mean * mean) + EPS)
            has = (deg > 0)[:, None]
            mx = jnp.where(has, jax.ops.segment_max(m, dst_idx, num_segments=n), 0.0)
            mn = jnp.where(has, jax.ops.segment_min(m, dst_idx, num_segments=n), 0.0)
            agg = jnp.concatenate([mean, mx, mn, std], axis=1)
            logD = jnp.log(deg + 1.0)
            amp = (logD / AVG_D)[:, None]
            att = (AVG_D / jnp.maximum(logD, EPS))[:, None]
            scaled = jnp.concatenate([agg, agg * amp, agg * att], axis=1)
            h_cat = jnp.concatenate([h, scaled], axis=1)
            h_t = jax.nn.relu(h_cat @ post_W + post_b)
            out = jax.nn.relu(h_t @ mix_W + mix_b)
            return out
        return _pna_forward(h, src_idx, dst_idx, pre_W, pre_b, post_W, post_b, mix_W, mix_b)

    def _L3_gnn_ref(X, edge_src, edge_dst, edge_vals, W, b):
        import jax, jax.numpy as jnp
        import numpy as np
        N_NODES = 3125
        N_EDGES = 100000
        D_IN = 256
        D_OUT = 256
        msgs = edge_vals[:, None] * X[edge_src]
        H = jax.ops.segment_sum(msgs, edge_dst, num_segments=N_NODES)
        H = jnp.dot(H, W) + b
        return jax.nn.relu(H)
    edge_index = jnp.stack([src, dst])
    x = _layernorm(x + _L0_gnn_ref(x, edge_index, edge_weight, L0_gnn_W1, L0_gnn_b1, L0_gnn_W2, L0_gnn_b2), axis=-1)
    x = _layernorm(x + _L1_gnn_ref(x, src, dst, L1_gnn_W_conv, L1_gnn_b_conv, L1_gnn_W1, L1_gnn_b1, L1_gnn_W2, L1_gnn_b2), axis=-1)
    x = _layernorm(x + _L2_gnn_ref(x, src, dst, L2_gnn_pre_W, L2_gnn_pre_b, L2_gnn_post_W, L2_gnn_post_b, L2_gnn_mix_W, L2_gnn_mix_b), axis=-1)
    x = _layernorm(x + _L3_gnn_ref(x, src, dst, edge_weight, L3_gnn_W, L3_gnn_b), axis=-1)
    return x

_drawn_inputs = setup_inputs


def setup_inputs(seed=0):
    import zlib

    import numpy as np

    out = dict(_drawn_inputs(seed))
    spreads = {'L1_gnn_b_conv': (0.0, 0.1),
     'L2_gnn_pre_b': (0.0, 0.44),
     'L2_gnn_post_b': (0.0, 0.333),
     'L2_gnn_mix_b': (0.0, 0.1)}
    factors = {'L0_gnn_b1': 2.743, 'L3_gnn_b': 8.0}
    for name, (base, spread) in spreads.items():
        noise = np.random.default_rng([zlib.crc32(name.encode()), seed]).standard_normal(out[name].shape)
        drawn = base * np.exp(spread * noise) if base else spread * noise
        out[name] = jnp.asarray(drawn.astype(out[name].dtype))
    for name, factor in factors.items():
        out[name] = (out[name] * factor).astype(out[name].dtype)
    return out
```

```python
from contextlib import ExitStack

import concourse.bass as bass
from concourse import mybir
from concourse.bass import IndirectOffsetOnAxis, ds

F32, I32, BF16 = mybir.dt.float32, mybir.dt.int32, mybir.dt.bfloat16
ALU, ACT, AX = mybir.AluOpType, mybir.ActivationFunctionType, mybir.AxisListType

P = 128
N, E, D = 3125, 53125, 256
HID0, HID1 = 512, 128
NT = -(-N // P)
NP = NT * P
GT = 5
NG = NT // GT
EC = -(-E // P)
EP = EC * P
K = 40
RND = 2
SLOTS = RND * GT
HALF = K // RND
PAD = NP
DUMMY = NP * NP
KEY = 4096
KEYCAP = 2047
CH = 32
NCH = EC // CH
DT0 = 13
BLK = 400
NB = NP // BLK
WR = 4
GW = GT * D
EPS, AVG_D = 1e-5, 3.4965
LOW = -1e30
assert NP * NP + SLOTS * P < 1 << 24 and NCH * CH == EC and NG * GT == NT and NB * BLK == NP


class Steps:

    def __init__(self, engine, sem, base=0, spacer=None):
        self.engine, self.sem, self.base, self.n, self.spacer = engine, sem, base, 0, spacer

    def __call__(self, instruction):
        self.n += 1
        return instruction.then_inc(self.sem, 1)

    def settle(self):
        value = self.base + self.n
        if self.spacer is not None:
            value = self.engine.snap(self.engine.to_reg(value), min_val=1, max_val=1 << 30)
            self.engine.wait_ge(*self.spacer)
        self.engine.wait_ge(self.sem, value)


def build(nc, x, xT, src, dst, w, L0_W1, L0_b1, L0_W2, L0_b2, L1_Wc, L1_bc, L1_W1T, L1_b1, L1_W2T, L1_b2,
          L2_preW, L2_preb, L2_postW, L2_postb, L2_mixW, L2_mixb, L3_W, L3_b, out):
    def dram(name, shape, dt):
        return nc.dram_tensor(name, shape, dt, kind="Internal").ap()

    edges = dram("edges", (EP, 2), I32)
    keys_dram = dram("keys_dram", (1, NP), F32)
    ranked_dram = dram("ranked_dram", (NP, 4), I32)
    dense = dram("dense", (NP * NP + SLOTS * P, 1), F32)
    x1_dram = dram("x1_dram", (NP, D), F32)
    h1_dram = dram("h1_dram", (NP + 1, HID1), F32)
    p2_dram = dram("p2_dram", (NP + 1, D), F32)
    x3_dram = dram("x3_dram", (NP + 1, D), F32)

    whole = ExitStack()
    with whole:
        def maker(stack):
            return lambda name, shape, dt=F32: stack.enter_context(nc.sbuf_tensor(name, shape, dt))

        sb = maker(whole)

        used_sems = []

        def sem(name):
            used_sems.append(nc.alloc_semaphore(name))
            return used_sems[-1]

        def recycle_sems():
            nc.clear_and_free_semaphores(used_sems[1:])
            del used_sems[1:]
            nc.all_engine_barrier()

        banks = whole.enter_context(nc.psum_tensor("banks", [P, 8, 512], F32))

        ident = sb("ident", [P, P])
        node_of_rank = sb("node_of_rank", [P, NT, 4], I32)
        deg_rank = sb("deg_rank", [P, NT])
        iters = sb("iters", [P, 2 * NG], I32)
        slot_k = sb("slot_k", [P, K])
        tab_edge = sb("tab_edge", [P, NT, K, 2], I32)
        tab_once = sb("tab_once", [P, NT, K, 2], I32)
        tab_dense = tab_once
        tab_pna = tab_once
        row_base = sb("row_base", [P, NT])
        dummy_at = sb("dummy_at", [P, GT, K])
        out_scale = sb("out_scale", [P, NT])
        stage = sb("stage", [P, RND, GT, 2], I32)
        more = sb("more", [P, GT, K, 2], I32)
        more_f = sb("more_f", [P, 3, GT, K])
        more_at = sb("more_at", [P, 3, GT])
        more_idx = sb("more_idx", [P, GT], I32)
        big_a = sb("big_a", [P, NT * D])
        big_b = sb("big_b", [P, NT * D])
        big_c = sb("big_c", [P, NT * D])
        zrow = sb("zrow", [1, D])
        lowrow = sb("lowrow", [1, D])
        bn = sb("bn", [P, GT, 6])
        mv = sb("mv", [P, GT, 2])
        rstd = sb("rstd", [P, GT])
        dev = sb("dev", [P, GT])
        eps = sb("eps", [P, 1])

        const_step = sem("const_step")
        CONSTS = 10

        def hold(engine, semaphore, value):
            if not isinstance(value, int):
                value = engine.snap(engine.to_reg(value), min_val=1, max_val=1 << 30)
                engine.wait_ge(const_step, CONSTS)
            engine.wait_ge(semaphore, value)

        def layer_norm(dve, steps, y, to, signal, g, var_ready, std_ready):
            steps.settle()
            for i in range(GT):
                steps(nc.vector.bn_stats(bn[:, i, :], y(i)))
            steps.settle()
            for i in range(GT):
                last = nc.vector.bn_aggr(mv[:, i, :], bn[:, i, :])
            last.then_inc(var_ready, 1)
            hold(dve, std_ready, g + 1)
            steps(nc.vector.reciprocal(rstd[:, :], dev[:, :]))
            steps.settle()
            for i in range(GT):
                signal(i, nc.vector.tensor_scalar(to(i), y(i), mv[:, i, 0:1], rstd[:, i:i + 1],
                                                  ALU.subtract, ALU.mult))

        def deviation(act, g, var_ready, std_ready):
            hold(act, var_ready, g + 1)
            nc.scalar.activation(dev[:, :], mv[:, :, 1], ACT.Sqrt, bias=eps[:, :]).then_inc(std_ready, 1)

        def gather(to, table, index):
            return nc.gpsimd.indirect_dma_start(to, None, table, IndirectOffsetOnAxis(ap=index, axis=0))

        def scatter(table, index, rows, **how):
            return nc.gpsimd.indirect_dma_start(table, IndirectOffsetOnAxis(ap=index, axis=0), rows, None, **how)

        prep = ExitStack()
        psb = maker(prep)
        onehot_lo = psb("onehot_lo", [P, 2, CH, P], BF16)
        onehot_hi = psb("onehot_hi", [P, EC, NT], BF16)
        iota_lo = psb("iota_lo", [P, P], BF16)
        iota_hi = psb("iota_hi", [P, NT], BF16)
        end_i = psb("end_i", [P, 2, EC], I32)
        half_i = psb("half_i", [P, EC], I32)
        hi_b = psb("hi_b", [P, EC], BF16)
        lo_b = psb("lo_b", [P, EC], BF16)
        zeros = psb("zeros", [P, NP])
        tmp = ExitStack()
        tsb = maker(tmp)
        w_in = tsb("w_in", [P, EC])
        pairs = tsb("pairs", [P, EC, 2], I32)
        before = tsb("before", [P, P])
        ones = tsb("ones", [P, P])
        node_id = tsb("node_id", [P, NT])
        deg = tsb("deg", [P, NT])
        total = tsb("total", [P, NT])
        running = tsb("running", [P, NT])
        first = tsb("first", [P, NT])
        key = tsb("key", [P, NT])
        neg_key = tsb("neg_key", [P, NT])
        key_t = tsb("key_t", [NT, P])
        key_row = tsb("key_row", [P, NP])
        junk = tsb("junk", [P, 2, NP], BF16)
        rank = tsb("rank", [P, NT])
        rank_i = tsb("rank_i", [P, NT], I32)
        ranked = tsb("ranked", [P, NT, 4], I32)
        valid = tsb("valid", [P, NT, K])
        srcf = tsb("srcf", [P, NT, K])
        work = tsb("work", [P, NT, K])
        gmax = tsb("gmax", [P, NG])
        gmax_all = tsb("gmax_all", [P, NG])
        gmax_i = tsb("gmax_i", [P, NG], I32)

        ends_in, w_read, edges_out = sem("ends_in"), sem("w_read"), sem("edges_out")
        zero_set, dense_zero = sem("zero_set"), sem("dense_zero")
        prep_step, hot_ready, hot_used = sem("prep_step"), sem("hot_ready"), sem("hot_used")
        hist_done, deg_ready, pre_done = sem("hist_done"), sem("deg_ready"), sem("pre_done")
        key_ready, keyt_done, keyt_ready = sem("key_ready"), sem("keyt_done"), sem("keyt_ready")
        key_out, key_in, act_rank, ranked_ready = sem("key_out"), sem("key_in"), sem("act_rank"), sem("ranked_ready")
        ranked_out, ranked_in, runs_in = sem("ranked_out"), sem("ranked_in"), sem("runs_in")
        gmax_ready, gmax_done, pads_out, pair_ready = sem("gmax_ready"), sem("gmax_done"), sem("pads_out"), sem("pair_ready")
        neg_ready = sem("neg_ready")

        def one_hots(dve, steps, which, base):
            end = end_i[:, which, :]
            steps(nc.vector.tensor_scalar(half_i[:, :], end, 7, None, ALU.arith_shift_right))
            steps.settle()
            steps(nc.vector.tensor_copy(hi_b[:, :], half_i[:, :]))
            steps.settle()
            steps(nc.vector.tensor_scalar(half_i[:, :], end, P - 1, None, ALU.bitwise_and))
            steps.settle()
            steps(nc.vector.tensor_copy(lo_b[:, :], half_i[:, :]))
            steps(nc.vector.tensor_tensor(onehot_hi[:, :, :], hi_b[:, :, None].to_broadcast([P, EC, NT]),
                                          iota_hi[:, None, :].to_broadcast([P, EC, NT]), ALU.is_equal))
            steps.settle()
            for c in range(NCH):
                if base + c >= 2:
                    dve.wait_ge(hot_used, base + c - 1)
                at = slice(c * CH, (c + 1) * CH)
                nc.vector.tensor_tensor(onehot_lo[:, (base + c) % 2, :, :], lo_b[:, at, None].to_broadcast([P, CH, P]),
                                        iota_lo[:, None, :].to_broadcast([P, CH, P]), ALU.is_equal).then_inc(hot_ready, 1)

        def count_ends(pe, hist, base):
            for c in range(NCH):
                pe.wait_ge(hot_ready, base + c + 1)
                for e in range(CH):
                    at = c * CH + e
                    last = nc.tensor.matmul(hist, onehot_lo[:, (base + c) % 2, e, :], onehot_hi[:, at, :],
                                            start=at == 0, stop=at == EC - 1)
                last.then_inc(hot_used, 1)

        with nc.Block() as block:
            @block.sync
            def _(sp):
                sp.dma_start(end_i[:, 0, :], dst).then_inc(ends_in, 16)
                sp.dma_start(end_i[:, 1, :], src).then_inc(w_read, 16)
                sp.dma_start(w_in[:, :], w).then_inc(w_read, 16)
                sp.wait_ge(zero_set, 3)
                sp.dma_start(h1_dram[NP:NP + 1, :], zrow[:, 0:HID1]).then_inc(pads_out, 16)
                sp.dma_start(x3_dram[NP:NP + 1, :], zrow[:, :]).then_inc(pads_out, 16)
                sp.dma_start(p2_dram[NP:NP + 1, :], lowrow[:, :]).then_inc(pads_out, 16)
                sp.wait_ge(pair_ready, 2)
                sp.dma_start(edges.rearrange("(p c) two -> p (c two)", p=P),
                             pairs[:, :, :].rearrange("p c two -> p (c two)")).then_inc(edges_out, 16)
                rows = dense[0:NP * NP, :].rearrange("(t p s) o -> t p (s o)", p=P, s=NP)
                for t in range(6):
                    sp.dma_start(rows[t], zeros[:, :]).then_inc(dense_zero, 16)
                sp.wait_ge(keyt_ready, 1)
                sp.dma_start(keys_dram.rearrange("o (t p) -> (o t) p", p=P), key_t[:, :]).then_inc(key_out, 16)
                sp.wait_ge(key_out, 16)
                sp.dma_start(key_row[:, :], keys_dram.to_broadcast([P, NP])).then_inc(key_in, 16)
                for t in range(6, NT):
                    sp.dma_start(rows[t], zeros[:, :]).then_inc(dense_zero, 16)
                sp.dma_start(dense[NP * NP:, :].rearrange("(p c) o -> p (c o)", p=P),
                             zeros[:, 0:SLOTS]).then_inc(dense_zero, 16)
                sp.wait_ge(pads_out, 48)
                sp.wait_ge(edges_out, 16)
                sp.wait_ge(dense_zero, 16 * (NT + 1))

            @block.gpsimd
            def _(pool):
                c = Steps(pool, const_step)
                c(nc.gpsimd.memset(eps[:, :], EPS))
                nc.gpsimd.memset(zeros[:, :], 0.0).then_inc(zero_set, 1)
                nc.gpsimd.memset(zrow[:, :], 0.0).then_inc(zero_set, 1)
                nc.gpsimd.memset(lowrow[:, :], LOW).then_inc(zero_set, 1)
                c(nc.gpsimd.iota(iota_lo[:, :], [[1, P]], base=0, channel_multiplier=0,
                                 allow_small_or_imprecise_dtypes=True))
                c(nc.gpsimd.iota(iota_hi[:, :], [[1, NT]], base=0, channel_multiplier=0,
                                 allow_small_or_imprecise_dtypes=True))
                c(nc.gpsimd.iota(node_id[:, :], [[P, NT]], base=0, channel_multiplier=1,
                                 allow_small_or_imprecise_dtypes=True))
                c(nc.gpsimd.memset(ones[:, :], 1.0))
                c(nc.gpsimd.memset(ident[:, :], 1.0))
                c.settle()
                c(nc.gpsimd.affine_select(out=before[:, :], in_=ones[:, :], compare_op=ALU.is_gt, fill=0.0,
                                          base=0, pattern=[[1, P]], channel_multiplier=-1))
                c(nc.gpsimd.affine_select(out=ident[:, :], in_=ident[:, :], compare_op=ALU.is_equal, fill=0.0,
                                          base=0, pattern=[[1, P]], channel_multiplier=-1))
                c(nc.gpsimd.iota(slot_k[:, :], [[1, K]], base=0, channel_multiplier=0,
                                 allow_small_or_imprecise_dtypes=True))
                c(nc.gpsimd.iota(dummy_at[:, :, :], [[RND * P, GT], [0, K // RND], [P, RND]], base=DUMMY,
                                 channel_multiplier=1, allow_small_or_imprecise_dtypes=True))
                pool.wait_ge(w_read, 32)
                nc.gpsimd.tensor_copy(pairs[:, :, 0], end_i[:, 1, :]).then_inc(pair_ready, 1)
                nc.gpsimd.tensor_copy(pairs[:, :, 1].bitcast(F32), w_in[:, :]).then_inc(pair_ready, 1)
                pool.wait_ge(ranked_ready, 1)
                for t in range(NT):
                    scatter(ranked_dram, rank_i[:, t:t + 1], ranked[:, t, :]).then_inc(ranked_out, 16)
                pool.wait_ge(ranked_out, 16 * NT)
                pool.dma_start(node_of_rank[:, :, :], ranked_dram.rearrange("(t p) f -> p t f", p=P)).then_inc(ranked_in, 16)
                pool.wait_ge(ranked_in, 16)
                pool.wait_ge(edges_out, 16)
                for t in range(NT):
                    gather(tab_edge[:, t, :, :].rearrange("p k two -> p (k two)"), edges,
                           node_of_rank[:, t, 1:2]).then_inc(runs_in, 16)
                pool.wait_ge(gmax_ready, 1)
                nc.gpsimd.partition_all_reduce(gmax_all[:, :], gmax[:, :], P, bass.bass_isa.ReduceOp.max
                                               ).then_inc(gmax_done, 1)

            @block.tensor
            def _(pe):
                hist, prefix, totals, keyt = banks[:, 0, 0:NT], banks[:, 1, 0:NT], banks[:, 2, 0:NT], banks[0:NT, 3, 0:P]
                count_ends(pe, hist, 0)
                pe.wait_ge(const_step, CONSTS)
                pe.wait_ge(deg_ready, 1)
                nc.tensor.matmul(prefix, before[:, :], deg[:, :], start=True, stop=True)
                nc.tensor.matmul(totals, ones[:, :], deg[:, :], start=True, stop=True).then_inc(pre_done, 1)
                pe.wait_ge(key_ready, 1)
                nc.tensor.transpose(keyt, key[:, :], ident[:, :]).then_inc(keyt_done, 1)

            @block.scalar
            def _(act):
                act.wait_ge(key_in, 16)
                act.wait_ge(neg_ready, 1)
                for t in range(DT0, NT):
                    nc.scalar.activation(junk[:, 1, :], key_row[:, :], ACT.Sign, bias=neg_key[:, t:t + 1],
                                         accum_out=rank[:, t:t + 1]).then_inc(act_rank, 1)
                    act.wait_ge(act_rank, t - DT0 + 1)

            @block.vector
            def _(dve):
                s = Steps(dve, prep_step)
                dve.wait_ge(ends_in, 16)
                dve.wait_ge(const_step, 3)
                one_hots(dve, s, 0, 0)
                dve.wait_ge(hot_used, NCH)
                nc.vector.tensor_copy(deg[:, :], banks[:, 0, 0:NT]).then_inc(deg_ready, 1)
                dve.wait_ge(deg_ready, 1)
                dve.wait_ge(const_step, CONSTS)
                s(nc.vector.tensor_scalar(key[:, :], deg[:, :], float(KEYCAP), float(KEY), ALU.min, ALU.mult))
                s.settle()
                nc.vector.tensor_tensor(key[:, :], key[:, :], node_id[:, :], ALU.add).then_inc(key_ready, 1)
                dve.wait_ge(key_ready, 1)
                nc.vector.tensor_scalar(neg_key[:, :], key[:, :], -1.0, -0.5, ALU.mult, ALU.add).then_inc(neg_ready, 1)
                dve.wait_ge(keyt_done, 1)
                nc.vector.tensor_copy(key_t[:, :], banks[0:NT, 3, 0:P]).then_inc(keyt_ready, 1)
                dve.wait_ge(pre_done, 1)
                s(nc.vector.tensor_copy(total[:, :], banks[:, 2, 0:NT]))
                s.settle()
                dve.wait_ge(zero_set, 1)
                s(nc.vector.tensor_tensor_scan(running[:, :], total[:, :], zeros[:, 0:NT], 0.0, ALU.add, ALU.add))
                s.settle()
                s(nc.vector.tensor_tensor(running[:, :], running[:, :], total[:, :], ALU.subtract))
                s.settle()
                s(nc.vector.tensor_tensor(first[:, :], running[:, :], banks[:, 1, 0:NT], ALU.add))
                s.settle()
                s(nc.vector.tensor_copy(ranked[:, :, 0], node_id[:, :]))
                s(nc.vector.tensor_copy(ranked[:, :, 1], first[:, :]))
                s(nc.vector.tensor_copy(ranked[:, :, 2], deg[:, :]))
                s(nc.vector.memset(ranked[:, :, 3], 0))
                dve.wait_ge(key_in, 16)
                for t in range(DT0):
                    s(nc.vector.tensor_scalar(junk[:, 0, :], key_row[:, :], key[:, t:t + 1], 0.0, ALU.is_gt, ALU.add,
                                              accum_out=rank[:, t:t + 1]))
                    s.settle()
                dve.wait_ge(act_rank, NT - DT0)
                s(nc.vector.tensor_scalar(rank[:, DT0:NT], rank[:, DT0:NT], float(NP), 0.5, ALU.add, ALU.mult))
                s.settle()
                nc.vector.tensor_copy(rank_i[:, :], rank[:, :]).then_inc(ranked_ready, 1)
                dve.wait_ge(ranked_in, 16)
                s(nc.vector.tensor_copy(deg_rank[:, :], node_of_rank[:, :, 2]))
                s.settle()
                nc.vector.tensor_reduce(gmax[:, :], deg_rank[:, :].rearrange("p (g t) -> p g t", t=GT), AX.X,
                                        ALU.max).then_inc(gmax_ready, 1)
                s(nc.vector.tensor_tensor(valid[:, :, :], slot_k[:, None, :].to_broadcast([P, NT, K]),
                                          deg_rank[:, :, None].to_broadcast([P, NT, K]), ALU.is_lt))
                s(nc.vector.tensor_scalar(row_base[:, :], node_id[:, :], float(NP), None, ALU.mult))
                dve.wait_ge(runs_in, 16 * NT)
                s.settle()
                s(nc.vector.tensor_copy(srcf[:, :, :], tab_edge[:, :, :, 0]))
                s.settle()
                s(nc.vector.tensor_scalar(work[:, :, :], srcf[:, :, :], float(-PAD), None, ALU.add))
                s.settle()
                s(nc.vector.tensor_tensor(work[:, :, :], work[:, :, :], valid[:, :, :], ALU.mult))
                s.settle()
                s(nc.vector.tensor_scalar(tab_edge[:, :, :, 0], work[:, :, :], float(PAD), None, ALU.add))
                s.settle()
                s(nc.vector.tensor_tensor(tab_edge[:, :, :, 1].bitcast(F32), tab_edge[:, :, :, 1].bitcast(F32),
                                          valid[:, :, :], ALU.mult))
                s(nc.vector.tensor_tensor(srcf[:, :, :], srcf[:, :, :], row_base[:, :, None].to_broadcast([P, NT, K]),
                                          ALU.add))
                s.settle()
                s(nc.vector.tensor_copy(tab_dense[:, :, :, 1], tab_edge[:, :, :, 1]))
                for g in range(NG):
                    at = slice(g * GT, (g + 1) * GT)
                    s(nc.vector.tensor_tensor(srcf[:, at, :], srcf[:, at, :], dummy_at[:, :, :], ALU.subtract))
                s.settle()
                s(nc.vector.tensor_tensor(srcf[:, :, :], srcf[:, :, :], valid[:, :, :], ALU.mult))
                s.settle()
                for g in range(NG):
                    at = slice(g * GT, (g + 1) * GT)
                    s(nc.vector.tensor_tensor(tab_dense[:, at, :, 0], srcf[:, at, :], dummy_at[:, :, :], ALU.add))
                dve.wait_ge(gmax_done, 1)
                s(nc.vector.tensor_copy(gmax_i[:, :], gmax_all[:, :]))
                s.settle()
                s(nc.vector.tensor_scalar(gmax_i[:, :], gmax_i[:, :], RND - 1, None, ALU.add))
                s.settle()
                s(nc.vector.tensor_scalar(gmax_i[:, :], gmax_i[:, :], 1, None, ALU.arith_shift_right))
                s.settle()
                s(nc.vector.tensor_scalar(iters[:, 0:NG], gmax_i[:, :], 1, None, ALU.max))
                s.settle()
                s(nc.vector.tensor_scalar(gmax_i[:, :], iters[:, 0:NG], HALF, None, ALU.is_le))
                s.settle()
                s(nc.vector.tensor_tensor(iters[:, NG:2 * NG], iters[:, 0:NG], gmax_i[:, :], ALU.mult))
        tmp.close()

        RELOAD_STEPS = {"edge": 16, "pna": 16, "dense": 18}

        def reload_table(pool, table, kind, g, loads, reloaded, more_in):
            s = Steps(pool, reloaded, loads * RELOAD_STEPS[kind], (const_step, CONSTS))
            first, left, done = more_at[:, 0, :], more_at[:, 1, :], more_at[:, 2, :]
            tiles = ds(g * GT, GT)
            s(nc.gpsimd.tensor_copy(first, node_of_rank[:, tiles, 1]))
            s(nc.gpsimd.tensor_copy(left, node_of_rank[:, tiles, 2]))
            s.settle()
            s(nc.gpsimd.tensor_tensor(first, first, done, ALU.add))
            s(nc.gpsimd.tensor_tensor(left, left, done, ALU.subtract))
            s.settle()
            s(nc.gpsimd.tensor_scalar(first, first, float(EP - K), None, ALU.min))
            s(nc.gpsimd.tensor_scalar(done, done, float(K), None, ALU.add))
            s.settle()
            s(nc.gpsimd.tensor_copy(more_idx[:, :], first))
            s.settle()
            for i in range(GT):
                gather(more[:, i, :, :].rearrange("p k two -> p (k two)"), edges, more_idx[:, i:i + 1]).then_inc(more_in, 16)
            hold(pool, more_in, loads * (16 * GT) + 16 * GT)
            source, ok = more_f[:, 0, :, :], more_f[:, 1, :, :]
            s(nc.gpsimd.tensor_copy(source, more[:, :, :, 0]))
            s(nc.gpsimd.tensor_tensor(ok, left[:, :, None].to_broadcast([P, GT, K]),
                                      slot_k[:, None, :].to_broadcast([P, GT, K]), ALU.subtract))
            s.settle()
            s(nc.gpsimd.tensor_scalar(ok, ok, 0.0, 1.0, ALU.max, ALU.min))
            s.settle()
            if kind == "dense":
                s(nc.gpsimd.tensor_copy(more_f[:, 2, :, 0], row_base[:, tiles]))
                s.settle()
                s(nc.gpsimd.tensor_tensor(source, source, more_f[:, 2, :, 0:1].to_broadcast([P, GT, K]), ALU.add))
                s.settle()
                s(nc.gpsimd.tensor_tensor(source, source, dummy_at[:, :, :], ALU.subtract))
                s.settle()
                s(nc.gpsimd.tensor_tensor(source, source, ok, ALU.mult))
                s.settle()
                s(nc.gpsimd.tensor_tensor(source, source, dummy_at[:, :, :], ALU.add))
                s.settle()
            else:
                s(nc.gpsimd.tensor_scalar(source, source, float(-PAD), None, ALU.add))
                s.settle()
                s(nc.gpsimd.tensor_tensor(source, source, ok, ALU.mult))
                s.settle()
                s(nc.gpsimd.tensor_scalar(source, source, float(PAD), None, ALU.add))
                s.settle()
            s(nc.gpsimd.tensor_copy(more[:, :, :, 0], source))
            value = more[:, :, :, 1].bitcast(F32)
            if kind == "pna":
                s(nc.gpsimd.tensor_scalar(value, ok, 2 * LOW, -2 * LOW, ALU.mult, ALU.add))
            else:
                s(nc.gpsimd.tensor_tensor(value, value, ok, ALU.mult))
            s.settle()
            s(nc.gpsimd.tensor_copy(table[:, tiles, :, :], more[:, :, :, :]))
            s.settle()
            assert s.n == RELOAD_STEPS[kind], s.n

        def pool_rounds(pool, name, table, kind, before_round, issue, after_group=None):
            staged, reloaded = sem(f"{name}_staged"), sem(f"{name}_reloaded")
            phase_reset, more_in = sem(f"{name}_reset"), sem(f"{name}_more_in")
            it_reg, pos_reg, room_reg, load_reg = (pool.alloc_register(f"{name}_{r}") for r in
                                                   ("it", "pos", "room", "loads"))
            pool.reg_mov(it_reg, 0)
            pool.reg_mov(load_reg, 0)
            with pool.Fori(0, NG) as g:
                nc.gpsimd.memset(more_at[:, 2, :], 0.0).then_inc(phase_reset, 1)
                hold(pool, phase_reset, g + 1)
                count = pool.value_load(iters[0:1, ds(g, 1)], min_val=1, max_val=E)
                pool.reg_load(room_reg, iters[0:1, ds(g + NG, 1)])
                pool.reg_mov(pos_reg, 0)
                with pool.Fori(0, count):
                    room = pool.snap(room_reg, min_val=0, max_val=E)
                    with pool.If(room == 0):
                        loads = pool.snap(load_reg, min_val=0, max_val=E)
                        reload_table(pool, table, kind, g, loads, reloaded, more_in)
                        pool.reg_add(load_reg, load_reg, 1)
                        pool.reg_mov(room_reg, HALF)
                        pool.reg_mov(pos_reg, 0)
                    pool.reg_sub(room_reg, room_reg, 1)
                    pos = pool.snap(pos_reg, min_val=0, max_val=HALF - 1)
                    it = pool.snap(it_reg, min_val=0, max_val=NG * E)
                    for r in range(RND):
                        before_round(it, r)
                        nc.gpsimd.tensor_copy(stage[:, r, :, :],
                                              table[:, ds(g * GT, GT), ds(pos * RND + r, 1), :]
                                              .rearrange("p t o two -> p (t o) two")).then_inc(staged, 1)
                        hold(pool, staged, it * RND + r + 1)
                        for i in range(GT):
                            issue(it, r, i)
                    pool.reg_add(it_reg, it_reg, 1)
                    pool.reg_add(pos_reg, pos_reg, 1)
                if after_group is not None:
                    after_group(pool.snap(it_reg, min_val=1, max_val=NG * E), g)

        def rounds(engine, name, body, before_group=None, after_group=None):
            it_reg = engine.alloc_register(f"{name}_it")
            engine.reg_mov(it_reg, 0)
            with engine.Fori(0, NG) as g:
                count = engine.value_load(iters[0:1, ds(g, 1)], min_val=1, max_val=E)
                if before_group is not None:
                    before_group(g, engine.snap(it_reg, min_val=0, max_val=NG * E))
                with engine.Fori(0, count):
                    body(g, engine.snap(it_reg, min_val=0, max_val=NG * E))
                    engine.reg_add(it_reg, it_reg, 1)
                if after_group is not None:
                    after_group(g, engine.snap(it_reg, min_val=1, max_val=NG * E))

        ph = ExitStack()
        psb1 = maker(ph)
        wt = psb1("wt", [P, WR, GT, BLK])
        xrank_in, group_built = sem("xrank_in"), sem("group_built")
        slot_done = [[sem(f"slot_done{r}{i}") for i in range(GT)] for r in range(RND)]
        block_in = [sem(f"block_in{i}") for i in range(WR)]
        half_done, agg_done, xt_in, out_deg_ready, out_dev_ready, step1 = (sem(n) for n in (
            "half_done", "agg_done", "xt_in", "out_deg_ready", "out_dev_ready", "step1"))

        with nc.Block() as block:
            @block.gpsimd
            def _(pool):
                for t in range(NT):
                    gather(big_a[:, t * D:(t + 1) * D], x, node_of_rank[:, t, 0:1]).then_inc(xrank_in, 16)
                for i in range(GT):
                    pool.dma_start(dense[DUMMY + i * P:DUMMY + (i + 1) * P, :], zeros[:, 0:1]
                                   ).then_inc(slot_done[RND - 1][i], 16)

                def issue(it, r, i):
                    hold(pool, slot_done[1 - r][i], (it + 1) * 16)
                    scatter(dense, stage[:, r, i, 0:1], stage[:, r, i, 1:2].bitcast(F32),
                            compute_op=ALU.add).then_inc(slot_done[r][i], 16)

                def built(it, g):
                    for i in range(GT):
                        hold(pool, slot_done[1][i], (it + 1) * 16)
                    pool.sem_inc(group_built, 1)

                pool_rounds(pool, "dense", tab_dense, "dense", lambda it, r: None, issue, built)

            @block.sync
            def _(sp):
                sp.dma_start(big_b[:, :].rearrange("p (h n) -> p h n", h=2), xT.rearrange("(h p) n -> p h n", p=P)
                             ).then_inc(xt_in, 16)
                sp.wait_ge(xt_in, 16)
                groups = dense[0:NP * NP, :].rearrange("(g t p s) o -> g p t (s o)", g=NG, t=GT, p=P)
                with sp.Fori(0, NG) as g:
                    hold(sp, group_built, g + 1)
                    for b in range(NB):
                        hold(sp, half_done, g * (2 * NB) + (2 * b + 2))
                        sp.dma_start(wt[:, b % WR, :, :],
                                     groups[ds(g, 1), :, :, b * BLK:(b + 1) * BLK].rearrange("o p t s -> p (o t) s")
                                     ).then_inc(block_in[b % WR], 16)
                for i in range(WR):
                    sp.wait_ge(block_in[i], 16 * NG * (NB // WR))

            @block.tensor
            def _(pe):
                count_ends(pe, banks[:, 0, 0:NT], NCH)
                pe.sem_inc(half_done, 2 * WR)
                pe.wait_ge(xrank_in, 16 * NT)
                for g in range(NG):
                    for b in range(NB):
                        hold(pe, block_in[b % WR], g * (16 * NB // WR) + 16 * (b // WR + 1))
                        hold(pe, agg_done, g * (2 * NB) + (2 * b + 2))
                        for h in range(2):
                            for i in range(GT):
                                last = nc.tensor.matmul(banks[:, 4 + 2 * (b % 2) + h, 0:BLK],
                                                        big_a[:, g * GW + i * D + h * P:g * GW + i * D + (h + 1) * P],
                                                        wt[:, b % WR, i, :], start=i == 0, stop=i == GT - 1)
                            last.then_inc(half_done, 1)

            @block.scalar
            def _(act):
                act.wait_ge(out_deg_ready, 1)
                nc.scalar.activation(out_scale[:, :], out_scale[:, :], ACT.Sqrt).then_inc(out_dev_ready, 1)

            @block.vector
            def _(dve):
                s = Steps(dve, step1)
                one_hots(dve, s, 1, NCH)
                dve.wait_ge(hot_used, 2 * NCH)
                nc.vector.tensor_scalar(out_scale[:, :], banks[:, 0, 0:NT], 1.0, None, ALU.max).then_inc(out_deg_ready, 1)
                dve.wait_ge(out_dev_ready, 1)
                s(nc.vector.reciprocal(out_scale[:, :], out_scale[:, :]))
                dve.sem_inc(agg_done, 4)
                dve.wait_ge(xt_in, 16)
                with dve.Fori(0, NG) as g:
                    for b in range(NB):
                        for h in range(2):
                            hold(dve, half_done, g * (2 * NB) + (2 * WR + 2 * b + h + 1))
                            hold(dve, agg_done, g * (2 * NB) + (4 + 2 * b + h))
                            at = slice(h * NP + b * BLK, h * NP + (b + 1) * BLK)
                            nc.vector.tensor_tensor(big_b[:, at], big_b[:, at],
                                                    banks[:, 4 + 2 * (b % 2) + h, 0:BLK], ALU.add).then_inc(agg_done, 1)
        ph.close()
        prep.close()

        ph = ExitStack()
        psb2 = maker(ph)
        w1 = psb2("w1", [P, 2, HID0])
        w2 = psb2("w2", [P, HID0 // P, D])
        wc = psb2("wc", [P, 2, HID1])
        b1 = psb2("b1", [P, HID0 // P])
        b2 = psb2("b2", [P, D])
        hid = psb2("hid", [P, HID0 // P, GT * P])
        yg = psb2("yg", [P, GT, D])
        x1g = psb2("x1g", [P, GT, D])
        x1t = psb2("x1t", [P, 2, GT * P])
        h1g = psb2("h1g", [P, GT, HID1])
        w_in2, x_in2, hid_psum, hid_ready, out_psum, y_ready, step2, stored = (sem(n) for n in (
            "w_in2", "x_in2", "hid_psum", "hid_ready", "out_psum", "y_ready", "step2", "stored"))
        x1_ready, x1_out, t_psum, t_ready, h_psum, h1_ready, h1_out, pna_step = (sem(n) for n in (
            "x1_ready", "x1_out", "t_psum", "t_ready", "h_psum", "h1_ready", "h1_out", "pna_step"))
        var2, dev2 = sem("var2"), sem("dev2")
        flat = banks[:, :, :].rearrange("p b f -> p (b f)")
        GTP = GT * P
        HGT = GTP // 2
        five = flat[:, 6 * 512:6 * 512 + GTP]
        STEP2 = 7

        with nc.Block() as block:
            @block.sync
            def _(sp):
                sp.dma_start(w1[:, :, :], L0_W1.rearrange("(k p) m -> p k m", p=P)).then_inc(w_in2, 16)
                sp.dma_start(w2[:, :, :], L0_W2.rearrange("(k p) m -> p k m", p=P)).then_inc(w_in2, 16)
                sp.dma_start(wc[:, :, :], L1_Wc.rearrange("(k p) m -> p k m", p=P)).then_inc(w_in2, 16)
                sp.dma_start(b1[:, :], L0_b1).then_inc(w_in2, 16)
                sp.dma_start(b2[:, :], L0_b2.to_broadcast([P, D])).then_inc(w_in2, 16)
                sp.dma_start(big_c[:, :].rearrange("p (t d) -> p t d", t=NT), x.rearrange("(t p) d -> p t d", p=P)
                             ).then_inc(x_in2, 16)
                x1_rows = x1_dram.rearrange("(g t p) d -> g p t d", t=GT, p=P)
                h1_rows = h1_dram[0:NP, :].rearrange("(g t p) d -> g p t d", t=GT, p=P)
                sp.sem_inc(stored, 1)
                with sp.Fori(0, NG) as g:
                    hold(sp, x1_ready, g * GT + GT)
                    sp.dma_start(x1_rows[ds(g, 1), :, :, :].rearrange("o p t d -> p (o t) d"), x1g[:, :, :]
                                 ).then_inc(x1_out, 16)
                    hold(sp, h1_ready, g * GT + (GT + 1))
                    sp.dma_start(h1_rows[ds(g, 1), :, :, :].rearrange("o p t d -> p (o t) d"), h1g[:, :, :]
                                 ).then_inc(h1_out, 16)
                    hold(sp, x1_out, g * 16 + 16)
                    hold(sp, h1_out, g * 16 + 16)
                    sp.sem_inc(stored, 1)
                sp.wait_ge(x_in2, 16)
                sp.wait_ge(x1_out, 16 * NG)
                sp.wait_ge(h1_out, 16 * NG)

            @block.gpsimd
            def _(pool):
                s = Steps(pool, pna_step)
                s(nc.gpsimd.tensor_copy(tab_pna[:, :, :, 0], tab_edge[:, :, :, 0]))
                s(nc.gpsimd.tensor_tensor(tab_pna[:, :, :, 1].bitcast(F32),
                                          deg_rank[:, :, None].to_broadcast([P, NT, K]),
                                          slot_k[:, None, :].to_broadcast([P, NT, K]), ALU.subtract))
                s.settle()
                s(nc.gpsimd.tensor_scalar(tab_pna[:, :, :, 1].bitcast(F32), tab_pna[:, :, :, 1].bitcast(F32),
                                          0.0, 1.0, ALU.max, ALU.min))
                s.settle()
                s(nc.gpsimd.tensor_scalar(tab_pna[:, :, :, 1].bitcast(F32), tab_pna[:, :, :, 1].bitcast(F32),
                                          2 * LOW, -2 * LOW, ALU.mult, ALU.add))

            @block.tensor
            def _(pe):
                pe.wait_ge(w_in2, 16 * 5)
                pe.sem_inc(out_psum, 1)
                with pe.Fori(0, NG) as g:
                    for c in range(HID0 // P):
                        pair = 2 * (c % 2)
                        hold(pe, hid_ready, g * 4 + (c + 1))
                        for h in range(2):
                            for k in range(2):
                                last = nc.tensor.matmul(banks[:, pair + h, 0:HGT], w1[:, k, c * P:(c + 1) * P],
                                                        big_b[:, ds(g * GTP + (k * NP + h * HGT), HGT)],
                                                        start=k == 0, stop=k == 1)
                        last.then_inc(hid_psum, 1)
                    hold(pe, hid_ready, g * 4 + 6)
                    for i in range(GT):
                        hold(pe, y_ready, g * GT + (i + (2 if i == 0 else 1)))
                        for c in range(4):
                            last = nc.tensor.matmul(banks[:, 4 + i % 2, 0:D], hid[:, c, i * P:(i + 1) * P], w2[:, c, :],
                                                    start=c == 0, stop=c == 3)
                        last.then_inc(out_psum, 1)
                    hold(pe, x1_ready, g * GT + GT)
                    hold(pe, h1_ready, g * GT + 1)
                    for k in range(2):
                        hold(pe, t_ready, g * 2 + (1 + k))
                        for i in range(GT):
                            last = nc.tensor.transpose(five[:, i * P:(i + 1) * P], x1g[:, i, k * P:(k + 1) * P], ident[:, :])
                        last.then_inc(t_psum, 1)
                    hold(pe, t_ready, g * 2 + 3)
                    for i in range(GT):
                        for k in range(2):
                            last = nc.tensor.matmul(five[:, i * P:(i + 1) * P], x1t[:, k, i * P:(i + 1) * P], wc[:, k, :],
                                                    start=k == 0, stop=k == 1)
                    last.then_inc(h_psum, 1)

            @block.scalar
            def _(act):
                act.wait_ge(w_in2, 16 * 5)
                act.sem_inc(hid_ready, 2)
                act.sem_inc(t_ready, 1)
                act.sem_inc(h1_ready, 1)
                with act.Fori(0, NG) as g:
                    hold(act, out_psum, g * GT + 1)
                    for c in range(HID0 // P):
                        pair = 2 * (c % 2)
                        hold(act, hid_psum, g * 4 + (c + 1))
                        nc.scalar.activation(hid[:, c, :].rearrange("p (h n) -> p h n", h=2), banks[:, pair:pair + 2, 0:HGT],
                                             ACT.Relu, bias=b1[:, c:c + 1]).then_inc(hid_ready, 1)
                    deviation(act, g, var2, dev2)
                    for k in range(2):
                        hold(act, t_psum, g * 2 + (k + 1))
                        nc.scalar.activation(x1t[:, k, :], five, ACT.Copy).then_inc(t_ready, 1)
                    hold(act, h_psum, g + 1)
                    hold(act, stored, g + 1)
                    for i in range(GT):
                        nc.scalar.activation(h1g[:, i, :], five[:, i * P:(i + 1) * P], ACT.Copy,
                                             scale=out_scale[:, ds(g * GT + i, 1)]).then_inc(h1_ready, 1)

            @block.vector
            def _(dve):
                dve.wait_ge(w_in2, 16 * 5)
                dve.wait_ge(x_in2, 16)
                dve.sem_inc(y_ready, 2)
                with dve.Fori(0, NG) as g:
                    s = Steps(dve, step2, g * STEP2, (const_step, CONSTS))
                    for i in range(GT):
                        hold(dve, out_psum, g * GT + (i + 2))
                        nc.vector.tensor_tensor(yg[:, i, :], banks[:, 4 + i % 2, 0:D],
                                                big_c[:, ds(g * GW + i * D, D)], ALU.add).then_inc(y_ready, 1)
                    hold(dve, y_ready, g * GT + (GT + 2))
                    s(nc.vector.tensor_tensor(yg[:, :, :], yg[:, :, :], b2[:, None, :].to_broadcast([P, GT, D]), ALU.add))
                    hold(dve, stored, g + 1)
                    hold(dve, h1_ready, g * GT + 1)
                    layer_norm(dve, s, lambda i: yg[:, i, :], lambda i: x1g[:, i, :],
                               lambda i, ins: ins.then_inc(x1_ready, 1), g, var2, dev2)
                    assert s.n == STEP2, s.n
        ph.close()

        recycle_sems()

        big_d = sb("big_d", [P, NT * D])
        in_scale = sb("in_scale", [P, NT])
        deg_inv = sb("deg_inv", [P, NT])
        has = sb("has", [P, NT])
        amp = sb("amp", [P, NT])
        att = sb("att", [P, NT])
        late = ExitStack()
        psb3 = maker(late)
        sum1 = psb3("sum1", [P, NT * HID1])
        gath1 = psb3("gath1", [P, RND, GT * HID1])
        land1 = [[sem(f"land1_{r}{i}") for i in range(GT)] for r in range(RND)]
        used1, sum_zero, x1rank_in, step3, log_done, in_deg_ready = (sem(n) for n in (
            "used1", "sum_zero", "x1rank_in", "step3", "log_done", "in_deg_ready"))

        with nc.Block() as block:
            @block.gpsimd
            def _(pool):
                def before_round(it, r):
                    hold(pool, used1, it * RND + (r + 1))

                def issue(it, r, i):
                    gather(gath1[:, r, i * HID1:(i + 1) * HID1], h1_dram, stage[:, r, i, 0:1]).then_inc(land1[r][i], 16)

                pool_rounds(pool, "gcn", tab_edge, "edge", before_round, issue)
                for t in range(NT):
                    gather(big_a[:, t * D:(t + 1) * D], x1_dram, node_of_rank[:, t, 0:1]).then_inc(x1rank_in, 16)
                pool.wait_ge(x1rank_in, 16 * NT)

            @block.scalar
            def _(act):
                nc.scalar.activation(amp[:, :], deg_rank[:, :], ACT.Ln, bias=1.0).then_inc(log_done, 1)
                act.wait_ge(in_deg_ready, 1)
                nc.scalar.activation(in_scale[:, :], in_scale[:, :], ACT.Sqrt).then_inc(log_done, 1)

            @block.vector
            def _(dve):
                s = Steps(dve, step3)
                nc.vector.memset(sum1[:, :], 0.0).then_inc(sum_zero, 1)
                nc.vector.tensor_scalar(in_scale[:, :], deg_rank[:, :], 1.0, None, ALU.max).then_inc(in_deg_ready, 1)
                s(nc.vector.tensor_scalar(deg_inv[:, :], deg_rank[:, :], 1.0, None, ALU.max))
                s(nc.vector.tensor_scalar(has[:, :], deg_rank[:, :], 1.0, None, ALU.min))
                dve.wait_ge(log_done, 2)
                s(nc.vector.tensor_scalar(att[:, :], amp[:, :], EPS, None, ALU.max))
                s.settle()
                s(nc.vector.reciprocal(att[:, :], att[:, :]))
                s(nc.vector.reciprocal(in_scale[:, :], in_scale[:, :]))
                s(nc.vector.reciprocal(deg_inv[:, :], deg_inv[:, :]))
                s.settle()
                s(nc.vector.tensor_scalar(att[:, :], att[:, :], AVG_D, None, ALU.mult))
                s(nc.vector.tensor_scalar(amp[:, :], amp[:, :], 1.0 / AVG_D, None, ALU.mult))
                dve.wait_ge(sum_zero, 1)
                dve.sem_inc(used1, RND)

                def body(g, it):
                    for r in range(RND):
                        for i in range(GT):
                            hold(dve, land1[r][i], it * 16 + 16)
                        hold(dve, used1, it * RND + (r + RND))
                        at = sum1[:, ds(g * (GT * HID1), GT * HID1)]
                        nc.vector.tensor_tensor(at, at, gath1[:, r, :], ALU.add).then_inc(used1, 1)

                rounds(dve, "gcn_sum", body)

        w1t = psb3("w1t", [P, HID1])
        w2t = psb3("w2t", [P, D])
        wp = psb3("wp", [P, 2, D])
        whq = psb3("whq", [P, 2, 2 * D])
        bc, b1c, b2c, bq, bp = (psb3(n, [P, m]) for n, m in (("bc", HID1), ("b1c", 1), ("b2c", D), ("bq", D), ("bp", D)))
        hm = psb3("hm", [P, GTP])
        hmt = psb3("hmt", [P, GTP])
        h2t = psb3("h2t", [P, GTP])
        y4 = psb3("y4", [P, GT, D])
        x2t = psb3("x2t", [P, 2, GTP])
        w_in4, hm_ready, t4_psum, hmt_ready, h2_psum, h2_ready, out4_psum, y4_ready = (sem(n) for n in (
            "w_in4", "hm_ready", "t4_psum", "hmt_ready", "h2_psum", "h2_ready", "out4_psum", "y4_ready"))
        x2_ready, x2t_psum, x2t_ready, pq_psum, p_ready, q_ready, step4, p_out = (sem(n) for n in (
            "x2_ready", "x2t_psum", "x2t_ready", "pq_psum", "p_ready", "q_ready", "step4", "p_out"))
        var4, dev4 = sem("var4"), sem("dev4")
        STEP4 = 12

        with nc.Block() as block:
            @block.sync
            def _(sp):
                sp.dma_start(w1t[:, :], L1_W1T).then_inc(w_in4, 16)
                sp.dma_start(w2t[:, :], L1_W2T).then_inc(w_in4, 16)
                pre = L2_preW.rearrange("(h k p) m -> h p k m", h=2, p=P)
                sp.dma_start(wp[:, :, :], pre[0]).then_inc(w_in4, 16)
                sp.dma_start(whq[:, :, D:2 * D], pre[1]).then_inc(w_in4, 16)
                sp.dma_start(whq[:, :, 0:D], L2_postW[0:D, :].rearrange("(k p) m -> p k m", p=P)).then_inc(w_in4, 16)
                sp.dma_start(bc[:, :], L1_bc.to_broadcast([P, HID1])).then_inc(w_in4, 16)
                sp.dma_start(b1c[:, :], L1_b1).then_inc(w_in4, 16)
                for a, b in ((b2c, L1_b2), (bq, L2_preb), (bp, L2_postb)):
                    sp.dma_start(a[:, :], b.to_broadcast([P, D])).then_inc(w_in4, 16)
                sp.wait_ge(w_in4, 160)

            @block.gpsimd
            def _(pool):
                for t in range(NT):
                    pool.wait_ge(p_ready, t + 2)
                    scatter(p2_dram, node_of_rank[:, t, 0:1], big_a[:, t * D:(t + 1) * D]).then_inc(p_out, 16)
                pool.wait_ge(p_out, 16 * NT)

            @block.tensor
            def _(pe):
                pe.wait_ge(w_in4, 160)
                for g in range(NG):
                    hold(pe, hm_ready, g + 1)
                    hold(pe, p_ready, g * GT + 1)
                    hold(pe, q_ready, g * GT + 2)
                    for i in range(GT):
                        last = nc.tensor.transpose(flat[:, i * P:(i + 1) * P], hm[:, i * P:(i + 1) * P], ident[:, :])
                    last.then_inc(t4_psum, 1)
                    hold(pe, hmt_ready, g + 1)
                    for h in range(2):
                        last = nc.tensor.matmul(banks[:, 2 + h, 0:HGT], w1t[:, :], hmt[:, h * HGT:(h + 1) * HGT],
                                                start=True, stop=True)
                    last.then_inc(h2_psum, 1)
                    hold(pe, h2_ready, g + 1)
                    for i in range(GT):
                        hold(pe, y4_ready, g * GT + (i + (2 if i == 0 else 1)))
                        nc.tensor.matmul(banks[:, 4 + i % 2, 0:D], h2t[:, i * P:(i + 1) * P], w2t[:, :],
                                         start=True, stop=True).then_inc(out4_psum, 1)
                    hold(pe, x2_ready, g * GT + GT)
                    for k in range(2):
                        hold(pe, x2t_ready, g * 2 + (1 + k))
                        for i in range(GT):
                            last = nc.tensor.transpose(five[:, i * P:(i + 1) * P],
                                                       big_c[:, g * GW + i * D + k * P:g * GW + i * D + (k + 1) * P], ident[:, :])
                        last.then_inc(x2t_psum, 1)
                    hold(pe, x2t_ready, g * 2 + 3)
                    for i in range(GT):
                        if i > 0:
                            hold(pe, p_ready, g * GT + i)
                            hold(pe, q_ready, g * GT + (i + 1))
                        for k in range(2):
                            nc.tensor.matmul(banks[:, i % 2, 0:D], x2t[:, k, i * P:(i + 1) * P], wp[:, k, :],
                                             start=k == 0, stop=k == 1)
                        for k in range(2):
                            last = nc.tensor.matmul(banks[:, 2 + i % 2, :], x2t[:, k, i * P:(i + 1) * P], whq[:, k, :],
                                                    start=k == 0, stop=k == 1)
                        last.then_inc(pq_psum, 1)

            @block.scalar
            def _(act):
                act.wait_ge(w_in4, 160)
                act.sem_inc(p_ready, 1)
                act.sem_inc(x2t_ready, 1)
                with act.Fori(0, NG) as g:
                    hold(act, t4_psum, g + 1)
                    nc.scalar.activation(hmt[:, :], flat[:, 0:GTP], ACT.Copy).then_inc(hmt_ready, 1)
                    hold(act, h2_psum, g + 1)
                    nc.scalar.activation(h2t[:, :].rearrange("p (h n) -> p h n", h=2), banks[:, 2:4, 0:HGT],
                                         ACT.Relu, bias=b1c[:, :]).then_inc(h2_ready, 1)
                    deviation(act, g, var4, dev4)
                    for k in range(2):
                        hold(act, x2t_psum, g * 2 + (k + 1))
                        nc.scalar.activation(x2t[:, k, :], five, ACT.Copy).then_inc(x2t_ready, 1)
                    for i in range(GT):
                        hold(act, pq_psum, g * GT + (i + 1))
                        nc.scalar.activation(big_a[:, ds(g * GW + i * D, D)], banks[:, i % 2, 0:D], ACT.Copy
                                             ).then_inc(p_ready, 1)

            @block.vector
            def _(dve):
                dve.wait_ge(w_in4, 160)
                dve.sem_inc(y4_ready, 2)
                dve.sem_inc(q_ready, 2)
                with dve.Fori(0, NG) as g:
                    s = Steps(dve, step4, g * STEP4, (const_step, CONSTS))
                    for i in range(GT):
                        s(nc.vector.scalar_tensor_tensor(hm[:, i * P:(i + 1) * P], sum1[:, ds(g * (GT * HID1) + i * P, P)],
                                                         in_scale[:, ds(g * GT + i, 1)], bc[:, :], ALU.mult, ALU.add))
                    s.settle()
                    nc.vector.tensor_scalar(hm[:, :], hm[:, :], 0.0, None, ALU.max).then_inc(hm_ready, 1)
                    for i in range(GT):
                        hold(dve, out4_psum, g * GT + (i + 1))
                        nc.vector.tensor_tensor(y4[:, i, :], banks[:, 4 + i % 2, 0:D],
                                                big_a[:, ds(g * GW + i * D, D)], ALU.add).then_inc(y4_ready, 1)
                    hold(dve, y4_ready, g * GT + (GT + 2))
                    s(nc.vector.tensor_tensor(y4[:, :, :], y4[:, :, :], b2c[:, None, :].to_broadcast([P, GT, D]), ALU.add))
                    layer_norm(dve, s, lambda i: y4[:, i, :], lambda i: big_c[:, ds(g * GW + i * D, D)],
                               lambda i, ins: ins.then_inc(x2_ready, 1), g, var4, dev4)
                    for i in range(GT):
                        hold(dve, pq_psum, g * GT + (i + 1))
                        at = ds(g * GW + i * D, D)
                        nc.vector.tensor_tensor(big_d[:, at], banks[:, 2 + i % 2, 0:D], bp[:, :], ALU.add)
                        nc.vector.tensor_tensor(big_b[:, at], banks[:, 2 + i % 2, D:2 * D], bq[:, :], ALU.add
                                                ).then_inc(q_ready, 1)
                    assert s.n == STEP4, s.n
        late.close()

        recycle_sems()

        late = ExitStack()
        psb5 = maker(late)
        gath = psb5("gath", [P, RND, GT, D])
        z = psb5("z", [P, RND, GW])
        ms = psb5("ms", [P, RND, 2 * GW])
        nothing = psb5("nothing", [1, 512], BF16)
        wpost = psb5("wpost", [P, 8, 3 * D])
        wmix = psb5("wmix", [P, 2, D])
        bmix = psb5("bmix", [P, D])
        aggt = psb5("aggt", [P, 8, P])
        ht = psb5("ht", [P, D])
        htt = psb5("htt", [P, D])
        mean, mx, mn, std, y5 = (big_a[:, n * GW:(n + 1) * GW] for n in range(5))
        land = [[sem(f"land_{r}{i}") for i in range(GT)] for r in range(RND)]
        w_in5, used, z_ready, m_ready, max_done, sq_ready, sums_done = (sem(n) for n in (
            "w_in5", "used", "z_ready", "m_ready", "max_done", "sq_ready", "sums_done"))
        sums_final, evac_done, x3_ready, nothing_set, step5, var_ready, std_ready, mn_ready = (sem(n) for n in (
            "sums_final", "evac_done", "x3_ready", "nothing_set", "step5", "var_ready", "std_ready", "mn_ready"))
        t5_psum, t5_read, abc_psum, ht_ready, mix_psum, x3_out, w_used5 = (sem(n) for n in (
            "t5_psum", "t5_read", "abc_psum", "ht_ready", "mix_psum", "x3_out", "w_used5"))
        var5, dev5 = sem("var5"), sem("dev5")
        mix_read = sem("mix_read")
        STEP5 = 22

        with nc.Block() as block:
            @block.sync
            def _(sp):
                post = L2_postW[D:, :].rearrange("(s c p) m -> s p c m", s=3, p=P)
                for n in range(3):
                    sp.dma_start(wpost[:, :, n * D:(n + 1) * D], post[n]).then_inc(w_in5, 16)
                sp.dma_start(wmix[:, :, :], L2_mixW.rearrange("(k p) m -> p k m", p=P)).then_inc(w_in5, 16)
                sp.dma_start(bmix[:, :], L2_mixb.to_broadcast([P, D])).then_inc(w_in5, 16)
                sp.wait_ge(w_in5, 80)

            @block.gpsimd
            def _(pool):
                nc.gpsimd.memset(nothing[:, :], 0.0).then_inc(nothing_set, 1)

                def before_round(it, r):
                    hold(pool, used, it * SLOTS + (r + 1) * GT)

                def issue(it, r, i):
                    gather(gath[:, r, i, :], p2_dram, stage[:, r, i, 0:1]).then_inc(land[r][i], 16)

                pool_rounds(pool, "pna", tab_pna, "pna", before_round, issue)
                for t in range(NT):
                    pool.wait_ge(x3_ready, t + 2)
                    scatter(x3_dram, node_of_rank[:, t, 0:1], big_c[:, t * D:(t + 1) * D]).then_inc(x3_out, 16)
                pool.wait_ge(x3_out, 16 * NT)

            @block.vector
            def _(dve):
                dve.sem_inc(used, SLOTS)
                dve.sem_inc(max_done, RND)
                dve.sem_inc(x3_ready, 1)
                dve.sem_inc(ht_ready, 1)
                dve.sem_inc(mix_read, 1)
                dve.wait_ge(w_in5, 80)

                def before(g, it):
                    s = Steps(dve, step5, g * STEP5, (const_step, CONSTS))
                    s(nc.vector.memset(mx, 0.0))
                    s(nc.vector.memset(mn, -LOW))
                    s.settle()

                def body(g, it):
                    for r in range(RND):
                        hold(dve, m_ready, it * RND + (r + 1))
                        for i in range(GT):
                            hold(dve, land[r][i], it * 16 + 16)
                            last = nc.vector.tensor_tensor(z[:, r, i * D:(i + 1) * D], gath[:, r, i, :],
                                                           big_b[:, ds(g * GW + i * D, D)], ALU.add)
                        last.then_inc(z_ready, 1)
                        hold(dve, used, it * SLOTS + (r + 1) * GT + GT)
                        for i in range(GT):
                            at = mn[:, i * D:(i + 1) * D]
                            nc.vector.scalar_tensor_tensor(at, gath[:, r, i, :], stage[:, r, i, 1:2].bitcast(F32), at,
                                                           ALU.add, ALU.min).then_inc(used, 1)
                    for r in range(RND):
                        hold(dve, m_ready, it * RND + (r + 3))
                        hold(dve, max_done, it * RND + (r + 2))
                        nc.vector.tensor_tensor(mx, mx, ms[:, r, 0:GW], ALU.max).then_inc(max_done, 1)

                def after(g, it):
                    s = Steps(dve, step5, g * STEP5, (const_step, CONSTS))
                    s.n = 2
                    hold(dve, used, it * SLOTS + SLOTS)
                    hold(dve, max_done, it * RND + RND)
                    s(nc.vector.tensor_tensor(mn, mn, big_b[:, ds(g * GW, GW)], ALU.add))
                    hold(dve, evac_done, g + 2)
                    s(nc.vector.tensor_tensor(y5, mean, mean, ALU.mult))
                    s.settle()
                    s(nc.vector.tensor_tensor(std, std, y5, ALU.subtract))
                    s.settle()
                    nc.vector.tensor_scalar(std, std, 0.0, EPS, ALU.max, ALU.add).then_inc(var_ready, 1)
                    for i in range(GT):
                        at = mn[:, i * D:(i + 1) * D]
                        last = nc.vector.tensor_scalar(at, at, 0.0, has[:, ds(g * GT + i, 1)], ALU.max, ALU.mult)
                    last.then_inc(mn_ready, 1)
                    for i in range(GT):
                        tile = ds(g * GT + i, 1)
                        hold(dve, abc_psum, g * GT + (i + 1))
                        s(nc.vector.tensor_tensor(ht[:, :], banks[:, 6, 0:D], big_d[:, ds(g * GW + i * D, D)], ALU.add))
                        s.settle()
                        s(nc.vector.scalar_tensor_tensor(ht[:, :], banks[:, 6, D:2 * D], amp[:, tile], ht[:, :],
                                                         ALU.mult, ALU.add))
                        s.settle()
                        nc.vector.scalar_tensor_tensor(ht[:, :], banks[:, 7, 0:D], att[:, tile], ht[:, :],
                                                       ALU.mult, ALU.add).then_inc(ht_ready, 1)
                        hold(dve, mix_psum, g * GT + (i + 1))
                        nc.vector.tensor_tensor(y5[:, i * D:(i + 1) * D], banks[:, 7, D:2 * D], bmix[:, :], ALU.add
                                                ).then_inc(mix_read, 1)
                    hold(dve, mix_read, g * GT + (GT + 1))
                    s(nc.vector.scalar_tensor_tensor(y5, y5, 0.0, big_c[:, ds(g * GW, GW)], ALU.max, ALU.add))
                    layer_norm(dve, s, lambda i: y5[:, i * D:(i + 1) * D], lambda i: big_c[:, ds(g * GW + i * D, D)],
                               lambda i, ins: ins.then_inc(x3_ready, 1), g, var5, dev5)
                    assert s.n == STEP5, s.n

                rounds(dve, "pna_dve", body, before, after)

            @block.scalar
            def _(act):
                act.sem_inc(m_ready, RND)
                act.sem_inc(evac_done, 1)
                act.sem_inc(t5_read, 1)

                def body(g, it):
                    for r in range(RND):
                        hold(act, z_ready, it * RND + (r + 1))
                        hold(act, max_done, it * RND + (r + 1))
                        hold(act, sums_done, it * RND + (r + 1))
                        nc.scalar.activation(ms[:, r, 0:GW], z[:, r, :], ACT.Relu).then_inc(m_ready, 1)
                        hold(act, m_ready, it * RND + (r + 3))
                        nc.scalar.activation(ms[:, r, GW:2 * GW], ms[:, r, 0:GW], ACT.Square).then_inc(sq_ready, 1)

                def after(g, it):
                    hold(act, sums_final, g + 1)
                    hold(act, x3_ready, g * GT + 1)
                    for n, to in ((0, mean), (1, std)):
                        for i in range(GT):
                            last = nc.scalar.activation(to[:, i * D:(i + 1) * D], flat[:, n * GW + i * D:n * GW + (i + 1) * D],
                                                        ACT.Copy, scale=deg_inv[:, ds(g * GT + i, 1)])
                    last.then_inc(evac_done, 1)
                    hold(act, var_ready, g + 1)
                    nc.scalar.activation(std, std, ACT.Sqrt).then_inc(std_ready, 1)
                    for i in range(GT):
                        for q in range(2):
                            hold(act, t5_psum, g * (3 * GT) + (3 * i + q + 1))
                            nc.scalar.activation(aggt[:, 4 * q:4 * q + 4, :].rearrange("p c n -> p (c n)"), banks[:, 5, :],
                                                 ACT.Copy).then_inc(t5_read, 1)
                        hold(act, t5_psum, g * (3 * GT) + (3 * i + 3))
                        nc.scalar.activation(htt[:, :], banks[:, 5, 0:D], ACT.Relu).then_inc(t5_read, 1)
                    deviation(act, g, var5, dev5)

                rounds(act, "pna_act", body, None, after)

            @block.tensor
            def _(pe):
                pe.sem_inc(sums_done, RND)
                pe.wait_ge(w_in5, 80)
                pe.wait_ge(nothing_set, 1)

                def before(g, it):
                    hold(pe, evac_done, g + 1)
                    for b in range(5):
                        nc.tensor.matmul(banks[:, b, :], nothing[:, 0:P], nothing[:, :], start=True, stop=False)

                def body(g, it):
                    for r in range(RND):
                        hold(pe, sq_ready, it * RND + (r + 1))
                        for b in range(5):
                            last = nc.tensor.matmul(banks[:, b, :], ident[:, :], ms[:, r, b * 512:(b + 1) * 512],
                                                    start=False, stop=False)
                        last.then_inc(sums_done, 1)

                def after(g, it):
                    for b in range(5):
                        last = nc.tensor.matmul(banks[:, b, :], nothing[:, 0:P], nothing[:, :], start=False, stop=True)
                    last.then_inc(sums_final, 1)
                    hold(pe, mn_ready, g + 1)
                    hold(pe, std_ready, g + 1)
                    for i in range(GT):
                        for q in range(2):
                            hold(pe, t5_read, g * (3 * GT) + (3 * i + q + 1))
                            for c in range(4):
                                what = ((mean, mx), (mn, std))[q][c // 2]
                                last = nc.tensor.transpose(banks[:, 5, c * P:(c + 1) * P],
                                                           what[:, i * D + (c % 2) * P:i * D + (c % 2 + 1) * P], ident[:, :])
                            last.then_inc(t5_psum, 1)
                        hold(pe, t5_read, g * (3 * GT) + (3 * i + 3))
                        hold(pe, mix_read, g * GT + (i + 1))
                        for c in range(8):
                            nc.tensor.matmul(banks[:, 6, :], aggt[:, c, :], wpost[:, c, 0:2 * D], start=c == 0, stop=c == 7)
                        for c in range(8):
                            last = nc.tensor.matmul(banks[:, 7, 0:D], aggt[:, c, :], wpost[:, c, 2 * D:3 * D],
                                                    start=c == 0, stop=c == 7)
                        last.then_inc(abc_psum, 1)
                        hold(pe, ht_ready, g * GT + (i + 2))
                        for k in range(2):
                            last = nc.tensor.transpose(banks[:, 5, k * P:(k + 1) * P], ht[:, k * P:(k + 1) * P], ident[:, :])
                        last.then_inc(t5_psum, 1)
                        hold(pe, t5_read, g * (3 * GT) + (3 * i + 4))
                        for k in range(2):
                            last = nc.tensor.matmul(banks[:, 7, D:2 * D], htt[:, k * P:(k + 1) * P], wmix[:, k, :],
                                                    start=k == 0, stop=k == 1)
                        last.then_inc(mix_psum, 1)

                rounds(pe, "pna_pe", body, before, after)
        late.close()

        late = ExitStack()
        psb6 = maker(late)
        gath6 = psb6("gath6", [P, RND, GT, D])
        land6 = [[sem(f"land6_{r}{i}") for i in range(GT)] for r in range(RND)]
        used6, zero6 = sem("used6"), sem("zero6")

        with nc.Block() as block:
            @block.gpsimd
            def _(pool):
                def before_round(it, r):
                    hold(pool, used6, it * SLOTS + (r + 1) * GT)

                def issue(it, r, i):
                    gather(gath6[:, r, i, :], x3_dram, stage[:, r, i, 0:1]).then_inc(land6[r][i], 16)

                pool_rounds(pool, "wgcn", tab_edge, "edge", before_round, issue)

            @block.vector
            def _(dve):
                nc.vector.memset(big_a[:, :], 0.0).then_inc(zero6, 1)
                dve.wait_ge(zero6, 1)
                dve.sem_inc(used6, SLOTS)

                def body(g, it):
                    for r in range(RND):
                        hold(dve, used6, it * SLOTS + (r + 1) * GT + GT)
                        for i in range(GT):
                            hold(dve, land6[r][i], it * 16 + 16)
                            at = big_a[:, ds(g * GW + i * D, D)]
                            nc.vector.scalar_tensor_tensor(at, gath6[:, r, i, :], stage[:, r, i, 1:2].bitcast(F32), at,
                                                           ALU.mult, ALU.add).then_inc(used6, 1)

                rounds(dve, "wgcn_dve", body)

        w7 = psb6("w7", [P, 2, D])
        b7 = psb6("b7", [P, D])
        st = psb6("st", [P, 2, GTP])
        y7 = psb6("y7", [P, GT, D])
        w_in7, t7_psum, t7_read, out7_psum, y7_ready, x4_ready, x4_out, step7 = (sem(n) for n in (
            "w_in7", "t7_psum", "t7_read", "out7_psum", "y7_ready", "x4_ready", "x4_out", "step7"))
        var7, dev7 = sem("var7"), sem("dev7")
        STEP7 = 7

        with nc.Block() as block:
            @block.sync
            def _(sp):
                sp.dma_start(w7[:, :, :], L3_W.rearrange("(k p) m -> p k m", p=P)).then_inc(w_in7, 16)
                sp.dma_start(b7[:, :], L3_b.to_broadcast([P, D])).then_inc(w_in7, 16)
                sp.wait_ge(w_in7, 32)

            @block.tensor
            def _(pe):
                pe.wait_ge(w_in7, 32)
                for g in range(NG):
                    for k in range(2):
                        hold(pe, t7_read, g * 2 + (1 + k))
                        for i in range(GT):
                            last = nc.tensor.transpose(five[:, i * P:(i + 1) * P],
                                                       big_a[:, g * GW + i * D + k * P:g * GW + i * D + (k + 1) * P], ident[:, :])
                        last.then_inc(t7_psum, 1)
                    hold(pe, t7_read, g * 2 + 3)
                    for i in range(GT):
                        hold(pe, y7_ready, g * GT + (i + (2 if i == 0 else 1)))
                        for k in range(2):
                            last = nc.tensor.matmul(banks[:, 4 + i % 2, 0:D], st[:, k, i * P:(i + 1) * P], w7[:, k, :],
                                                    start=k == 0, stop=k == 1)
                        last.then_inc(out7_psum, 1)

            @block.scalar
            def _(act):
                act.sem_inc(t7_read, 1)
                with act.Fori(0, NG) as g:
                    for k in range(2):
                        hold(act, t7_psum, g * 2 + (k + 1))
                        nc.scalar.activation(st[:, k, :], five, ACT.Copy).then_inc(t7_read, 1)
                    deviation(act, g, var7, dev7)

            @block.vector
            def _(dve):
                dve.wait_ge(w_in7, 32)
                dve.sem_inc(y7_ready, 2)
                dve.sem_inc(x4_ready, 1)
                with dve.Fori(0, NG) as g:
                    s = Steps(dve, step7, g * STEP7, (const_step, CONSTS))
                    hold(dve, x4_ready, g * GT + 1)
                    for i in range(GT):
                        hold(dve, out7_psum, g * GT + (i + 1))
                        nc.vector.tensor_tensor(y7[:, i, :], banks[:, 4 + i % 2, 0:D], b7[:, :], ALU.add
                                                ).then_inc(y7_ready, 1)
                    hold(dve, y7_ready, g * GT + (GT + 2))
                    s(nc.vector.scalar_tensor_tensor(y7[:, :, :].rearrange("p t d -> p (t d)"),
                                                     y7[:, :, :].rearrange("p t d -> p (t d)"), 0.0,
                                                     big_c[:, ds(g * GW, GW)], ALU.max, ALU.add))
                    layer_norm(dve, s, lambda i: y7[:, i, :], lambda i: big_b[:, ds(g * GW + i * D, D)],
                               lambda i, ins: ins.then_inc(x4_ready, 1), g, var7, dev7)
                    assert s.n == STEP7, s.n

            @block.gpsimd
            def _(pool):
                for t in range(NT):
                    pool.wait_ge(x4_ready, t + 2)
                    scatter(out, node_of_rank[:, t, 0:1], big_b[:, t * D:(t + 1) * D], bounds_check=N - 1,
                            oob_is_err=False).then_inc(x4_out, 16)
                pool.wait_ge(x4_out, 16 * NT)
        late.close()


def kernel(x, src, dst, edge_weight, L0_gnn_W1, L0_gnn_b1, L0_gnn_W2, L0_gnn_b2, L1_gnn_W_conv, L1_gnn_b_conv,
           L1_gnn_W1, L1_gnn_b1, L1_gnn_W2, L1_gnn_b2, L2_gnn_pre_W, L2_gnn_pre_b, L2_gnn_post_W, L2_gnn_post_b,
           L2_gnn_mix_W, L2_gnn_mix_b, L3_gnn_W, L3_gnn_b):
    import numpy as np
    from concourse import bacc
    from concourse.bass_utils import run_bass_kernel_spmd

    def rows(a, n, fill):
        a = np.asarray(a)
        return np.concatenate([a, np.full((n - a.shape[0],) + a.shape[1:], fill, a.dtype)])

    xp = rows(x, NP, 0)
    line = lambda a: np.asarray(a).reshape(1, -1)
    arrays = {
        "x": xp, "xT": np.ascontiguousarray(xp.T),
        "src": rows(src, EP, NP).reshape(P, EC), "dst": rows(dst, EP, NP).reshape(P, EC),
        "w": rows(edge_weight, EP, 0).reshape(P, EC),
        "L0_W1": L0_gnn_W1, "L0_b1": np.ascontiguousarray(np.asarray(L0_gnn_b1).reshape(-1, P).T),
        "L0_W2": L0_gnn_W2, "L0_b2": line(L0_gnn_b2),
        "L1_Wc": L1_gnn_W_conv, "L1_bc": line(L1_gnn_b_conv),
        "L1_W1T": np.ascontiguousarray(np.asarray(L1_gnn_W1).T), "L1_b1": np.asarray(L1_gnn_b1).reshape(-1, 1),
        "L1_W2T": np.ascontiguousarray(np.asarray(L1_gnn_W2).T), "L1_b2": line(L1_gnn_b2),
        "L2_preW": L2_gnn_pre_W, "L2_preb": line(L2_gnn_pre_b), "L2_postW": L2_gnn_post_W,
        "L2_postb": line(L2_gnn_post_b), "L2_mixW": L2_gnn_mix_W, "L2_mixb": line(L2_gnn_mix_b),
        "L3_W": L3_gnn_W, "L3_b": line(L3_gnn_b),
    }
    arrays = {f"in_{k}": np.ascontiguousarray(v) for k, v in arrays.items()}
    nc = bacc.Bacc("TRN2", target_bir_lowering=False, num_devices=1)
    args = [nc.dram_tensor(k, v.shape, mybir.dt.from_np(v.dtype), kind="ExternalInput").ap() for k, v in arrays.items()]
    out = nc.dram_tensor("out", (N, D), F32, kind="ExternalOutput").ap()
    build(nc, *args, out)
    result = run_bass_kernel_spmd(nc, [arrays], core_ids=[0])
    return result.results[0]["out"]
```

```python
from contextlib import ExitStack

import concourse.bass as bass
from concourse import mybir
from concourse.bass import IndirectOffsetOnAxis, ds

F32, I32, BF16 = mybir.dt.float32, mybir.dt.int32, mybir.dt.bfloat16
ALU, ACT, AX = mybir.AluOpType, mybir.ActivationFunctionType, mybir.AxisListType

P = 128
N, E, D = 3125, 53125, 256
HID0, HID1 = 512, 128
NT = -(-N // P)
NP = NT * P
GT = 5
NG = NT // GT
EC = -(-E // P)
EP = EC * P
K = 40
RND = 2
SLOTS = RND * GT
HALF = K // RND
PAD = NP
DUMMY = NP * NP
KEY = 4096
KEYCAP = 2047
CH = 32
NCH = EC // CH
DT0 = 13
GTP = GT * P
HGT = GTP // 2
WR = GT
GW = GT * D
EPS, AVG_D = 1e-5, 3.4965
LOW = -1e30
assert NP * NP + SLOTS * P < 1 << 24 and NCH * CH == EC and NG * GT == NT


class Steps:

    def __init__(self, engine, sem, base=0, spacer=None):
        self.engine, self.sem, self.base, self.n, self.spacer = engine, sem, base, 0, spacer

    def __call__(self, instruction):
        self.n += 1
        return instruction.then_inc(self.sem, 1)

    def settle(self):
        value = self.base + self.n
        if self.spacer is not None:
            value = self.engine.snap(self.engine.to_reg(value), min_val=1, max_val=1 << 30)
            self.engine.wait_ge(*self.spacer)
        self.engine.wait_ge(self.sem, value)


def build(nc, x, xT, src, dst, w, L0_W1, L0_b1, L0_W2, L0_b2, L1_Wc, L1_bc, L1_W1T, L1_b1, L1_W2T, L1_b2,
          L2_preW, L2_preb, L2_postW, L2_postb, L2_mixW, L2_mixb, L3_W, L3_b, out):
    def dram(name, shape, dt):
        return nc.dram_tensor(name, shape, dt, kind="Internal").ap()

    edges = dram("edges", (EP, 2), I32)
    keys_dram = dram("keys_dram", (1, NP), F32)
    ranked_dram = dram("ranked_dram", (NP, 4), I32)
    dense = dram("dense", (NP * NP + SLOTS * P, 2), F32)
    x1_dram = dram("x1_dram", (NP, D), F32)
    p2_dram = dram("p2_dram", (NP + 1, D), F32)
    x3_dram = dram("x3_dram", (NP, D), F32)

    whole = ExitStack()
    with whole:
        def maker(stack):
            return lambda name, shape, dt=F32: stack.enter_context(nc.sbuf_tensor(name, shape, dt))

        sb = maker(whole)

        used_sems = []

        def sem(name):
            used_sems.append(nc.alloc_semaphore(name))
            return used_sems[-1]

        def recycle_sems():
            nc.clear_and_free_semaphores(used_sems[1:])
            del used_sems[1:]
            nc.all_engine_barrier()

        banks = whole.enter_context(nc.psum_tensor("banks", [P, 8, 512], F32))
        flat = banks[:, :, :].rearrange("p b f -> p (b f)")

        ident = sb("ident", [P, P])
        node_of_rank = sb("node_of_rank", [P, NT, 4], I32)
        deg_rank = sb("deg_rank", [P, NT])
        iters = sb("iters", [P, 2 * NG], I32)
        slot_k = sb("slot_k", [P, K])
        tab_edge = sb("tab_edge", [P, NT, K, 2], I32)
        tab_pna = tab_edge
        row_base = sb("row_base", [P, NT])
        dummy_at = sb("dummy_at", [P, GT, K])
        out_scale = sb("out_scale", [P, NT])
        stage = sb("stage", [P, RND, GT, 3], I32)
        more = sb("more", [P, GT, K, 2], I32)
        more_f = sb("more_f", [P, 3, GT, K])
        more_at = sb("more_at", [P, 3, GT])
        more_idx = sb("more_idx", [P, GT], I32)
        big_a = sb("big_a", [P, NT * D])
        big_b = sb("big_b", [P, NT * D])
        big_c = sb("big_c", [P, NT * D])
        lowrow = sb("lowrow", [1, D])
        bn = sb("bn", [P, GT, 6])
        mv = sb("mv", [P, GT, 2])
        rstd = sb("rstd", [P, GT])
        dev = sb("dev", [P, GT])
        eps = sb("eps", [P, 1])

        const_step = sem("const_step")
        CONSTS = 11

        def hold(engine, semaphore, value):
            if not isinstance(value, int):
                value = engine.snap(engine.to_reg(value), min_val=1, max_val=1 << 30)
                engine.wait_ge(const_step, CONSTS)
            engine.wait_ge(semaphore, value)

        def layer_norm(dve, steps, y, to, signal, g, var_ready, std_ready):
            steps.settle()
            for i in range(GT):
                steps(nc.vector.bn_stats(bn[:, i, :], y(i)))
            steps.settle()
            for i in range(GT):
                last = nc.vector.bn_aggr(mv[:, i, :], bn[:, i, :])
            last.then_inc(var_ready, 1)
            hold(dve, std_ready, g + 1)
            steps(nc.vector.reciprocal(rstd[:, :], dev[:, :]))
            steps.settle()
            for i in range(GT):
                signal(i, nc.vector.tensor_scalar(to(i), y(i), mv[:, i, 0:1], rstd[:, i:i + 1],
                                                  ALU.subtract, ALU.mult))

        def deviation(act, g, var_ready, std_ready):
            hold(act, var_ready, g + 1)
            nc.scalar.activation(dev[:, :], mv[:, :, 1], ACT.Sqrt, bias=eps[:, :]).then_inc(std_ready, 1)

        def gather(to, table, index):
            return nc.gpsimd.indirect_dma_start(to, None, table, IndirectOffsetOnAxis(ap=index, axis=0))

        def scatter(table, index, rows, **how):
            return nc.gpsimd.indirect_dma_start(table, IndirectOffsetOnAxis(ap=index, axis=0), rows, None, **how)

        prep = ExitStack()
        psb = maker(prep)
        onehot_lo = psb("onehot_lo", [P, 2, CH, P], BF16)
        onehot_hi = psb("onehot_hi", [P, EC, NT], BF16)
        iota_lo = psb("iota_lo", [P, P], BF16)
        iota_hi = psb("iota_hi", [P, NT], BF16)
        end_i = psb("end_i", [P, 2, EC], I32)
        half_i = psb("half_i", [P, EC], I32)
        hi_b = psb("hi_b", [P, EC], BF16)
        lo_b = psb("lo_b", [P, EC], BF16)
        zeros = psb("zeros", [P, NP])
        tab_dense = psb("tab_dense", [P, NT, K, 2], I32)
        tmp = ExitStack()
        tsb = maker(tmp)
        w_in = tsb("w_in", [P, EC])
        pairs = tsb("pairs", [P, EC, 2], I32)
        before = tsb("before", [P, P])
        ones = tsb("ones", [P, P])
        node_id = tsb("node_id", [P, NT])
        deg = tsb("deg", [P, NT])
        total = tsb("total", [P, NT])
        running = tsb("running", [P, NT])
        first = tsb("first", [P, NT])
        key = tsb("key", [P, NT])
        neg_key = tsb("neg_key", [P, NT])
        key_t = tsb("key_t", [NT, P])
        key_row = tsb("key_row", [P, NP])
        junk = tsb("junk", [P, 2, NP], BF16)
        rank = tsb("rank", [P, NT])
        rank_i = tsb("rank_i", [P, NT], I32)
        ranked = tsb("ranked", [P, NT, 4], I32)
        valid = tsb("valid", [P, NT, K])
        srcf = tsb("srcf", [P, NT, K])
        work = tsb("work", [P, NT, K])
        gmax = tsb("gmax", [P, NG])
        gmax_all = tsb("gmax_all", [P, NG])
        gmax_i = tsb("gmax_i", [P, NG], I32)

        ends_in, w_read, edges_out = sem("ends_in"), sem("w_read"), sem("edges_out")
        zero_set, zero_out, part_zero = sem("zero_set"), [sem(f"zero_out{g}") for g in range(2)], sem("part_zero")
        prep_step, hot_ready, hot_used = sem("prep_step"), sem("hot_ready"), sem("hot_used")
        hist_done, deg_ready, pre_done = sem("hist_done"), sem("deg_ready"), sem("pre_done")
        key_ready, keyt_done, keyt_ready = sem("key_ready"), sem("keyt_done"), sem("keyt_ready")
        key_out, key_in, act_rank, ranked_ready = sem("key_out"), sem("key_in"), sem("act_rank"), sem("ranked_ready")
        ranked_out, ranked_in, runs_in = sem("ranked_out"), sem("ranked_in"), sem("runs_in")
        gmax_ready, gmax_done, pads_out, pair_ready = sem("gmax_ready"), sem("gmax_done"), sem("pads_out"), sem("pair_ready")
        neg_ready = sem("neg_ready")

        def one_hots(dve, steps, which, base):
            end = end_i[:, which, :]
            steps(nc.vector.tensor_scalar(half_i[:, :], end, 7, None, ALU.arith_shift_right))
            steps.settle()
            steps(nc.vector.tensor_copy(hi_b[:, :], half_i[:, :]))
            steps.settle()
            steps(nc.vector.tensor_scalar(half_i[:, :], end, P - 1, None, ALU.bitwise_and))
            steps.settle()
            steps(nc.vector.tensor_copy(lo_b[:, :], half_i[:, :]))
            steps(nc.vector.tensor_tensor(onehot_hi[:, :, :], hi_b[:, :, None].to_broadcast([P, EC, NT]),
                                          iota_hi[:, None, :].to_broadcast([P, EC, NT]), ALU.is_equal))
            steps.settle()
            for c in range(NCH):
                if base + c >= 2:
                    dve.wait_ge(hot_used, base + c - 1)
                at = slice(c * CH, (c + 1) * CH)
                nc.vector.tensor_tensor(onehot_lo[:, (base + c) % 2, :, :], lo_b[:, at, None].to_broadcast([P, CH, P]),
                                        iota_lo[:, None, :].to_broadcast([P, CH, P]), ALU.is_equal).then_inc(hot_ready, 1)

        def count_ends(pe, hist, base):
            for c in range(NCH):
                pe.wait_ge(hot_ready, base + c + 1)
                for e in range(CH):
                    at = c * CH + e
                    last = nc.tensor.matmul(hist, onehot_lo[:, (base + c) % 2, e, :], onehot_hi[:, at, :],
                                            start=at == 0, stop=at == EC - 1)
                last.then_inc(hot_used, 1)

        rows = dense[0:NP * NP, :].rearrange("(t p s) two -> t p (s two)", t=2 * NT, p=P)
        ZG = 2 * GT
        ZERO_A, ZERO_B = 6, 2 * ZG

        with nc.Block() as block:
            @block.sync
            def _(sp):
                sp.dma_start(end_i[:, 0, :], dst).then_inc(ends_in, 16)
                sp.dma_start(end_i[:, 1, :], src).then_inc(w_read, 16)
                sp.dma_start(w_in[:, :], w).then_inc(w_read, 16)
                sp.wait_ge(zero_set, 2)
                sp.dma_start(p2_dram[NP:NP + 1, :], lowrow[:, :]).then_inc(pads_out, 16)
                sp.wait_ge(pair_ready, 2)
                sp.dma_start(edges.rearrange("(p c) two -> p (c two)", p=P),
                             pairs[:, :, :].rearrange("p c two -> p (c two)")).then_inc(edges_out, 16)
                sp.dma_start(dense[NP * NP:, :].rearrange("(p c) two -> p (c two)", p=P),
                             zeros[:, 0:2 * SLOTS]).then_inc(pads_out, 16)
                for t in range(ZERO_A):
                    sp.dma_start(rows[t], zeros[:, :]).then_inc(zero_out[t // ZG], 16)
                sp.wait_ge(keyt_ready, 1)
                sp.dma_start(keys_dram.rearrange("o (t p) -> (o t) p", p=P), key_t[:, :]).then_inc(key_out, 16)
                sp.wait_ge(key_out, 16)
                sp.dma_start(key_row[:, :], keys_dram.to_broadcast([P, NP])).then_inc(key_in, 16)
                for t in range(ZERO_A, ZERO_B):
                    sp.dma_start(rows[t], zeros[:, :]).then_inc(zero_out[t // ZG], 16)
                sp.wait_ge(pads_out, 32)
                sp.wait_ge(edges_out, 16)
                for g in range(ZERO_B // ZG):
                    sp.wait_ge(zero_out[g], 16 * ZG)
                    sp.sem_inc(part_zero, 1)

            @block.gpsimd
            def _(pool):
                c = Steps(pool, const_step)
                c(nc.gpsimd.memset(eps[:, :], EPS))
                nc.gpsimd.memset(zeros[:, :], 0.0).then_inc(zero_set, 1)
                nc.gpsimd.memset(lowrow[:, :], LOW).then_inc(zero_set, 1)
                c(nc.gpsimd.iota(iota_lo[:, :], [[1, P]], base=0, channel_multiplier=0,
                                 allow_small_or_imprecise_dtypes=True))
                c(nc.gpsimd.iota(iota_hi[:, :], [[1, NT]], base=0, channel_multiplier=0,
                                 allow_small_or_imprecise_dtypes=True))
                c(nc.gpsimd.iota(node_id[:, :], [[P, NT]], base=0, channel_multiplier=1,
                                 allow_small_or_imprecise_dtypes=True))
                c(nc.gpsimd.memset(ones[:, :], 1.0))
                c(nc.gpsimd.memset(ident[:, :], 1.0))
                c.settle()
                c(nc.gpsimd.affine_select(out=before[:, :], in_=ones[:, :], compare_op=ALU.is_gt, fill=0.0,
                                          base=0, pattern=[[1, P]], channel_multiplier=-1))
                c(nc.gpsimd.affine_select(out=ident[:, :], in_=ident[:, :], compare_op=ALU.is_equal, fill=0.0,
                                          base=0, pattern=[[1, P]], channel_multiplier=-1))
                c(nc.gpsimd.iota(slot_k[:, :], [[1, K]], base=0, channel_multiplier=0,
                                 allow_small_or_imprecise_dtypes=True))
                c(nc.gpsimd.memset(stage[:, :, :, 2].bitcast(F32), 1.0))
                c(nc.gpsimd.iota(dummy_at[:, :, :], [[RND * P, GT], [0, K // RND], [P, RND]], base=DUMMY,
                                 channel_multiplier=1, allow_small_or_imprecise_dtypes=True))
                pool.wait_ge(w_read, 32)
                nc.gpsimd.tensor_copy(pairs[:, :, 0], end_i[:, 1, :]).then_inc(pair_ready, 1)
                nc.gpsimd.tensor_copy(pairs[:, :, 1].bitcast(F32), w_in[:, :]).then_inc(pair_ready, 1)
                pool.wait_ge(ranked_ready, 1)
                for t in range(NT):
                    scatter(ranked_dram, rank_i[:, t:t + 1], ranked[:, t, :]).then_inc(ranked_out, 16)
                pool.wait_ge(ranked_out, 16 * NT)
                pool.dma_start(node_of_rank[:, :, :], ranked_dram.rearrange("(t p) f -> p t f", p=P)).then_inc(ranked_in, 16)
                pool.wait_ge(ranked_in, 16)
                pool.wait_ge(edges_out, 16)
                for t in range(NT):
                    gather(tab_edge[:, t, :, :].rearrange("p k two -> p (k two)"), edges,
                           node_of_rank[:, t, 1:2]).then_inc(runs_in, 16)
                pool.wait_ge(gmax_ready, 1)
                nc.gpsimd.partition_all_reduce(gmax_all[:, :], gmax[:, :], P, bass.bass_isa.ReduceOp.max
                                               ).then_inc(gmax_done, 1)

            @block.tensor
            def _(pe):
                hist, prefix, totals, keyt = banks[:, 0, 0:NT], banks[:, 1, 0:NT], banks[:, 2, 0:NT], banks[0:NT, 3, 0:P]
                count_ends(pe, hist, 0)
                pe.wait_ge(const_step, CONSTS)
                pe.wait_ge(deg_ready, 1)
                nc.tensor.matmul(prefix, before[:, :], deg[:, :], start=True, stop=True)
                nc.tensor.matmul(totals, ones[:, :], deg[:, :], start=True, stop=True).then_inc(pre_done, 1)
                pe.wait_ge(key_ready, 1)
                nc.tensor.transpose(keyt, key[:, :], ident[:, :]).then_inc(keyt_done, 1)

            @block.scalar
            def _(act):
                act.wait_ge(key_in, 16)
                act.wait_ge(neg_ready, 1)
                for t in range(DT0, NT):
                    nc.scalar.activation(junk[:, 1, :], key_row[:, :], ACT.Sign, bias=neg_key[:, t:t + 1],
                                         accum_out=rank[:, t:t + 1]).then_inc(act_rank, 1)
                    act.wait_ge(act_rank, t - DT0 + 1)

            @block.vector
            def _(dve):
                s = Steps(dve, prep_step)
                dve.wait_ge(ends_in, 16)
                dve.wait_ge(const_step, 3)
                one_hots(dve, s, 0, 0)
                dve.wait_ge(hot_used, NCH)
                nc.vector.tensor_copy(deg[:, :], banks[:, 0, 0:NT]).then_inc(deg_ready, 1)
                dve.wait_ge(deg_ready, 1)
                dve.wait_ge(const_step, CONSTS)
                s(nc.vector.tensor_scalar(key[:, :], deg[:, :], float(KEYCAP), float(KEY), ALU.min, ALU.mult))
                s.settle()
                nc.vector.tensor_tensor(key[:, :], key[:, :], node_id[:, :], ALU.add).then_inc(key_ready, 1)
                dve.wait_ge(key_ready, 1)
                nc.vector.tensor_scalar(neg_key[:, :], key[:, :], -1.0, -0.5, ALU.mult, ALU.add).then_inc(neg_ready, 1)
                dve.wait_ge(keyt_done, 1)
                nc.vector.tensor_copy(key_t[:, :], banks[0:NT, 3, 0:P]).then_inc(keyt_ready, 1)
                dve.wait_ge(pre_done, 1)
                s(nc.vector.tensor_copy(total[:, :], banks[:, 2, 0:NT]))
                s.settle()
                dve.wait_ge(zero_set, 1)
                s(nc.vector.tensor_tensor_scan(running[:, :], total[:, :], zeros[:, 0:NT], 0.0, ALU.add, ALU.add))
                s.settle()
                s(nc.vector.tensor_tensor(running[:, :], running[:, :], total[:, :], ALU.subtract))
                s.settle()
                s(nc.vector.tensor_tensor(first[:, :], running[:, :], banks[:, 1, 0:NT], ALU.add))
                s.settle()
                s(nc.vector.tensor_copy(ranked[:, :, 0], node_id[:, :]))
                s(nc.vector.tensor_copy(ranked[:, :, 1], first[:, :]))
                s(nc.vector.tensor_copy(ranked[:, :, 2], deg[:, :]))
                s(nc.vector.memset(ranked[:, :, 3], 0))
                dve.wait_ge(key_in, 16)
                for t in range(DT0):
                    s(nc.vector.tensor_scalar(junk[:, 0, :], key_row[:, :], key[:, t:t + 1], 0.0, ALU.is_gt, ALU.add,
                                              accum_out=rank[:, t:t + 1]))
                    s.settle()
                dve.wait_ge(act_rank, NT - DT0)
                s(nc.vector.tensor_scalar(rank[:, DT0:NT], rank[:, DT0:NT], float(NP), 0.5, ALU.add, ALU.mult))
                s.settle()
                nc.vector.tensor_copy(rank_i[:, :], rank[:, :]).then_inc(ranked_ready, 1)
                dve.wait_ge(ranked_in, 16)
                s(nc.vector.tensor_copy(deg_rank[:, :], node_of_rank[:, :, 2]))
                s.settle()
                nc.vector.tensor_reduce(gmax[:, :], deg_rank[:, :].rearrange("p (g t) -> p g t", t=GT), AX.X,
                                        ALU.max).then_inc(gmax_ready, 1)
                s(nc.vector.tensor_tensor(valid[:, :, :], slot_k[:, None, :].to_broadcast([P, NT, K]),
                                          deg_rank[:, :, None].to_broadcast([P, NT, K]), ALU.is_lt))
                for g in range(NG):
                    at = slice(g * GT, (g + 1) * GT)
                    s(nc.vector.tensor_scalar(row_base[:, at], node_id[:, at], float(g * (NP - 1) * GTP), None, ALU.add))
                dve.wait_ge(runs_in, 16 * NT)
                s.settle()
                s(nc.vector.tensor_copy(srcf[:, :, :], tab_edge[:, :, :, 0]))
                s.settle()
                s(nc.vector.tensor_scalar(work[:, :, :], srcf[:, :, :], float(-PAD), None, ALU.add))
                s.settle()
                s(nc.vector.tensor_tensor(work[:, :, :], work[:, :, :], valid[:, :, :], ALU.mult))
                s.settle()
                s(nc.vector.tensor_scalar(tab_edge[:, :, :, 0], work[:, :, :], float(PAD), None, ALU.add))
                s.settle()
                s(nc.vector.tensor_tensor(tab_edge[:, :, :, 1].bitcast(F32), tab_edge[:, :, :, 1].bitcast(F32),
                                          valid[:, :, :], ALU.mult))
                s(nc.vector.tensor_scalar(srcf[:, :, :], srcf[:, :, :], float(GTP), None, ALU.mult))
                s.settle()
                s(nc.vector.tensor_tensor(srcf[:, :, :], srcf[:, :, :], row_base[:, :, None].to_broadcast([P, NT, K]),
                                          ALU.add))
                s.settle()
                s(nc.vector.tensor_copy(tab_dense[:, :, :, 1], tab_edge[:, :, :, 1]))
                for g in range(NG):
                    at = slice(g * GT, (g + 1) * GT)
                    s(nc.vector.tensor_tensor(srcf[:, at, :], srcf[:, at, :], dummy_at[:, :, :], ALU.subtract))
                s.settle()
                s(nc.vector.tensor_tensor(srcf[:, :, :], srcf[:, :, :], valid[:, :, :], ALU.mult))
                s.settle()
                for g in range(NG):
                    at = slice(g * GT, (g + 1) * GT)
                    s(nc.vector.tensor_tensor(tab_dense[:, at, :, 0], srcf[:, at, :], dummy_at[:, :, :], ALU.add))
                dve.wait_ge(gmax_done, 1)
                s(nc.vector.tensor_copy(gmax_i[:, :], gmax_all[:, :]))
                s.settle()
                s(nc.vector.tensor_scalar(gmax_i[:, :], gmax_i[:, :], RND - 1, None, ALU.add))
                s.settle()
                s(nc.vector.tensor_scalar(gmax_i[:, :], gmax_i[:, :], 1, None, ALU.arith_shift_right))
                s.settle()
                s(nc.vector.tensor_scalar(iters[:, 0:NG], gmax_i[:, :], 1, None, ALU.max))
                s.settle()
                s(nc.vector.tensor_scalar(gmax_i[:, :], iters[:, 0:NG], HALF, None, ALU.is_le))
                s.settle()
                s(nc.vector.tensor_tensor(iters[:, NG:2 * NG], iters[:, 0:NG], gmax_i[:, :], ALU.mult))
        tmp.close()

        RELOAD_STEPS = {"pna": 16, "dense": 19}

        def reload_table(pool, table, kind, g, loads, reloaded, more_in):
            s = Steps(pool, reloaded, loads * RELOAD_STEPS[kind], (const_step, CONSTS))
            first, left, done = more_at[:, 0, :], more_at[:, 1, :], more_at[:, 2, :]
            tiles = ds(g * GT, GT)
            s(nc.gpsimd.tensor_copy(first, node_of_rank[:, tiles, 1]))
            s(nc.gpsimd.tensor_copy(left, node_of_rank[:, tiles, 2]))
            s.settle()
            s(nc.gpsimd.tensor_tensor(first, first, done, ALU.add))
            s(nc.gpsimd.tensor_tensor(left, left, done, ALU.subtract))
            s.settle()
            s(nc.gpsimd.tensor_scalar(first, first, float(EP - K), None, ALU.min))
            s(nc.gpsimd.tensor_scalar(done, done, float(K), None, ALU.add))
            s.settle()
            s(nc.gpsimd.tensor_copy(more_idx[:, :], first))
            s.settle()
            for i in range(GT):
                gather(more[:, i, :, :].rearrange("p k two -> p (k two)"), edges, more_idx[:, i:i + 1]).then_inc(more_in, 16)
            hold(pool, more_in, loads * (16 * GT) + 16 * GT)
            source, ok = more_f[:, 0, :, :], more_f[:, 1, :, :]
            s(nc.gpsimd.tensor_copy(source, more[:, :, :, 0]))
            s(nc.gpsimd.tensor_tensor(ok, left[:, :, None].to_broadcast([P, GT, K]),
                                      slot_k[:, None, :].to_broadcast([P, GT, K]), ALU.subtract))
            s.settle()
            s(nc.gpsimd.tensor_scalar(ok, ok, 0.0, 1.0, ALU.max, ALU.min))
            s.settle()
            if kind == "dense":
                s(nc.gpsimd.tensor_copy(more_f[:, 2, :, 0], row_base[:, tiles]))
                s(nc.gpsimd.tensor_scalar(source, source, float(GTP), None, ALU.mult))
                s.settle()
                s(nc.gpsimd.tensor_tensor(source, source, more_f[:, 2, :, 0:1].to_broadcast([P, GT, K]), ALU.add))
                s.settle()
                s(nc.gpsimd.tensor_tensor(source, source, dummy_at[:, :, :], ALU.subtract))
                s.settle()
                s(nc.gpsimd.tensor_tensor(source, source, ok, ALU.mult))
                s.settle()
                s(nc.gpsimd.tensor_tensor(source, source, dummy_at[:, :, :], ALU.add))
                s.settle()
            else:
                s(nc.gpsimd.tensor_scalar(source, source, float(-PAD), None, ALU.add))
                s.settle()
                s(nc.gpsimd.tensor_tensor(source, source, ok, ALU.mult))
                s.settle()
                s(nc.gpsimd.tensor_scalar(source, source, float(PAD), None, ALU.add))
                s.settle()
            s(nc.gpsimd.tensor_copy(more[:, :, :, 0], source))
            value = more[:, :, :, 1].bitcast(F32)
            if kind == "pna":
                s(nc.gpsimd.tensor_scalar(value, ok, 2 * LOW, -2 * LOW, ALU.mult, ALU.add))
            else:
                s(nc.gpsimd.tensor_tensor(value, value, ok, ALU.mult))
            s.settle()
            s(nc.gpsimd.tensor_copy(table[:, tiles, :, :], more[:, :, :, :]))
            s.settle()
            assert s.n == RELOAD_STEPS[kind], s.n

        def pool_rounds(pool, name, table, kind, before_round, issue, before_group=None, after_group=None):
            staged, reloaded = sem(f"{name}_staged"), sem(f"{name}_reloaded")
            phase_reset, more_in = sem(f"{name}_reset"), sem(f"{name}_more_in")
            it_reg, pos_reg, room_reg, load_reg = (pool.alloc_register(f"{name}_{r}") for r in
                                                   ("it", "pos", "room", "loads"))
            pool.reg_mov(it_reg, 0)
            pool.reg_mov(load_reg, 0)
            with pool.Fori(0, NG) as g:
                if before_group is not None:
                    before_group(g)
                nc.gpsimd.memset(more_at[:, 2, :], 0.0).then_inc(phase_reset, 1)
                hold(pool, phase_reset, g + 1)
                count = pool.value_load(iters[0:1, ds(g, 1)], min_val=1, max_val=E)
                pool.reg_load(room_reg, iters[0:1, ds(g + NG, 1)])
                pool.reg_mov(pos_reg, 0)
                with pool.Fori(0, count):
                    room = pool.snap(room_reg, min_val=0, max_val=E)
                    with pool.If(room == 0):
                        loads = pool.snap(load_reg, min_val=0, max_val=E)
                        reload_table(pool, table, kind, g, loads, reloaded, more_in)
                        pool.reg_add(load_reg, load_reg, 1)
                        pool.reg_mov(room_reg, HALF)
                        pool.reg_mov(pos_reg, 0)
                    pool.reg_sub(room_reg, room_reg, 1)
                    pos = pool.snap(pos_reg, min_val=0, max_val=HALF - 1)
                    it = pool.snap(it_reg, min_val=0, max_val=NG * E)
                    for r in range(RND):
                        before_round(it, r)
                        nc.gpsimd.tensor_copy(stage[:, r, :, 0:2],
                                              table[:, ds(g * GT, GT), ds(pos * RND + r, 1), :]
                                              .rearrange("p t o two -> p (t o) two")).then_inc(staged, 1)
                        hold(pool, staged, it * RND + r + 1)
                        for i in range(GT):
                            issue(it, r, i)
                    pool.reg_add(it_reg, it_reg, 1)
                    pool.reg_add(pos_reg, pos_reg, 1)
                if after_group is not None:
                    after_group(pool.snap(it_reg, min_val=1, max_val=NG * E), g)

        def rounds(engine, name, body, before_group=None, after_group=None):
            it_reg = engine.alloc_register(f"{name}_it")
            engine.reg_mov(it_reg, 0)
            with engine.Fori(0, NG) as g:
                count = engine.value_load(iters[0:1, ds(g, 1)], min_val=1, max_val=E)
                if before_group is not None:
                    before_group(g, engine.snap(it_reg, min_val=0, max_val=NG * E))
                with engine.Fori(0, count):
                    body(g, engine.snap(it_reg, min_val=0, max_val=NG * E))
                    engine.reg_add(it_reg, it_reg, 1)
                if after_group is not None:
                    after_group(g, engine.snap(it_reg, min_val=1, max_val=NG * E))

        ph = ExitStack()
        psb1 = maker(ph)
        wt = psb1("wt", [P, WR, GTP, 2])
        turned_w = psb1("turned_w", [P, GT, GTP])
        xg = psb1("xg", [P, GW])
        xrank_in, group_built = sem("xrank_in"), sem("group_built")
        slot_done = [[sem(f"slot_done{r}{i}") for i in range(GT)] for r in range(RND)]
        block_in = [sem(f"block_in{i}") for i in range(WR)]
        xg_ready, turned, turned_read, part_done, agg_done = (sem(n) for n in (
            "xg_ready", "turned", "turned_read", "part_done", "agg_done"))
        zero_lane = [sem(f"zero_lane{i}") for i in range(2)]
        xt_in, out_deg_ready, out_dev_ready, step1 = (sem(n) for n in ("xt_in", "out_deg_ready", "out_dev_ready", "step1"))
        blocks = dense[0:NP * NP, :].rearrange("(g s p n) two -> (g s) p (n two)", g=NG, s=NT, p=P)

        with nc.Block() as block:
            @block.gpsimd
            def _(pool):
                for t in range(NT):
                    gather(big_a[:, t * D:(t + 1) * D], x, node_of_rank[:, t, 0:1]).then_inc(xrank_in, 16)
                for i in range(GT):
                    pool.dma_start(dense[DUMMY + i * P:DUMMY + (i + 1) * P, :], zeros[:, 0:2]
                                   ).then_inc(slot_done[RND - 1][i], 16)

                def before_group(g):
                    hold(pool, part_zero, g + 1)

                def issue(it, r, i):
                    hold(pool, slot_done[1 - r][i], (it + 1) * 16)
                    scatter(dense, stage[:, r, i, 0:1], stage[:, r, i, 1:3].bitcast(F32),
                            compute_op=ALU.add).then_inc(slot_done[r][i], 16)

                def built(it, g):
                    for i in range(GT):
                        hold(pool, slot_done[1][i], (it + 1) * 16)
                    pool.sem_inc(group_built, 1)

                pool_rounds(pool, "dense", tab_dense, "dense", lambda it, r: None, issue, before_group, built)

            @block.sync
            def _(sp):
                sp.dma_start(big_b[:, :].rearrange("p (h n) -> p h n", h=2), xT.rearrange("(h p) n -> p h n", p=P)
                             ).then_inc(xt_in, 16)
                for j in (WR - 2, WR - 1):
                    sp.sem_inc(block_in[j], 16)
                for t in range(ZERO_B, 2 * NT):
                    n = (t - ZERO_B) // 2
                    if n > 0:
                        sp.wait_ge(zero_lane[t % 2], 16 * n)
                    sp.dma_start(rows[t], zeros[:, :]).then_inc(zero_lane[t % 2], 16)
                    if t % ZG == ZG - 1:
                        for lane in range(2):
                            sp.wait_ge(zero_lane[lane], 16 * (n + 1))
                        sp.sem_inc(part_zero, 1)
                with sp.Fori(0, NG) as g:
                    hold(sp, group_built, g + 1)
                    with sp.Fori(0, NT // GT) as q:
                        for j in range(GT):
                            hold(sp, turned, g * NT + q * GT + (j + 1))
                            hold(sp, block_in[(j - 2) % WR], g * (16 * NT // GT) + q * 16 + 16)
                            sp.dma_start(wt[:, j, :, :].rearrange("p n two -> p (n two)"),
                                         blocks[ds(g * NT + q * GT + j, 1), :, :].rearrange("o p n -> (o p) n")
                                         ).then_inc(block_in[j], 16)
                sp.wait_ge(xt_in, 16)
                for j in range(WR):
                    sp.wait_ge(block_in[j], 16 * NG * (NT // GT) + (16 if j >= WR - 2 else 0))

            @block.tensor
            def _(pe):
                count_ends(pe, banks[:, 0, 0:NT], NCH)
                pe.wait_ge(out_deg_ready, 1)
                pe.sem_inc(turned, WR)
                with pe.Fori(0, NG) as g:
                    hold(pe, xg_ready, g + 1)
                    with pe.Fori(0, NT // GT) as q:
                        for j in range(GT):
                            hold(pe, block_in[j], g * (16 * NT // GT) + q * 16 + (32 if j >= WR - 2 else 16))
                            hold(pe, turned_read, g * NT + q * GT + (j + (2 if j == 0 else 1)))
                            for i in range(GT):
                                last = nc.tensor.transpose(flat[:, (j % 2) * 1024 + i * P:(j % 2) * 1024 + (i + 1) * P],
                                                           wt[:, j, i * P:(i + 1) * P, 0], ident[:, :])
                            last.then_inc(turned, 1)
                        for half in range(2):
                            hold(pe, turned_read, g * NT + q * GT + (2 + (3, 5)[half]))
                            for h in range(2):
                                part = half * 2 + h
                                hold(pe, agg_done, g * 20 + q * 4 + (part + 1))
                                for i in range(GT):
                                    last = nc.tensor.matmul(banks[:, 4 + part, 0:HGT],
                                                            xg[:, i * D + h * P:i * D + (h + 1) * P],
                                                            turned_w[:, i, half * HGT:(half + 1) * HGT],
                                                            start=i == 0, stop=i == GT - 1)
                                last.then_inc(part_done, 1)

            @block.scalar
            def _(act):
                act.wait_ge(out_deg_ready, 1)
                nc.scalar.activation(out_scale[:, :], out_scale[:, :], ACT.Sqrt).then_inc(out_dev_ready, 1)
                act.sem_inc(turned_read, 2)
                with act.Fori(0, NG) as g:
                    with act.Fori(0, NT // GT) as q:
                        for j in range(GT):
                            hold(act, turned, g * NT + q * GT + (WR + j + 1))
                            nc.scalar.activation(turned_w[:, :, j * P:(j + 1) * P],
                                                 flat[:, (j % 2) * 1024:(j % 2) * 1024 + GTP].rearrange(
                                                     "p (i n) -> p i n", i=GT), ACT.Copy).then_inc(turned_read, 1)

            @block.vector
            def _(dve):
                s = Steps(dve, step1)
                one_hots(dve, s, 1, NCH)
                dve.wait_ge(hot_used, 2 * NCH)
                nc.vector.tensor_scalar(out_scale[:, :], banks[:, 0, 0:NT], 1.0, None, ALU.max).then_inc(out_deg_ready, 1)
                dve.wait_ge(out_dev_ready, 1)
                s(nc.vector.reciprocal(out_scale[:, :], out_scale[:, :]))
                dve.sem_inc(agg_done, 4)
                dve.sem_inc(part_done, 1)
                dve.wait_ge(xt_in, 16)
                dve.wait_ge(xrank_in, 16 * NT)
                with dve.Fori(0, NG) as g:
                    hold(dve, part_done, g * 20 + 1)
                    nc.vector.tensor_copy(xg[:, :], big_a[:, ds(g * GW, GW)]).then_inc(xg_ready, 1)
                    with dve.Fori(0, NT // GT) as q:
                        for half in range(2):
                            for h in range(2):
                                part = half * 2 + h
                                hold(dve, part_done, g * 20 + q * 4 + (part + 2))
                                hold(dve, agg_done, g * 20 + q * 4 + (part + 1))
                                at = big_b[:, ds(q * GTP + (h * NP + half * HGT), HGT)]
                                nc.vector.tensor_tensor(at, at, banks[:, 4 + part, 0:HGT], ALU.add).then_inc(agg_done, 1)
        ph.close()
        prep.close()

        big_d = sb("big_d", [P, NT * D])
        in_scale = sb("in_scale", [P, NT])
        deg_inv = sb("deg_inv", [P, NT])
        has = sb("has", [P, NT])
        amp = sb("amp", [P, NT])
        att = sb("att", [P, NT])
        late = ExitStack()
        h1 = maker(late)("h1", [P, NT * HID1])
        ph = ExitStack()
        psb2 = maker(ph)
        w1 = psb2("w1", [P, 2, HID0])
        w2 = psb2("w2", [P, HID0 // P, D])
        wc = psb2("wc", [P, 2, HID1])
        b1 = psb2("b1", [P, HID0 // P])
        b2 = psb2("b2", [P, D])
        hid = psb2("hid", [P, HID0 // P, GT * P])
        yg = psb2("yg", [P, GT, D])
        x1g = psb2("x1g", [P, GT, D])
        x1t = psb2("x1t", [P, 2, GT * P])
        w_in2, x_in2, hid_psum, hid_ready, out_psum, y_ready, step2, stored = (sem(n) for n in (
            "w_in2", "x_in2", "hid_psum", "hid_ready", "out_psum", "y_ready", "step2", "stored"))
        x1_ready, x1_out, t_psum, t_ready, h_psum, h1_ready, pna_step = (sem(n) for n in (
            "x1_ready", "x1_out", "t_psum", "t_ready", "h_psum", "h1_ready", "pna_step"))
        var2, dev2 = sem("var2"), sem("dev2")
        five = flat[:, 6 * 512:6 * 512 + GTP]
        STEP2 = 7

        with nc.Block() as block:
            @block.sync
            def _(sp):
                sp.dma_start(w1[:, :, :], L0_W1.rearrange("(k p) m -> p k m", p=P)).then_inc(w_in2, 16)
                sp.dma_start(w2[:, :, :], L0_W2.rearrange("(k p) m -> p k m", p=P)).then_inc(w_in2, 16)
                sp.dma_start(wc[:, :, :], L1_Wc.rearrange("(k p) m -> p k m", p=P)).then_inc(w_in2, 16)
                sp.dma_start(b1[:, :], L0_b1).then_inc(w_in2, 16)
                sp.dma_start(b2[:, :], L0_b2.to_broadcast([P, D])).then_inc(w_in2, 16)
                sp.dma_start(big_c[:, :].rearrange("p (t d) -> p t d", t=NT), x.rearrange("(t p) d -> p t d", p=P)
                             ).then_inc(x_in2, 16)
                x1_rows = x1_dram.rearrange("(g t p) d -> g p t d", t=GT, p=P)
                sp.sem_inc(stored, 1)
                with sp.Fori(0, NG) as g:
                    hold(sp, x1_ready, g * GT + GT)
                    sp.dma_start(x1_rows[ds(g, 1), :, :, :].rearrange("o p t d -> p (o t) d"), x1g[:, :, :]
                                 ).then_inc(x1_out, 16)
                    hold(sp, x1_out, g * 16 + 16)
                    sp.sem_inc(stored, 1)
                sp.wait_ge(x_in2, 16)
                sp.wait_ge(x1_out, 16 * NG)

            @block.gpsimd
            def _(pool):
                s = Steps(pool, pna_step)
                s(nc.gpsimd.tensor_tensor(tab_pna[:, :, :, 1].bitcast(F32),
                                          deg_rank[:, :, None].to_broadcast([P, NT, K]),
                                          slot_k[:, None, :].to_broadcast([P, NT, K]), ALU.subtract))
                s.settle()
                s(nc.gpsimd.tensor_scalar(tab_pna[:, :, :, 1].bitcast(F32), tab_pna[:, :, :, 1].bitcast(F32),
                                          0.0, 1.0, ALU.max, ALU.min))
                s.settle()
                s(nc.gpsimd.tensor_scalar(tab_pna[:, :, :, 1].bitcast(F32), tab_pna[:, :, :, 1].bitcast(F32),
                                          2 * LOW, -2 * LOW, ALU.mult, ALU.add))

            @block.tensor
            def _(pe):
                pe.wait_ge(w_in2, 16 * 5)
                pe.sem_inc(out_psum, 1)
                with pe.Fori(0, NG) as g:
                    for c in range(HID0 // P):
                        pair = 2 * (c % 2)
                        hold(pe, hid_ready, g * 4 + (c + 1))
                        for h in range(2):
                            for k in range(2):
                                last = nc.tensor.matmul(banks[:, pair + h, 0:HGT], w1[:, k, c * P:(c + 1) * P],
                                                        big_b[:, ds(g * GTP + (k * NP + h * HGT), HGT)],
                                                        start=k == 0, stop=k == 1)
                        last.then_inc(hid_psum, 1)
                    hold(pe, hid_ready, g * 4 + 6)
                    for i in range(GT):
                        hold(pe, y_ready, g * GT + (i + (2 if i == 0 else 1)))
                        for c in range(4):
                            last = nc.tensor.matmul(banks[:, 4 + i % 2, 0:D], hid[:, c, i * P:(i + 1) * P], w2[:, c, :],
                                                    start=c == 0, stop=c == 3)
                        last.then_inc(out_psum, 1)
                    hold(pe, x1_ready, g * GT + GT)
                    hold(pe, h1_ready, g * GT + 1)
                    for k in range(2):
                        hold(pe, t_ready, g * 2 + (1 + k))
                        for i in range(GT):
                            last = nc.tensor.transpose(five[:, i * P:(i + 1) * P], x1g[:, i, k * P:(k + 1) * P], ident[:, :])
                        last.then_inc(t_psum, 1)
                    hold(pe, t_ready, g * 2 + 3)
                    for i in range(GT):
                        for k in range(2):
                            last = nc.tensor.matmul(five[:, i * P:(i + 1) * P], x1t[:, k, i * P:(i + 1) * P], wc[:, k, :],
                                                    start=k == 0, stop=k == 1)
                    last.then_inc(h_psum, 1)

            @block.scalar
            def _(act):
                act.wait_ge(w_in2, 16 * 5)
                act.sem_inc(hid_ready, 2)
                act.sem_inc(t_ready, 1)
                act.sem_inc(h1_ready, 1)
                with act.Fori(0, NG) as g:
                    hold(act, out_psum, g * GT + 1)
                    for c in range(HID0 // P):
                        pair = 2 * (c % 2)
                        hold(act, hid_psum, g * 4 + (c + 1))
                        nc.scalar.activation(hid[:, c, :].rearrange("p (h n) -> p h n", h=2), banks[:, pair:pair + 2, 0:HGT],
                                             ACT.Relu, bias=b1[:, c:c + 1]).then_inc(hid_ready, 1)
                    deviation(act, g, var2, dev2)
                    for k in range(2):
                        hold(act, t_psum, g * 2 + (k + 1))
                        nc.scalar.activation(x1t[:, k, :], five, ACT.Copy).then_inc(t_ready, 1)
                    hold(act, h_psum, g + 1)
                    for i in range(GT):
                        nc.scalar.activation(h1[:, ds(g * (GT * HID1) + i * HID1, HID1)], five[:, i * P:(i + 1) * P], ACT.Copy,
                                             scale=out_scale[:, ds(g * GT + i, 1)]).then_inc(h1_ready, 1)

            @block.vector
            def _(dve):
                dve.wait_ge(w_in2, 16 * 5)
                dve.wait_ge(x_in2, 16)
                dve.sem_inc(y_ready, 2)
                with dve.Fori(0, NG) as g:
                    s = Steps(dve, step2, g * STEP2, (const_step, CONSTS))
                    for i in range(GT):
                        hold(dve, out_psum, g * GT + (i + 2))
                        nc.vector.tensor_tensor(yg[:, i, :], banks[:, 4 + i % 2, 0:D],
                                                big_c[:, ds(g * GW + i * D, D)], ALU.add).then_inc(y_ready, 1)
                    hold(dve, y_ready, g * GT + (GT + 2))
                    s(nc.vector.tensor_tensor(yg[:, :, :], yg[:, :, :], b2[:, None, :].to_broadcast([P, GT, D]), ALU.add))
                    hold(dve, stored, g + 1)
                    hold(dve, h1_ready, g * GT + 1)
                    layer_norm(dve, s, lambda i: yg[:, i, :], lambda i: x1g[:, i, :],
                               lambda i, ins: ins.then_inc(x1_ready, 1), g, var2, dev2)
                    assert s.n == STEP2, s.n
        ph.close()

        recycle_sems()

        ph = ExitStack()
        psb3 = maker(ph)
        wt3 = psb3("wt3", [P, WR, GTP, 2])
        w1t = psb3("w1t", [P, HID1])
        w2t = psb3("w2t", [P, D])
        wp = psb3("wp", [P, 2, D])
        whq = psb3("whq", [P, 2, 2 * D])
        bc, b1c, b2c, bq, bp = (psb3(n, [P, m]) for n, m in (("bc", 1), ("b1c", 1), ("b2c", D), ("bq", D), ("bp", D)))
        ones3 = psb3("ones3", [P, P])
        diag = psb3("diag", [P, GTP])
        scale_row = psb3("scale_row", [P, GTP])
        hmt = psb3("hmt", [P, GTP])
        h2t = psb3("h2t", [P, GTP])
        y4 = psb3("y4", [P, GT, D])
        x2t = psb3("x2t", [P, 2, GTP])
        block3_in = [sem(f"block3_in{i}") for i in range(WR)]
        x1rank_in, step3, log_done, in_deg_ready, ones_set, diag_ready, scale_psum, scale_ready = (sem(n) for n in (
            "x1rank_in", "step3", "log_done", "in_deg_ready", "ones_set", "diag_ready", "scale_psum", "scale_ready"))
        block_used, sum_read, w_in4, hmt_ready, h2_psum, h2_ready, out4_psum, y4_ready = (sem(n) for n in (
            "block_used", "sum_read", "w_in4", "hmt_ready", "h2_psum", "h2_ready", "out4_psum", "y4_ready"))
        x2_ready, x2t_psum, x2t_ready, pq_psum, p_ready, q_ready, step4, p_out = (sem(n) for n in (
            "x2_ready", "x2t_psum", "x2t_ready", "pq_psum", "p_ready", "q_ready", "step4", "p_out"))
        var4, dev4 = sem("var4"), sem("dev4")
        STEP4 = 7
        halves = banks[:, 0:2, 0:HGT]

        def load_blocks(sp, ring, landed, used_sem):
            with sp.Fori(0, NT) as q:
                for j in range(WR):
                    hold(sp, used_sem, q * WR + (j + 1))
                    sp.dma_start(ring[:, j, :, :].rearrange("p n two -> p (n two)"),
                                 blocks[ds(q * WR + j, 1), :, :].rearrange("o p n -> (o p) n")).then_inc(landed[j], 16)
            for j in range(WR):
                sp.wait_ge(landed[j], 16 * NT)

        with nc.Block() as block:
            @block.sync
            def _(sp):
                sp.sem_inc(block_used, WR)
                load_blocks(sp, wt3, block3_in, block_used)

            @block.gpsimd
            def _(pool):
                nc.gpsimd.memset(ones3[:, :], 1.0).then_inc(ones_set, 1)
                pool.dma_start(w1t[:, :], L1_W1T).then_inc(w_in4, 16)
                pool.dma_start(w2t[:, :], L1_W2T).then_inc(w_in4, 16)
                pre = L2_preW.rearrange("(h k p) m -> h p k m", h=2, p=P)
                pool.dma_start(wp[:, :, :], pre[0]).then_inc(w_in4, 16)
                pool.dma_start(whq[:, :, D:2 * D], pre[1]).then_inc(w_in4, 16)
                pool.dma_start(whq[:, :, 0:D], L2_postW[0:D, :].rearrange("(k p) m -> p k m", p=P)).then_inc(w_in4, 16)
                pool.dma_start(bc[:, :], L1_bc).then_inc(w_in4, 16)
                pool.dma_start(b1c[:, :], L1_b1).then_inc(w_in4, 16)
                for a, b in ((b2c, L1_b2), (bq, L2_preb), (bp, L2_postb)):
                    pool.dma_start(a[:, :], b.to_broadcast([P, D])).then_inc(w_in4, 16)
                for t in range(NT):
                    gather(big_a[:, t * D:(t + 1) * D], x1_dram, node_of_rank[:, t, 0:1]).then_inc(x1rank_in, 16)
                pool.wait_ge(x1rank_in, 16 * NT)
                for t in range(NT):
                    pool.wait_ge(p_ready, t + 2)
                    scatter(p2_dram, node_of_rank[:, t, 0:1], big_a[:, t * D:(t + 1) * D]).then_inc(p_out, 16)
                pool.wait_ge(p_out, 16 * NT)

            @block.tensor
            def _(pe):
                def scales(g):
                    pe.wait_ge(x2t_ready, g * 2 + 1)
                    pe.wait_ge(diag_ready, g + 1)
                    for i in range(GT):
                        last = nc.tensor.matmul(five[:, i * P:(i + 1) * P], ones3[:, :], diag[:, i * P:(i + 1) * P],
                                                start=True, stop=True)
                    last.then_inc(scale_psum, 1)

                def first_product(g):
                    pe.wait_ge(hmt_ready, g + 1)
                    pe.wait_ge(q_ready, g * GT + 2)
                    for h in range(2):
                        last = nc.tensor.matmul(banks[:, 2 + h, 0:HGT], w1t[:, :], hmt[:, h * HGT:(h + 1) * HGT],
                                                start=True, stop=True)
                    last.then_inc(h2_psum, 1)

                def second_product(g):
                    pe.wait_ge(h2_ready, g + 1)
                    pe.wait_ge(p_ready, g * GT + 1)
                    for i in range(GT):
                        pe.wait_ge(y4_ready, g * GT + i + (2 if i == 0 else 1))
                        nc.tensor.matmul(banks[:, 4 + i % 2, 0:D], h2t[:, i * P:(i + 1) * P], w2t[:, :],
                                         start=True, stop=True).then_inc(out4_psum, 1)

                def turn_x2(g, k):
                    pe.wait_ge(x2_ready, g * GT + GT)
                    pe.wait_ge(scale_ready, g + 1)
                    pe.wait_ge(x2t_ready, g * 2 + 1 + k)
                    for i in range(GT):
                        last = nc.tensor.transpose(five[:, i * P:(i + 1) * P],
                                                   big_c[:, g * GW + i * D + k * P:g * GW + i * D + (k + 1) * P], ident[:, :])
                    last.then_inc(x2t_psum, 1)

                def pna_products(g, i):
                    pe.wait_ge(x2t_ready, g * 2 + 3)
                    pe.wait_ge(y4_ready, g * GT + GT + 2)
                    if i > 0:
                        pe.wait_ge(p_ready, g * GT + i)
                        pe.wait_ge(q_ready, g * GT + (i + 1))
                    for k in range(2):
                        nc.tensor.matmul(banks[:, 4 + i % 2, 0:D], x2t[:, k, i * P:(i + 1) * P], wp[:, k, :],
                                         start=k == 0, stop=k == 1)
                    for k in range(2):
                        last = nc.tensor.matmul(banks[:, 2 + i % 2, :], x2t[:, k, i * P:(i + 1) * P], whq[:, k, :],
                                                start=k == 0, stop=k == 1)
                    last.then_inc(pq_psum, 1)

                between = {1: lambda g: first_product(g), 3: lambda g: second_product(g),
                           15: lambda g: turn_x2(g, 0), 17: lambda g: turn_x2(g, 1)}
                for i in range(GT):
                    between[19 + i] = lambda g, i=i: pna_products(g, i)
                pe.wait_ge(ones_set, 1)
                for g in range(NG):
                    pe.wait_ge(sum_read, g + 1)
                    for b in range(NT):
                        if g > 0 and b in between:
                            between[b](g - 1)
                        pe.wait_ge(block3_in[b % WR], g * (16 * NT // WR) + 16 * (b // WR + 1))
                        for h in range(2):
                            last = nc.tensor.matmul(banks[:, h, 0:HGT], h1[:, b * HID1:(b + 1) * HID1],
                                                    wt3[:, b % WR, h * HGT:(h + 1) * HGT, 1],
                                                    start=b == 0, stop=b == NT - 1)
                        last.then_inc(block_used, 1)
                    scales(g)
                    pe.wait_ge(w_in4, 160)
                for b in sorted(between):
                    between[b](NG - 1)

            @block.scalar
            def _(act):
                nc.scalar.activation(amp[:, :], deg_rank[:, :], ACT.Ln, bias=1.0).then_inc(log_done, 1)
                act.wait_ge(in_deg_ready, 1)
                nc.scalar.activation(in_scale[:, :], in_scale[:, :], ACT.Sqrt).then_inc(log_done, 1)
                act.wait_ge(w_in4, 160)
                act.wait_ge(x1rank_in, 16 * NT)
                act.sem_inc(p_ready, 1)
                act.sem_inc(x2t_ready, 1)

                with act.Fori(0, NG) as g:
                    hold(act, scale_psum, g + 1)
                    hold(act, sum_read, g + 1)
                    nc.scalar.activation(scale_row[:, :], five, ACT.Copy).then_inc(scale_ready, 1)
                    hold(act, sum_read, g + 2)
                    nc.scalar.activation(hmt[:, :], hmt[:, :], ACT.Relu, bias=bc[:, :]).then_inc(hmt_ready, 1)
                    hold(act, h2_psum, g + 1)
                    nc.scalar.activation(h2t[:, :].rearrange("p (h n) -> p h n", h=2), banks[:, 2:4, 0:HGT],
                                         ACT.Relu, bias=b1c[:, :]).then_inc(h2_ready, 1)
                    deviation(act, g, var4, dev4)
                    for k in range(2):
                        hold(act, x2t_psum, g * 2 + (k + 1))
                        nc.scalar.activation(x2t[:, k, :], five, ACT.Copy).then_inc(x2t_ready, 1)
                    for i in range(GT):
                        hold(act, pq_psum, g * GT + (i + 1))
                        nc.scalar.activation(big_a[:, ds(g * GW + i * D, D)], banks[:, 4 + i % 2, 0:D], ACT.Copy
                                             ).then_inc(p_ready, 1)

            @block.vector
            def _(dve):
                s = Steps(dve, step3)
                nc.vector.tensor_scalar(in_scale[:, :], deg_rank[:, :], 1.0, None, ALU.max).then_inc(in_deg_ready, 1)
                s(nc.vector.tensor_scalar(deg_inv[:, :], deg_rank[:, :], 1.0, None, ALU.max))
                s(nc.vector.tensor_scalar(has[:, :], deg_rank[:, :], 1.0, None, ALU.min))
                dve.wait_ge(log_done, 2)
                s(nc.vector.tensor_scalar(att[:, :], amp[:, :], EPS, None, ALU.max))
                s.settle()
                s(nc.vector.reciprocal(att[:, :], att[:, :]))
                s(nc.vector.reciprocal(in_scale[:, :], in_scale[:, :]))
                s(nc.vector.reciprocal(deg_inv[:, :], deg_inv[:, :]))
                s.settle()
                s(nc.vector.tensor_scalar(att[:, :], att[:, :], AVG_D, None, ALU.mult))
                s(nc.vector.tensor_scalar(amp[:, :], amp[:, :], 1.0 / AVG_D, None, ALU.mult))
                dve.sem_inc(sum_read, 1)
                dve.sem_inc(y4_ready, 2)
                dve.sem_inc(q_ready, 2)

                dve.wait_ge(w_in4, 160)
                dve.wait_ge(x1rank_in, 16 * NT)
                with dve.Fori(0, NG) as g:
                    s = Steps(dve, step4, g * STEP4, (const_step, CONSTS))
                    nc.vector.tensor_tensor(diag[:, :].rearrange("p (t n) -> p t n", t=GT),
                                            ident[:, None, :].to_broadcast([P, GT, P]),
                                            in_scale[:, ds(g * GT, GT), None].to_broadcast([P, GT, P]), ALU.mult
                                            ).then_inc(diag_ready, 1)
                    hold(dve, block_used, g * NT + (NT + WR))
                    hold(dve, scale_ready, g + 1)
                    nc.vector.tensor_tensor(hmt[:, :].rearrange("p (h n) -> p h n", h=2), halves,
                                            scale_row[:, :].rearrange("p (h n) -> p h n", h=2), ALU.mult
                                            ).then_inc(sum_read, 1)
                    for i in range(GT):
                        hold(dve, out4_psum, g * GT + (i + 1))
                        nc.vector.tensor_tensor(y4[:, i, :], banks[:, 4 + i % 2, 0:D],
                                                big_a[:, ds(g * GW + i * D, D)], ALU.add).then_inc(y4_ready, 1)
                    hold(dve, y4_ready, g * GT + (GT + 2))
                    s(nc.vector.tensor_tensor(y4[:, :, :], y4[:, :, :], b2c[:, None, :].to_broadcast([P, GT, D]), ALU.add))
                    layer_norm(dve, s, lambda i: y4[:, i, :], lambda i: big_c[:, ds(g * GW + i * D, D)],
                               lambda i, ins: ins.then_inc(x2_ready, 1), g, var4, dev4)
                    for i in range(GT):
                        hold(dve, pq_psum, g * GT + (i + 1))
                        at = ds(g * GW + i * D, D)
                        nc.vector.tensor_tensor(big_d[:, at], banks[:, 2 + i % 2, 0:D], bp[:, :], ALU.add)
                        nc.vector.tensor_tensor(big_b[:, at], banks[:, 2 + i % 2, D:2 * D], bq[:, :], ALU.add
                                                ).then_inc(q_ready, 1)
                    assert s.n == STEP4, s.n
        ph.close()
        late.close()

        recycle_sems()

        late = ExitStack()
        psb5 = maker(late)
        gath = psb5("gath", [P, RND, GT, D])
        z = psb5("z", [P, RND, GW])
        ms = psb5("ms", [P, RND, 2 * GW])
        nothing = psb5("nothing", [1, 512], BF16)
        wpost = psb5("wpost", [P, 8, 3 * D])
        wmix = psb5("wmix", [P, 2, D])
        bmix = psb5("bmix", [P, D])
        aggt = psb5("aggt", [P, 8, P])
        ht = psb5("ht", [P, D])
        htt = psb5("htt", [P, D])
        mean, mx, mn, std, y5 = (big_a[:, n * GW:(n + 1) * GW] for n in range(5))
        land = [[sem(f"land_{r}{i}") for i in range(GT)] for r in range(RND)]
        w_in5, used, z_ready, m_ready, max_done, sq_ready, sums_done = (sem(n) for n in (
            "w_in5", "used", "z_ready", "m_ready", "max_done", "sq_ready", "sums_done"))
        sums_final, evac_done, x3_ready, nothing_set, step5, var_ready, std_ready, mn_ready = (sem(n) for n in (
            "sums_final", "evac_done", "x3_ready", "nothing_set", "step5", "var_ready", "std_ready", "mn_ready"))
        t5_psum, t5_read, abc_psum, ht_ready, mix_psum, x3_out, w_used5 = (sem(n) for n in (
            "t5_psum", "t5_read", "abc_psum", "ht_ready", "mix_psum", "x3_out", "w_used5"))
        var5, dev5 = sem("var5"), sem("dev5")
        mix_read = sem("mix_read")
        STEP5 = 22

        with nc.Block() as block:
            @block.sync
            def _(sp):
                post = L2_postW[D:, :].rearrange("(s c p) m -> s p c m", s=3, p=P)
                for n in range(3):
                    sp.dma_start(wpost[:, :, n * D:(n + 1) * D], post[n]).then_inc(w_in5, 16)
                sp.dma_start(wmix[:, :, :], L2_mixW.rearrange("(k p) m -> p k m", p=P)).then_inc(w_in5, 16)
                sp.dma_start(bmix[:, :], L2_mixb.to_broadcast([P, D])).then_inc(w_in5, 16)
                sp.wait_ge(w_in5, 80)

            @block.gpsimd
            def _(pool):
                nc.gpsimd.memset(nothing[:, :], 0.0).then_inc(nothing_set, 1)

                def before_round(it, r):
                    hold(pool, used, it * SLOTS + (r + 1) * GT)

                def issue(it, r, i):
                    gather(gath[:, r, i, :], p2_dram, stage[:, r, i, 0:1]).then_inc(land[r][i], 16)

                pool_rounds(pool, "pna", tab_pna, "pna", before_round, issue)
                for t in range(NT):
                    pool.wait_ge(x3_ready, t + 2)
                    scatter(x3_dram, node_of_rank[:, t, 0:1], big_c[:, t * D:(t + 1) * D]).then_inc(x3_out, 16)
                pool.wait_ge(x3_out, 16 * NT)

            @block.vector
            def _(dve):
                dve.sem_inc(used, SLOTS)
                dve.sem_inc(max_done, RND)
                dve.sem_inc(x3_ready, 1)
                dve.sem_inc(ht_ready, 1)
                dve.sem_inc(mix_read, 1)
                dve.wait_ge(w_in5, 80)

                def before(g, it):
                    s = Steps(dve, step5, g * STEP5, (const_step, CONSTS))
                    s(nc.vector.memset(mx, 0.0))
                    s(nc.vector.memset(mn, -LOW))
                    s.settle()

                def body(g, it):
                    for r in range(RND):
                        hold(dve, m_ready, it * RND + (r + 1))
                        for i in range(GT):
                            hold(dve, land[r][i], it * 16 + 16)
                            last = nc.vector.tensor_tensor(z[:, r, i * D:(i + 1) * D], gath[:, r, i, :],
                                                           big_b[:, ds(g * GW + i * D, D)], ALU.add)
                        last.then_inc(z_ready, 1)
                        hold(dve, used, it * SLOTS + (r + 1) * GT + GT)
                        for i in range(GT):
                            at = mn[:, i * D:(i + 1) * D]
                            nc.vector.scalar_tensor_tensor(at, gath[:, r, i, :], stage[:, r, i, 1:2].bitcast(F32), at,
                                                           ALU.add, ALU.min).then_inc(used, 1)
                    for r in range(RND):
                        hold(dve, m_ready, it * RND + (r + 3))
                        hold(dve, max_done, it * RND + (r + 2))
                        nc.vector.tensor_tensor(mx, mx, ms[:, r, 0:GW], ALU.max).then_inc(max_done, 1)

                def after(g, it):
                    s = Steps(dve, step5, g * STEP5, (const_step, CONSTS))
                    s.n = 2
                    hold(dve, used, it * SLOTS + SLOTS)
                    hold(dve, max_done, it * RND + RND)
                    s(nc.vector.tensor_tensor(mn, mn, big_b[:, ds(g * GW, GW)], ALU.add))
                    hold(dve, evac_done, g + 2)
                    s(nc.vector.tensor_tensor(y5, mean, mean, ALU.mult))
                    s.settle()
                    s(nc.vector.tensor_tensor(std, std, y5, ALU.subtract))
                    s.settle()
                    nc.vector.tensor_scalar(std, std, 0.0, EPS, ALU.max, ALU.add).then_inc(var_ready, 1)
                    for i in range(GT):
                        at = mn[:, i * D:(i + 1) * D]
                        last = nc.vector.tensor_scalar(at, at, 0.0, has[:, ds(g * GT + i, 1)], ALU.max, ALU.mult)
                    last.then_inc(mn_ready, 1)
                    for i in range(GT):
                        tile = ds(g * GT + i, 1)
                        hold(dve, abc_psum, g * GT + (i + 1))
                        s(nc.vector.tensor_tensor(ht[:, :], banks[:, 6, 0:D], big_d[:, ds(g * GW + i * D, D)], ALU.add))
                        s.settle()
                        s(nc.vector.scalar_tensor_tensor(ht[:, :], banks[:, 6, D:2 * D], amp[:, tile], ht[:, :],
                                                         ALU.mult, ALU.add))
                        s.settle()
                        nc.vector.scalar_tensor_tensor(ht[:, :], banks[:, 7, 0:D], att[:, tile], ht[:, :],
                                                       ALU.mult, ALU.add).then_inc(ht_ready, 1)
                        hold(dve, mix_psum, g * GT + (i + 1))
                        nc.vector.tensor_tensor(y5[:, i * D:(i + 1) * D], banks[:, 7, D:2 * D], bmix[:, :], ALU.add
                                                ).then_inc(mix_read, 1)
                    hold(dve, mix_read, g * GT + (GT + 1))
                    s(nc.vector.scalar_tensor_tensor(y5, y5, 0.0, big_c[:, ds(g * GW, GW)], ALU.max, ALU.add))
                    layer_norm(dve, s, lambda i: y5[:, i * D:(i + 1) * D], lambda i: big_c[:, ds(g * GW + i * D, D)],
                               lambda i, ins: ins.then_inc(x3_ready, 1), g, var5, dev5)
                    assert s.n == STEP5, s.n

                rounds(dve, "pna_dve", body, before, after)

            @block.scalar
            def _(act):
                act.sem_inc(m_ready, RND)
                act.sem_inc(evac_done, 1)
                act.sem_inc(t5_read, 1)

                def body(g, it):
                    for r in range(RND):
                        hold(act, z_ready, it * RND + (r + 1))
                        hold(act, max_done, it * RND + (r + 1))
                        hold(act, sums_done, it * RND + (r + 1))
                        nc.scalar.activation(ms[:, r, 0:GW], z[:, r, :], ACT.Relu).then_inc(m_ready, 1)
                        hold(act, m_ready, it * RND + (r + 3))
                        nc.scalar.activation(ms[:, r, GW:2 * GW], ms[:, r, 0:GW], ACT.Square).then_inc(sq_ready, 1)

                def after(g, it):
                    hold(act, sums_final, g + 1)
                    hold(act, x3_ready, g * GT + 1)
                    for n, to in ((0, mean), (1, std)):
                        for i in range(GT):
                            last = nc.scalar.activation(to[:, i * D:(i + 1) * D], flat[:, n * GW + i * D:n * GW + (i + 1) * D],
                                                        ACT.Copy, scale=deg_inv[:, ds(g * GT + i, 1)])
                    last.then_inc(evac_done, 1)
                    hold(act, var_ready, g + 1)
                    nc.scalar.activation(std, std, ACT.Sqrt).then_inc(std_ready, 1)
                    for i in range(GT):
                        for q in range(2):
                            hold(act, t5_psum, g * (3 * GT) + (3 * i + q + 1))
                            nc.scalar.activation(aggt[:, 4 * q:4 * q + 4, :].rearrange("p c n -> p (c n)"), banks[:, 5, :],
                                                 ACT.Copy).then_inc(t5_read, 1)
                        hold(act, t5_psum, g * (3 * GT) + (3 * i + 3))
                        nc.scalar.activation(htt[:, :], banks[:, 5, 0:D], ACT.Relu).then_inc(t5_read, 1)
                    deviation(act, g, var5, dev5)

                rounds(act, "pna_act", body, None, after)

            @block.tensor
            def _(pe):
                pe.sem_inc(sums_done, RND)
                pe.wait_ge(w_in5, 80)
                pe.wait_ge(nothing_set, 1)

                def before(g, it):
                    hold(pe, evac_done, g + 1)
                    for b in range(5):
                        nc.tensor.matmul(banks[:, b, :], nothing[:, 0:P], nothing[:, :], start=True, stop=False)

                def body(g, it):
                    for r in range(RND):
                        hold(pe, sq_ready, it * RND + (r + 1))
                        for b in range(5):
                            last = nc.tensor.matmul(banks[:, b, :], ident[:, :], ms[:, r, b * 512:(b + 1) * 512],
                                                    start=False, stop=False)
                        last.then_inc(sums_done, 1)

                def after(g, it):
                    for b in range(5):
                        last = nc.tensor.matmul(banks[:, b, :], nothing[:, 0:P], nothing[:, :], start=False, stop=True)
                    last.then_inc(sums_final, 1)
                    hold(pe, mn_ready, g + 1)
                    hold(pe, std_ready, g + 1)
                    for i in range(GT):
                        for q in range(2):
                            hold(pe, t5_read, g * (3 * GT) + (3 * i + q + 1))
                            for c in range(4):
                                what = ((mean, mx), (mn, std))[q][c // 2]
                                last = nc.tensor.transpose(banks[:, 5, c * P:(c + 1) * P],
                                                           what[:, i * D + (c % 2) * P:i * D + (c % 2 + 1) * P], ident[:, :])
                            last.then_inc(t5_psum, 1)
                        hold(pe, t5_read, g * (3 * GT) + (3 * i + 3))
                        hold(pe, mix_read, g * GT + (i + 1))
                        for c in range(8):
                            nc.tensor.matmul(banks[:, 6, :], aggt[:, c, :], wpost[:, c, 0:2 * D], start=c == 0, stop=c == 7)
                        for c in range(8):
                            last = nc.tensor.matmul(banks[:, 7, 0:D], aggt[:, c, :], wpost[:, c, 2 * D:3 * D],
                                                    start=c == 0, stop=c == 7)
                        last.then_inc(abc_psum, 1)
                        hold(pe, ht_ready, g * GT + (i + 2))
                        for k in range(2):
                            last = nc.tensor.transpose(banks[:, 5, k * P:(k + 1) * P], ht[:, k * P:(k + 1) * P], ident[:, :])
                        last.then_inc(t5_psum, 1)
                        hold(pe, t5_read, g * (3 * GT) + (3 * i + 4))
                        for k in range(2):
                            last = nc.tensor.matmul(banks[:, 7, D:2 * D], htt[:, k * P:(k + 1) * P], wmix[:, k, :],
                                                    start=k == 0, stop=k == 1)
                        last.then_inc(mix_psum, 1)

                rounds(pe, "pna_pe", body, before, after)
        late.close()

        late = ExitStack()
        psb6 = maker(late)
        wt6 = psb6("wt6", [P, WR, GTP, 2])
        w6 = psb6("w6", [P, 2, D])
        b6 = psb6("b6", [P, D])
        st = psb6("st", [P, 2, GTP])
        y6 = psb6("y6", [P, GT, D])
        block6_in = [sem(f"block6_in{i}") for i in range(WR)]
        x3_in, w_in6, block_used6, st_ready, out6_psum, y6_ready, x4_ready, x4_out, step6 = (sem(n) for n in (
            "x3_in", "w_in6", "block_used6", "st_ready", "out6_psum", "y6_ready", "x4_ready", "x4_out", "step6"))
        var6, dev6 = sem("var6"), sem("dev6")
        STEP6 = 7

        with nc.Block() as block:
            @block.sync
            def _(sp):
                sp.dma_start(big_b[:, :].rearrange("p (t d) -> p t d", t=NT), x3_dram.rearrange("(t p) d -> p t d", p=P)
                             ).then_inc(x3_in, 16)
                sp.dma_start(w6[:, :, :], L3_W.rearrange("(k p) m -> p k m", p=P)).then_inc(w_in6, 16)
                sp.dma_start(b6[:, :], L3_b.to_broadcast([P, D])).then_inc(w_in6, 16)
                sp.sem_inc(block_used6, WR)
                load_blocks(sp, wt6, block6_in, block_used6)

            @block.tensor
            def _(pe):
                pe.wait_ge(x3_in, 16)
                pe.wait_ge(w_in6, 32)
                with pe.Fori(0, NG) as g:
                    hold(pe, st_ready, g * 4 + 4)
                    for b in range(NT):
                        hold(pe, block6_in[b % WR], g * (16 * NT // WR) + 16 * (b // WR + 1))
                        for k in range(2):
                            for h in range(2):
                                last = nc.tensor.matmul(banks[:, 2 * k + h, 0:HGT], big_b[:, b * D + k * P:b * D + (k + 1) * P],
                                                        wt6[:, b % WR, h * HGT:(h + 1) * HGT, 0],
                                                        start=b == 0, stop=b == NT - 1)
                        last.then_inc(block_used6, 1)
                    hold(pe, st_ready, g * 4 + 8)
                    for i in range(GT):
                        hold(pe, y6_ready, g * GT + (i + (2 if i == 0 else 1)))
                        for k in range(2):
                            last = nc.tensor.matmul(banks[:, 4 + i % 2, 0:D], st[:, k, i * P:(i + 1) * P], w6[:, k, :],
                                                    start=k == 0, stop=k == 1)
                        last.then_inc(out6_psum, 1)

            @block.scalar
            def _(act):
                act.sem_inc(st_ready, 4)
                act.sem_inc(out6_psum, 1)
                with act.Fori(0, NG) as g:
                    hold(act, block_used6, g * NT + (NT + WR))
                    hold(act, out6_psum, g * GT + 1)
                    for k in range(2):
                        for h in range(2):
                            nc.scalar.activation(st[:, k, h * HGT:(h + 1) * HGT], banks[:, 2 * k + h, 0:HGT], ACT.Copy
                                                 ).then_inc(st_ready, 1)
                    deviation(act, g, var6, dev6)

            @block.vector
            def _(dve):
                dve.wait_ge(w_in6, 32)
                dve.sem_inc(y6_ready, 2)
                dve.sem_inc(x4_ready, 1)
                with dve.Fori(0, NG) as g:
                    s = Steps(dve, step6, g * STEP6, (const_step, CONSTS))
                    hold(dve, x4_ready, g * GT + 1)
                    for i in range(GT):
                        hold(dve, out6_psum, g * GT + (i + 2))
                        nc.vector.tensor_tensor(y6[:, i, :], banks[:, 4 + i % 2, 0:D], b6[:, :], ALU.add
                                                ).then_inc(y6_ready, 1)
                    hold(dve, y6_ready, g * GT + (GT + 2))
                    s(nc.vector.scalar_tensor_tensor(y6[:, :, :].rearrange("p t d -> p (t d)"),
                                                     y6[:, :, :].rearrange("p t d -> p (t d)"), 0.0,
                                                     big_c[:, ds(g * GW, GW)], ALU.max, ALU.add))
                    layer_norm(dve, s, lambda i: y6[:, i, :], lambda i: big_d[:, ds(g * GW + i * D, D)],
                               lambda i, ins: ins.then_inc(x4_ready, 1), g, var6, dev6)
                    assert s.n == STEP6, s.n

            @block.gpsimd
            def _(pool):
                for t in range(NT):
                    pool.wait_ge(x4_ready, t + 2)
                    scatter(out, node_of_rank[:, t, 0:1], big_d[:, t * D:(t + 1) * D], bounds_check=N - 1,
                            oob_is_err=False).then_inc(x4_out, 16)
                pool.wait_ge(x4_out, 16 * NT)
        late.close()


def kernel(x, src, dst, edge_weight, L0_gnn_W1, L0_gnn_b1, L0_gnn_W2, L0_gnn_b2, L1_gnn_W_conv, L1_gnn_b_conv,
           L1_gnn_W1, L1_gnn_b1, L1_gnn_W2, L1_gnn_b2, L2_gnn_pre_W, L2_gnn_pre_b, L2_gnn_post_W, L2_gnn_post_b,
           L2_gnn_mix_W, L2_gnn_mix_b, L3_gnn_W, L3_gnn_b):
    import numpy as np
    from concourse import bacc
    from concourse.bass_utils import run_bass_kernel_spmd

    def rows(a, n, fill):
        a = np.asarray(a)
        return np.concatenate([a, np.full((n - a.shape[0],) + a.shape[1:], fill, a.dtype)])

    xp = rows(x, NP, 0)
    line = lambda a: np.asarray(a).reshape(1, -1)
    arrays = {
        "x": xp, "xT": np.ascontiguousarray(xp.T),
        "src": rows(src, EP, NP).reshape(P, EC), "dst": rows(dst, EP, NP).reshape(P, EC),
        "w": rows(edge_weight, EP, 0).reshape(P, EC),
        "L0_W1": L0_gnn_W1, "L0_b1": np.ascontiguousarray(np.asarray(L0_gnn_b1).reshape(-1, P).T),
        "L0_W2": L0_gnn_W2, "L0_b2": line(L0_gnn_b2),
        "L1_Wc": L1_gnn_W_conv, "L1_bc": np.asarray(L1_gnn_b_conv).reshape(-1, 1),
        "L1_W1T": np.ascontiguousarray(np.asarray(L1_gnn_W1).T), "L1_b1": np.asarray(L1_gnn_b1).reshape(-1, 1),
        "L1_W2T": np.ascontiguousarray(np.asarray(L1_gnn_W2).T), "L1_b2": line(L1_gnn_b2),
        "L2_preW": L2_gnn_pre_W, "L2_preb": line(L2_gnn_pre_b), "L2_postW": L2_gnn_post_W,
        "L2_postb": line(L2_gnn_post_b), "L2_mixW": L2_gnn_mix_W, "L2_mixb": line(L2_gnn_mix_b),
        "L3_W": L3_gnn_W, "L3_b": line(L3_gnn_b),
    }
    arrays = {f"in_{k}": np.ascontiguousarray(v) for k, v in arrays.items()}
    nc = bacc.Bacc("TRN2", target_bir_lowering=False, num_devices=1)
    args = [nc.dram_tensor(k, v.shape, mybir.dt.from_np(v.dtype), kind="ExternalInput").ap() for k, v in arrays.items()]
    out = nc.dram_tensor("out", (N, D), F32, kind="ExternalOutput").ap()
    build(nc, *args, out)
    result = run_bass_kernel_spmd(nc, [arrays], core_ids=[0])
    return result.results[0]["out"]
```

```python
from contextlib import ExitStack

import concourse.bass as bass
from concourse import mybir
from concourse.bass import IndirectOffsetOnAxis, ds

F32, I32, BF16 = mybir.dt.float32, mybir.dt.int32, mybir.dt.bfloat16
ALU, ACT, AX = mybir.AluOpType, mybir.ActivationFunctionType, mybir.AxisListType

P = 128
N, E, D = 3125, 53125, 256
HID0, HID1 = 512, 128
NT = -(-N // P)
NP = NT * P
GT = 5
NG = NT // GT
EC = -(-E // P)
EP = EC * P
K = 40
RND = 2
SLOTS = RND * GT
HALF = K // RND
PAD = NP
DUMMY = NP * NP
KEY = 4096
KEYCAP = 2047
CH = 32
NCH = EC // CH
DT0 = 13
GTP = GT * P
HGT = GTP // 2
WR = GT
GW = GT * D
EPS, AVG_D = 1e-5, 3.4965
LOW = -1e30
assert NP * NP + SLOTS * P < 1 << 24 and NCH * CH == EC and NG * GT == NT


class Steps:

    def __init__(self, engine, sem, base=0, spacer=None):
        self.engine, self.sem, self.base, self.n, self.spacer = engine, sem, base, 0, spacer

    def __call__(self, instruction):
        self.n += 1
        return instruction.then_inc(self.sem, 1)

    def settle(self):
        value = self.base + self.n
        if self.spacer is not None:
            value = self.engine.snap(self.engine.to_reg(value), min_val=1, max_val=1 << 30)
            self.engine.wait_ge(*self.spacer)
        self.engine.wait_ge(self.sem, value)


def build(nc, x, xT, src, dst, w, L0_W1, L0_b1, L0_W2, L0_b2, L1_Wc, L1_bc, L1_W1T, L1_b1, L1_W2T, L1_b2,
          L2_preW, L2_preb, L2_postW, L2_postb, L2_mixW, L2_mixb, L3_W, L3_b, out):
    def dram(name, shape, dt):
        return nc.dram_tensor(name, shape, dt, kind="Internal").ap()

    edges = dram("edges", (EP, 2), I32)
    keys_dram = dram("keys_dram", (1, NP), F32)
    ranked_dram = dram("ranked_dram", (NP, 4), I32)
    dense = dram("dense", (NP * NP + SLOTS * P, 2), F32)
    x1_dram = dram("x1_dram", (NP, D), F32)
    p2_dram = dram("p2_dram", (NP + 1, D), F32)
    x3_dram = dram("x3_dram", (NP, D), F32)

    whole = ExitStack()
    with whole:
        def maker(stack):
            return lambda name, shape, dt=F32: stack.enter_context(nc.sbuf_tensor(name, shape, dt))

        sb = maker(whole)

        used_sems = []

        def sem(name):
            used_sems.append(nc.alloc_semaphore(name))
            return used_sems[-1]

        def recycle_sems():
            nc.clear_and_free_semaphores(used_sems[1:])
            del used_sems[1:]
            nc.all_engine_barrier()

        banks = whole.enter_context(nc.psum_tensor("banks", [P, 8, 512], F32))
        flat = banks[:, :, :].rearrange("p b f -> p (b f)")

        ident = sb("ident", [P, P])
        node_of_rank = sb("node_of_rank", [P, NT, 4], I32)
        deg_rank = sb("deg_rank", [P, NT])
        iters = sb("iters", [P, 3 * NG], I32)
        slot_k = sb("slot_k", [P, K])
        tab_edge = sb("tab_edge", [P, NT, K, 2], I32)
        tab_pna = tab_edge
        row_base = sb("row_base", [P, NT])
        dummy_at = sb("dummy_at", [P, GT, K])
        out_scale = sb("out_scale", [P, NT])
        stage = sb("stage", [P, RND, GT, 3], I32)
        more = sb("more", [P, GT, K, 2], I32)
        more_f = sb("more_f", [P, 3, GT, K])
        more_at = sb("more_at", [P, 3, GT])
        more_idx = sb("more_idx", [P, GT], I32)
        big_a = sb("big_a", [P, NT * D])
        big_b = sb("big_b", [P, NT * D])
        big_c = sb("big_c", [P, NT * D])
        lowrow = sb("lowrow", [1, D])
        bn = sb("bn", [P, GT, 6])
        mv = sb("mv", [P, GT, 2])
        rstd = sb("rstd", [P, GT])
        dev = sb("dev", [P, GT])
        eps = sb("eps", [P, 1])

        const_step = sem("const_step")
        CONSTS = 11

        def hold(engine, semaphore, value):
            if not isinstance(value, int):
                value = engine.snap(engine.to_reg(value), min_val=1, max_val=1 << 30)
                engine.wait_ge(const_step, CONSTS)
            engine.wait_ge(semaphore, value)

        def bounded(engine, value, low, high):
            return engine.snap(engine.to_reg(value), min_val=low, max_val=high)

        def layer_norm(dve, steps, y, to, signal, g, var_ready, std_ready):
            steps.settle()
            for i in range(GT):
                steps(nc.vector.bn_stats(bn[:, i, :], y(i)))
            steps.settle()
            for i in range(GT):
                last = nc.vector.bn_aggr(mv[:, i, :], bn[:, i, :])
            last.then_inc(var_ready, 1)
            hold(dve, std_ready, g + 1)
            steps(nc.vector.reciprocal(rstd[:, :], dev[:, :]))
            steps.settle()
            for i in range(GT):
                signal(i, nc.vector.tensor_scalar(to(i), y(i), mv[:, i, 0:1], rstd[:, i:i + 1],
                                                  ALU.subtract, ALU.mult))

        def deviation(act, g, var_ready, std_ready):
            hold(act, var_ready, g + 1)
            nc.scalar.activation(dev[:, :], mv[:, :, 1], ACT.Sqrt, bias=eps[:, :]).then_inc(std_ready, 1)

        def gather(to, table, index):
            return nc.gpsimd.indirect_dma_start(to, None, table, IndirectOffsetOnAxis(ap=index, axis=0))

        def scatter(table, index, rows, **how):
            return nc.gpsimd.indirect_dma_start(table, IndirectOffsetOnAxis(ap=index, axis=0), rows, None, **how)

        prep = ExitStack()
        psb = maker(prep)
        onehot_lo = psb("onehot_lo", [P, 2, P, CH], BF16)
        onehot_hi = psb("onehot_hi", [P, EC, NT], BF16)
        iota_lo = psb("iota_lo", [P, P, CH], BF16)
        iota_hi = psb("iota_hi", [P, NT], BF16)
        end_i = psb("end_i", [P, 2, EC], I32)
        half_i = psb("half_i", [P, EC], I32)
        hi_b = psb("hi_b", [P, EC], BF16)
        lo_b = psb("lo_b", [P, EC], BF16)
        zeros = psb("zeros", [P, NP])
        tab_dense = psb("tab_dense", [P, NT, K, 2], I32)
        tmp = ExitStack()
        tsb = maker(tmp)
        w_in = tsb("w_in", [P, EC])
        pairs = tsb("pairs", [P, EC, 2], I32)
        before = tsb("before", [P, P])
        ones = tsb("ones", [P, P])
        node_id = tsb("node_id", [P, NT])
        deg = tsb("deg", [P, NT])
        total = tsb("total", [P, NT])
        running = tsb("running", [P, NT])
        first = tsb("first", [P, NT])
        key = tsb("key", [P, NT])
        neg_key = tsb("neg_key", [P, NT])
        key_t = tsb("key_t", [NT, P])
        key_row = tsb("key_row", [P, NP])
        junk = tsb("junk", [P, 2, NP], BF16)
        rank = tsb("rank", [P, NT])
        rank_i = tsb("rank_i", [P, NT], I32)
        ranked = tsb("ranked", [P, NT, 4], I32)
        valid = tsb("valid", [P, NT, K])
        srcf = tsb("srcf", [P, NT, K])
        work = tsb("work", [P, NT, K])
        gmax = tsb("gmax", [P, 2 * NG])
        gmax_all = tsb("gmax_all", [P, 2 * NG])
        gmax_i = tsb("gmax_i", [P, 2 * NG], I32)

        ends_in, w_read, edges_out = sem("ends_in"), sem("w_read"), sem("edges_out")
        zero_set, zero_out, part_zero = sem("zero_set"), [sem(f"zero_out{g}") for g in range(NG)], sem("part_zero")
        prep_step, hot_ready, hot_used = sem("prep_step"), sem("hot_ready"), sem("hot_used")
        deg_ready, pre_done = sem("deg_ready"), sem("pre_done")
        key_ready, keyt_done, keyt_ready = sem("key_ready"), sem("keyt_done"), sem("keyt_ready")
        key_out, key_in, act_rank, ranked_ready = sem("key_out"), sem("key_in"), sem("act_rank"), sem("ranked_ready")
        ranked_out, ranked_in, runs_in = sem("ranked_out"), sem("ranked_in"), sem("runs_in")
        gmax_ready, gmax_done, pads_out, pair_ready = sem("gmax_ready"), sem("gmax_done"), sem("pads_out"), sem("pair_ready")
        neg_ready, xrank_in = sem("neg_ready"), sem("xrank_in")
        XT0 = 12

        def one_hots(dve, steps, which, base):
            end = end_i[:, which, :]
            steps(nc.vector.tensor_scalar(half_i[:, :], end, 7, None, ALU.arith_shift_right))
            steps.settle()
            steps(nc.vector.tensor_copy(hi_b[:, :], half_i[:, :]))
            steps.settle()
            steps(nc.vector.tensor_scalar(half_i[:, :], end, P - 1, None, ALU.bitwise_and))
            steps.settle()
            steps(nc.vector.tensor_copy(lo_b[:, :], half_i[:, :]))
            steps(nc.vector.tensor_tensor(onehot_hi[:, :, :], hi_b[:, :, None].to_broadcast([P, EC, NT]),
                                          iota_hi[:, None, :].to_broadcast([P, EC, NT]), ALU.is_equal))
            steps.settle()
            for c in range(NCH):
                if base + c >= 2:
                    dve.wait_ge(hot_used, base + c - 1)
                at = slice(c * CH, (c + 1) * CH)
                nc.vector.tensor_tensor(onehot_lo[:, (base + c) % 2, :, :], lo_b[:, None, at].to_broadcast([P, P, CH]),
                                        iota_lo[:, :, :], ALU.is_equal).then_inc(hot_ready, 1)

        def count_ends(pe, hist, base):
            for c in range(NCH):
                pe.wait_ge(hot_ready, base + c + 1)
                for e in range(CH):
                    at = c * CH + e
                    last = nc.tensor.matmul(hist, onehot_lo[:, (base + c) % 2, :, e], onehot_hi[:, at, :],
                                            start=at == 0, stop=at == EC - 1)
                last.then_inc(hot_used, 1)

        rows = dense[0:NP * NP, :].rearrange("(t p s) two -> t p (s two)", t=2 * NT, p=P)
        ZG = 2 * GT
        ZERO_A, ZERO_B = 8, 20

        with nc.Block() as block:
            @block.sync
            def _(sp):
                sp.dma_start(end_i[:, 0, :], dst).then_inc(ends_in, 16)
                sp.dma_start(end_i[:, 1, :], src).then_inc(w_read, 16)
                sp.dma_start(w_in[:, :], w).then_inc(w_read, 16)
                sp.wait_ge(zero_set, 2)
                sp.dma_start(p2_dram[NP:NP + 1, :], lowrow[:, :]).then_inc(pads_out, 16)
                sp.wait_ge(pair_ready, 2)
                sp.dma_start(edges.rearrange("(p c) two -> p (c two)", p=P),
                             pairs[:, :, :].rearrange("p c two -> p (c two)")).then_inc(edges_out, 16)
                sp.dma_start(dense[NP * NP:, :].rearrange("(p c) two -> p (c two)", p=P),
                             zeros[:, 0:2 * SLOTS]).then_inc(pads_out, 16)
                for t in range(ZERO_A):
                    sp.dma_start(rows[t], zeros[:, :]).then_inc(zero_out[t // ZG], 16)
                sp.wait_ge(keyt_ready, 1)
                sp.dma_start(keys_dram.rearrange("o (t p) -> (o t) p", p=P), key_t[:, :]).then_inc(key_out, 16)
                sp.wait_ge(key_out, 16)
                sp.dma_start(key_row[:, :], keys_dram.to_broadcast([P, NP])).then_inc(key_in, 16)
                for t in range(ZERO_A, ZERO_B):
                    sp.dma_start(rows[t], zeros[:, :]).then_inc(zero_out[t // ZG], 16)
                sp.wait_ge(pads_out, 32)
                sp.wait_ge(edges_out, 16)
                for g in range(-(-ZERO_B // ZG)):
                    sp.wait_ge(zero_out[g], 16 * (min((g + 1) * ZG, ZERO_B) - g * ZG))
                    if (g + 1) * ZG <= ZERO_B:
                        sp.sem_inc(part_zero, 1)

            @block.gpsimd
            def _(pool):
                c = Steps(pool, const_step)
                c(nc.gpsimd.iota(iota_lo[:, :, :], [[1, P], [0, CH]], base=0, channel_multiplier=0,
                                 allow_small_or_imprecise_dtypes=True))
                c(nc.gpsimd.iota(iota_hi[:, :], [[1, NT]], base=0, channel_multiplier=0,
                                 allow_small_or_imprecise_dtypes=True))
                nc.gpsimd.memset(zeros[:, :], 0.0).then_inc(zero_set, 1)
                c(nc.gpsimd.memset(eps[:, :], EPS))
                nc.gpsimd.memset(lowrow[:, :], LOW).then_inc(zero_set, 1)
                c(nc.gpsimd.iota(node_id[:, :], [[P, NT]], base=0, channel_multiplier=1,
                                 allow_small_or_imprecise_dtypes=True))
                c(nc.gpsimd.memset(ones[:, :], 1.0))
                c(nc.gpsimd.memset(ident[:, :], 1.0))
                c.settle()
                c(nc.gpsimd.affine_select(out=before[:, :], in_=ones[:, :], compare_op=ALU.is_gt, fill=0.0,
                                          base=0, pattern=[[1, P]], channel_multiplier=-1))
                c(nc.gpsimd.affine_select(out=ident[:, :], in_=ident[:, :], compare_op=ALU.is_equal, fill=0.0,
                                          base=0, pattern=[[1, P]], channel_multiplier=-1))
                c(nc.gpsimd.iota(slot_k[:, :], [[1, K]], base=0, channel_multiplier=0,
                                 allow_small_or_imprecise_dtypes=True))
                c(nc.gpsimd.memset(stage[:, :, :, 2].bitcast(F32), 1.0))
                c(nc.gpsimd.iota(dummy_at[:, :, :], [[RND * P, GT], [0, K // RND], [P, RND]], base=DUMMY,
                                 channel_multiplier=1, allow_small_or_imprecise_dtypes=True))
                pool.wait_ge(w_read, 32)
                nc.gpsimd.tensor_copy(pairs[:, :, 0], end_i[:, 1, :]).then_inc(pair_ready, 1)
                nc.gpsimd.tensor_copy(pairs[:, :, 1].bitcast(F32), w_in[:, :]).then_inc(pair_ready, 1)
                in_turn = [t for both in zip(range(DT0), range(DT0, 2 * DT0)) for t in both if t < NT]
                for n, t in enumerate(in_turn):
                    pool.wait_ge(ranked_ready, n + 1)
                    scatter(ranked_dram, rank_i[:, t:t + 1], ranked[:, t, :]).then_inc(ranked_out, 16)
                pool.wait_ge(ranked_out, 16 * NT)
                pool.dma_start(node_of_rank[:, :, :], ranked_dram.rearrange("(t p) f -> p t f", p=P)).then_inc(ranked_in, 16)
                pool.wait_ge(ranked_in, 16)
                pool.wait_ge(edges_out, 16)
                for t in range(NT):
                    gather(tab_edge[:, t, :, :].rearrange("p k two -> p (k two)"), edges,
                           node_of_rank[:, t, 1:2]).then_inc(runs_in, 16)
                pool.wait_ge(gmax_ready, 2)
                nc.gpsimd.partition_all_reduce(gmax_all[:, :], gmax[:, :], P, bass.bass_isa.ReduceOp.max
                                               ).then_inc(gmax_done, 1)
                for t in range(XT0):
                    gather(big_a[:, t * D:(t + 1) * D], x, node_of_rank[:, t, 0:1]).then_inc(xrank_in, 16)

            @block.tensor
            def _(pe):
                hist, prefix, totals, keyt = banks[:, 0, 0:NT], banks[:, 1, 0:NT], banks[:, 2, 0:NT], banks[0:NT, 3, 0:P]
                count_ends(pe, hist, 0)
                pe.wait_ge(const_step, CONSTS)
                pe.wait_ge(deg_ready, 1)
                nc.tensor.matmul(prefix, before[:, :], deg[:, :], start=True, stop=True)
                nc.tensor.matmul(totals, ones[:, :], deg[:, :], start=True, stop=True).then_inc(pre_done, 1)
                pe.wait_ge(key_ready, 1)
                nc.tensor.transpose(keyt, key[:, :], ident[:, :]).then_inc(keyt_done, 1)

            @block.scalar
            def _(act):
                act.wait_ge(key_in, 16)
                act.wait_ge(neg_ready, 1)
                for t in range(DT0, NT):
                    nc.scalar.activation(junk[:, 1, :], key_row[:, :], ACT.Sign, bias=neg_key[:, t:t + 1],
                                         accum_out=rank[:, t:t + 1]).then_inc(act_rank, 1)
                    act.wait_ge(act_rank, t - DT0 + 1)

            @block.vector
            def _(dve):
                s = Steps(dve, prep_step)
                dve.wait_ge(ends_in, 16)
                dve.wait_ge(const_step, 2)
                one_hots(dve, s, 0, 0)
                dve.wait_ge(hot_used, NCH)
                nc.vector.tensor_copy(deg[:, :], banks[:, 0, 0:NT]).then_inc(deg_ready, 1)
                dve.wait_ge(deg_ready, 1)
                dve.wait_ge(const_step, CONSTS)
                s(nc.vector.tensor_scalar(key[:, :], deg[:, :], float(KEYCAP), float(KEY), ALU.min, ALU.mult))
                s.settle()
                nc.vector.tensor_tensor(key[:, :], key[:, :], node_id[:, :], ALU.add).then_inc(key_ready, 1)
                dve.wait_ge(key_ready, 1)
                nc.vector.tensor_scalar(neg_key[:, :], key[:, :], -1.0, -0.5, ALU.mult, ALU.add).then_inc(neg_ready, 1)
                dve.wait_ge(keyt_done, 1)
                nc.vector.tensor_copy(key_t[:, :], banks[0:NT, 3, 0:P]).then_inc(keyt_ready, 1)
                dve.wait_ge(pre_done, 1)
                s(nc.vector.tensor_copy(total[:, :], banks[:, 2, 0:NT]))
                s.settle()
                dve.wait_ge(zero_set, 1)
                s(nc.vector.tensor_tensor_scan(running[:, :], total[:, :], zeros[:, 0:NT], 0.0, ALU.add, ALU.add))
                s.settle()
                s(nc.vector.tensor_tensor(running[:, :], running[:, :], total[:, :], ALU.subtract))
                s.settle()
                s(nc.vector.tensor_tensor(first[:, :], running[:, :], banks[:, 1, 0:NT], ALU.add))
                s.settle()
                s(nc.vector.tensor_copy(ranked[:, :, 0], node_id[:, :]))
                s(nc.vector.tensor_copy(ranked[:, :, 1], first[:, :]))
                s(nc.vector.tensor_copy(ranked[:, :, 2], deg[:, :]))
                s(nc.vector.memset(ranked[:, :, 3], 0))
                dve.wait_ge(key_in, 16)
                for t in range(DT0):
                    s(nc.vector.tensor_scalar(junk[:, 0, :], key_row[:, :], key[:, t:t + 1], 0.0, ALU.is_gt, ALU.add,
                                              accum_out=rank[:, t:t + 1]))
                    s.settle()
                    nc.vector.tensor_copy(rank_i[:, t:t + 1], rank[:, t:t + 1]).then_inc(ranked_ready, 1)
                    if DT0 + t < NT:
                        dve.wait_ge(act_rank, t + 1)
                        nc.vector.tensor_scalar(rank_i[:, DT0 + t:DT0 + t + 1], rank[:, DT0 + t:DT0 + t + 1],
                                                float(NP), 0.5, ALU.add, ALU.mult).then_inc(ranked_ready, 1)
                dve.wait_ge(ranked_in, 16)
                s(nc.vector.tensor_copy(deg_rank[:, :], node_of_rank[:, :, 2]))
                s.settle()
                by_group = deg_rank[:, :].rearrange("p (g t) -> p g t", t=GT)
                nc.vector.tensor_reduce(gmax[:, 0:NG], by_group, AX.X, ALU.max).then_inc(gmax_ready, 1)
                nc.vector.tensor_reduce(gmax[:, NG:2 * NG], by_group[:, :, 1:GT], AX.X, ALU.max).then_inc(gmax_ready, 1)
                s(nc.vector.tensor_tensor(valid[:, :, :], slot_k[:, None, :].to_broadcast([P, NT, K]),
                                          deg_rank[:, :, None].to_broadcast([P, NT, K]), ALU.is_lt))
                for g in range(NG):
                    at = slice(g * GT, (g + 1) * GT)
                    s(nc.vector.tensor_scalar(row_base[:, at], node_id[:, at], float(g * (NP - 1) * GTP), None, ALU.add))
                dve.wait_ge(runs_in, 16 * NT)
                s.settle()
                s(nc.vector.tensor_copy(srcf[:, :, :], tab_edge[:, :, :, 0]))
                s.settle()
                s(nc.vector.tensor_scalar(work[:, :, :], srcf[:, :, :], float(-PAD), None, ALU.add))
                s.settle()
                s(nc.vector.tensor_tensor(work[:, :, :], work[:, :, :], valid[:, :, :], ALU.mult))
                s.settle()
                s(nc.vector.tensor_scalar(tab_edge[:, :, :, 0], work[:, :, :], float(PAD), None, ALU.add))
                s.settle()
                s(nc.vector.tensor_tensor(tab_edge[:, :, :, 1].bitcast(F32), tab_edge[:, :, :, 1].bitcast(F32),
                                          valid[:, :, :], ALU.mult))
                s(nc.vector.tensor_scalar(srcf[:, :, :], srcf[:, :, :], float(GTP), None, ALU.mult))
                s.settle()
                s(nc.vector.tensor_tensor(srcf[:, :, :], srcf[:, :, :], row_base[:, :, None].to_broadcast([P, NT, K]),
                                          ALU.add))
                s.settle()
                s(nc.vector.tensor_copy(tab_dense[:, :, :, 1], tab_edge[:, :, :, 1]))
                for g in range(NG):
                    at = slice(g * GT, (g + 1) * GT)
                    s(nc.vector.tensor_tensor(srcf[:, at, :], srcf[:, at, :], dummy_at[:, :, :], ALU.subtract))
                s.settle()
                s(nc.vector.tensor_tensor(srcf[:, :, :], srcf[:, :, :], valid[:, :, :], ALU.mult))
                s.settle()
                for g in range(NG):
                    at = slice(g * GT, (g + 1) * GT)
                    s(nc.vector.tensor_tensor(tab_dense[:, at, :, 0], srcf[:, at, :], dummy_at[:, :, :], ALU.add))
                dve.wait_ge(gmax_done, 1)
                s(nc.vector.tensor_copy(gmax_i[:, :], gmax_all[:, :]))
                s.settle()
                s(nc.vector.tensor_scalar(gmax_i[:, :], gmax_i[:, :], RND - 1, None, ALU.add))
                s.settle()
                s(nc.vector.tensor_scalar(gmax_i[:, :], gmax_i[:, :], 1, None, ALU.arith_shift_right))
                s.settle()
                s(nc.vector.tensor_scalar(iters[:, 0:NG], gmax_i[:, 0:NG], GT, None, ALU.max))
                s(nc.vector.tensor_scalar(iters[:, 2 * NG:3 * NG], gmax_i[:, NG:2 * NG], 1, None, ALU.max))
                s.settle()
                s(nc.vector.tensor_scalar(gmax_i[:, 0:NG], iters[:, 0:NG], HALF, None, ALU.is_le))
                s.settle()
                s(nc.vector.tensor_tensor(iters[:, NG:2 * NG], iters[:, 0:NG], gmax_i[:, 0:NG], ALU.mult))
        tmp.close()

        RELOAD_STEPS = {"pna": 16, "dense": 19}

        def reload_table(pool, table, kind, g, loads, reloaded, more_in):
            s = Steps(pool, reloaded, loads * RELOAD_STEPS[kind], (const_step, CONSTS))
            first, left, done = more_at[:, 0, :], more_at[:, 1, :], more_at[:, 2, :]
            tiles = ds(g * GT, GT)
            s(nc.gpsimd.tensor_copy(first, node_of_rank[:, tiles, 1]))
            s(nc.gpsimd.tensor_copy(left, node_of_rank[:, tiles, 2]))
            s.settle()
            s(nc.gpsimd.tensor_tensor(first, first, done, ALU.add))
            s(nc.gpsimd.tensor_tensor(left, left, done, ALU.subtract))
            s.settle()
            s(nc.gpsimd.tensor_scalar(first, first, float(EP - K), None, ALU.min))
            s(nc.gpsimd.tensor_scalar(done, done, float(K), None, ALU.add))
            s.settle()
            s(nc.gpsimd.tensor_copy(more_idx[:, :], first))
            s.settle()
            for i in range(GT):
                gather(more[:, i, :, :].rearrange("p k two -> p (k two)"), edges, more_idx[:, i:i + 1]).then_inc(more_in, 16)
            hold(pool, more_in, loads * (16 * GT) + 16 * GT)
            source, ok = more_f[:, 0, :, :], more_f[:, 1, :, :]
            s(nc.gpsimd.tensor_copy(source, more[:, :, :, 0]))
            s(nc.gpsimd.tensor_tensor(ok, left[:, :, None].to_broadcast([P, GT, K]),
                                      slot_k[:, None, :].to_broadcast([P, GT, K]), ALU.subtract))
            s.settle()
            s(nc.gpsimd.tensor_scalar(ok, ok, 0.0, 1.0, ALU.max, ALU.min))
            s.settle()
            if kind == "dense":
                s(nc.gpsimd.tensor_copy(more_f[:, 2, :, 0], row_base[:, tiles]))
                s(nc.gpsimd.tensor_scalar(source, source, float(GTP), None, ALU.mult))
                s.settle()
                s(nc.gpsimd.tensor_tensor(source, source, more_f[:, 2, :, 0:1].to_broadcast([P, GT, K]), ALU.add))
                s.settle()
                s(nc.gpsimd.tensor_tensor(source, source, dummy_at[:, :, :], ALU.subtract))
                s.settle()
                s(nc.gpsimd.tensor_tensor(source, source, ok, ALU.mult))
                s.settle()
                s(nc.gpsimd.tensor_tensor(source, source, dummy_at[:, :, :], ALU.add))
                s.settle()
            else:
                s(nc.gpsimd.tensor_scalar(source, source, float(-PAD), None, ALU.add))
                s.settle()
                s(nc.gpsimd.tensor_tensor(source, source, ok, ALU.mult))
                s.settle()
                s(nc.gpsimd.tensor_scalar(source, source, float(PAD), None, ALU.add))
                s.settle()
            s(nc.gpsimd.tensor_copy(more[:, :, :, 0], source))
            value = more[:, :, :, 1].bitcast(F32)
            if kind == "pna":
                s(nc.gpsimd.tensor_scalar(value, ok, 2 * LOW, -2 * LOW, ALU.mult, ALU.add))
            else:
                s(nc.gpsimd.tensor_tensor(value, value, ok, ALU.mult))
            s.settle()
            s(nc.gpsimd.tensor_copy(table[:, tiles, :, :], more[:, :, :, :]))
            s.settle()
            assert s.n == RELOAD_STEPS[kind], s.n

        def pool_rounds(pool, name, table, kind, before_round, issue, before_group=None, after_group=None,
                        leave_out=None):
            staged, reloaded = sem(f"{name}_staged"), sem(f"{name}_reloaded")
            phase_reset, more_in = sem(f"{name}_reset"), sem(f"{name}_more_in")
            it_reg, pos_reg, room_reg, load_reg, others_reg = (pool.alloc_register(f"{name}_{r}") for r in
                                                               ("it", "pos", "room", "loads", "others"))
            pool.reg_mov(it_reg, 0)
            pool.reg_mov(others_reg, 0)
            pool.reg_mov(load_reg, 0)
            with pool.Fori(0, NG) as g:
                if before_group is not None:
                    before_group(g)
                nc.gpsimd.memset(more_at[:, 2, :], 0.0).then_inc(phase_reset, 1)
                hold(pool, phase_reset, g + 1)
                count = pool.value_load(iters[0:1, ds(g, 1)], min_val=1, max_val=E)
                pool.reg_load(room_reg, iters[0:1, ds(g + NG, 1)])
                pool.reg_mov(pos_reg, 0)

                def iteration(tiles):
                    room = pool.snap(room_reg, min_val=0, max_val=E)
                    with pool.If(room == 0):
                        loads = pool.snap(load_reg, min_val=0, max_val=E)
                        reload_table(pool, table, kind, g, loads, reloaded, more_in)
                        pool.reg_add(load_reg, load_reg, 1)
                        pool.reg_mov(room_reg, HALF)
                        pool.reg_mov(pos_reg, 0)
                    pool.reg_sub(room_reg, room_reg, 1)
                    pos = pool.snap(pos_reg, min_val=0, max_val=HALF - 1)
                    it = pool.snap(it_reg, min_val=0, max_val=NG * E)
                    others_it = it if leave_out is None else pool.snap(others_reg, min_val=0, max_val=NG * E)
                    for r in range(RND):
                        before_round(it, r)
                        nc.gpsimd.tensor_copy(stage[:, r, :, 0:2],
                                              table[:, ds(g * GT, GT), ds(pos * RND + r, 1), :]
                                              .rearrange("p t o two -> p (t o) two")).then_inc(staged, 1)
                        hold(pool, staged, it * RND + r + 1)
                        for i in range(GT):
                            if i in tiles:
                                issue(others_it if i > 0 else it, r, i)
                            else:
                                leave_out(others_it, r, i)
                    pool.reg_add(it_reg, it_reg, 1)
                    if len(tiles) > 1:
                        pool.reg_add(others_reg, others_reg, 1)
                    pool.reg_add(pos_reg, pos_reg, 1)

                if leave_out is None:
                    with pool.Fori(0, count):
                        iteration(range(GT))
                else:
                    others = pool.value_load(iters[0:1, ds(g + 2 * NG, 1)], min_val=1, max_val=E)
                    with pool.Fori(0, others):
                        iteration(range(GT))
                    with pool.If(count > others):
                        with pool.Fori(0, bounded(pool, count - others, 1, E)):
                            iteration(range(1))
                        pool.reg_mov(pos_reg, 0)
                if after_group is not None:
                    after_group(pool.snap(it_reg, min_val=1, max_val=NG * E),
                                pool.snap(others_reg, min_val=1, max_val=NG * E))

        def rounds(engine, name, body, before_group=None, after_group=None):
            it_reg = engine.alloc_register(f"{name}_it")
            engine.reg_mov(it_reg, 0)
            with engine.Fori(0, NG) as g:
                count = engine.value_load(iters[0:1, ds(g, 1)], min_val=1, max_val=E)
                if before_group is not None:
                    before_group(g, engine.snap(it_reg, min_val=0, max_val=NG * E))
                with engine.Fori(0, count):
                    body(g, engine.snap(it_reg, min_val=0, max_val=NG * E))
                    engine.reg_add(it_reg, it_reg, 1)
                if after_group is not None:
                    after_group(g, engine.snap(it_reg, min_val=1, max_val=NG * E))

        ph = ExitStack()
        psb1 = maker(ph)
        wt = psb1("wt", [P, WR, GTP, 2])
        turned_w = psb1("turned_w", [P, GT, GTP])
        xg = psb1("xg", [P, GW])
        group_built = sem("group_built")
        slot_done = [[sem(f"slot_done{r}{i}") for i in range(GT)] for r in range(RND)]
        block_in = [sem(f"block_in{i}") for i in range(WR)]
        xg_ready, turned, turned_read, part_done, agg_done = (sem(n) for n in (
            "xg_ready", "turned", "turned_read", "part_done", "agg_done"))
        zero_rest = sem("zero_rest")
        xt_in, out_deg_ready, out_dev_ready, step1 = (sem(n) for n in ("xt_in", "out_deg_ready", "out_dev_ready", "step1"))
        blocks = dense[0:NP * NP, :].rearrange("(g s p n) two -> (g s) p (n two)", g=NG, s=NT, p=P)

        with nc.Block() as block:
            @block.gpsimd
            def _(pool):
                for t in range(XT0, NT):
                    gather(big_a[:, t * D:(t + 1) * D], x, node_of_rank[:, t, 0:1]).then_inc(xrank_in, 16)
                for i in range(GT):
                    pool.dma_start(dense[DUMMY + i * P:DUMMY + (i + 1) * P, :], zeros[:, 0:2]
                                   ).then_inc(slot_done[RND - 1][i], 16)

                def before_group(g):
                    hold(pool, part_zero, g + 1)

                def issue(it, r, i):
                    hold(pool, slot_done[1 - r][i], (it + 1) * 16)
                    scatter(dense, stage[:, r, i, 0:1], stage[:, r, i, 1:3].bitcast(F32),
                            compute_op=ALU.add).then_inc(slot_done[r][i], 16)

                def leave_out(it, r, i):
                    if r == 0:
                        hold(pool, slot_done[1][i], (it + 1) * 16)

                def built(it, others_it):
                    for i in range(GT):
                        hold(pool, slot_done[1][i], ((others_it if i > 0 else it) + 1) * 16)
                    pool.sem_inc(group_built, 1)

                pool_rounds(pool, "dense", tab_dense, "dense", lambda it, r: None, issue, before_group, built, leave_out)

            @block.sync
            def _(sp):
                sp.dma_start(big_b[:, :].rearrange("p (h n) -> p h n", h=2), xT.rearrange("(h p) n -> p h n", p=P)
                             ).then_inc(xt_in, 16)
                for j in (WR - 2, WR - 1):
                    sp.sem_inc(block_in[j], 16)
                for t in range(ZERO_B, 2 * NT):
                    for half in range(2):
                        at = slice(half * NP // 2, (half + 1) * NP // 2)
                        sp.dma_start(rows[t][:, at], zeros[:, at]).then_inc(zero_rest, 16)
                        sp.wait_ge(zero_rest, 16 * (2 * (t - ZERO_B) + half + 1))
                    if t % ZG == ZG - 1:
                        sp.sem_inc(part_zero, 1)
                with sp.Fori(0, NG) as g:
                    hold(sp, group_built, g + 1)
                    with sp.Fori(0, NT // GT) as q:
                        for j in range(GT):
                            hold(sp, turned, g * NT + q * GT + (j + 1))
                            hold(sp, block_in[(j - 2) % WR], g * (16 * NT // GT) + q * 16 + 16)
                            sp.dma_start(wt[:, j, :, :].rearrange("p n two -> p (n two)"),
                                         blocks[ds(g * NT + q * GT + j, 1), :, :].rearrange("o p n -> (o p) n")
                                         ).then_inc(block_in[j], 16)
                sp.wait_ge(xt_in, 16)
                for j in range(WR):
                    sp.wait_ge(block_in[j], 16 * NG * (NT // GT) + (16 if j >= WR - 2 else 0))

            @block.tensor
            def _(pe):
                count_ends(pe, banks[:, 0, 0:NT], NCH)
                pe.wait_ge(out_deg_ready, 1)
                pe.sem_inc(turned, WR)
                with pe.Fori(0, NG) as g:
                    hold(pe, xg_ready, g + 1)
                    with pe.Fori(0, NT // GT) as q:
                        for j in range(GT):
                            hold(pe, block_in[j], g * (16 * NT // GT) + q * 16 + (32 if j >= WR - 2 else 16))
                            hold(pe, turned_read, g * NT + q * GT + (j + (2 if j == 0 else 1)))
                            for i in range(GT):
                                last = nc.tensor.transpose(flat[:, (j % 2) * 1024 + i * P:(j % 2) * 1024 + (i + 1) * P],
                                                           wt[:, j, i * P:(i + 1) * P, 0], ident[:, :])
                            last.then_inc(turned, 1)
                        for half in range(2):
                            hold(pe, turned_read, g * NT + q * GT + (2 + (3, 5)[half]))
                            for h in range(2):
                                part = half * 2 + h
                                hold(pe, agg_done, g * 20 + q * 4 + (part + 1))
                                for i in range(GT):
                                    last = nc.tensor.matmul(banks[:, 4 + part, 0:HGT],
                                                            xg[:, i * D + h * P:i * D + (h + 1) * P],
                                                            turned_w[:, i, half * HGT:(half + 1) * HGT],
                                                            start=i == 0, stop=i == GT - 1)
                                last.then_inc(part_done, 1)

            @block.scalar
            def _(act):
                act.wait_ge(out_deg_ready, 1)
                nc.scalar.activation(out_scale[:, :], out_scale[:, :], ACT.Sqrt).then_inc(out_dev_ready, 1)
                act.sem_inc(turned_read, 2)
                with act.Fori(0, NG) as g:
                    with act.Fori(0, NT // GT) as q:
                        for j in range(GT):
                            hold(act, turned, g * NT + q * GT + (WR + j + 1))
                            nc.scalar.activation(turned_w[:, :, j * P:(j + 1) * P],
                                                 flat[:, (j % 2) * 1024:(j % 2) * 1024 + GTP].rearrange(
                                                     "p (i n) -> p i n", i=GT), ACT.Copy).then_inc(turned_read, 1)

            @block.vector
            def _(dve):
                s = Steps(dve, step1)
                one_hots(dve, s, 1, NCH)
                dve.wait_ge(hot_used, 2 * NCH)
                nc.vector.tensor_scalar(out_scale[:, :], banks[:, 0, 0:NT], 1.0, None, ALU.max).then_inc(out_deg_ready, 1)
                dve.wait_ge(out_dev_ready, 1)
                s(nc.vector.reciprocal(out_scale[:, :], out_scale[:, :]))
                dve.sem_inc(agg_done, 4)
                dve.sem_inc(part_done, 1)
                dve.wait_ge(xt_in, 16)
                dve.wait_ge(xrank_in, 16 * NT)
                with dve.Fori(0, NG) as g:
                    hold(dve, part_done, g * 20 + 1)
                    nc.vector.tensor_copy(xg[:, :], big_a[:, ds(g * GW, GW)]).then_inc(xg_ready, 1)
                    with dve.Fori(0, NT // GT) as q:
                        for half in range(2):
                            for h in range(2):
                                part = half * 2 + h
                                hold(dve, part_done, g * 20 + q * 4 + (part + 2))
                                hold(dve, agg_done, g * 20 + q * 4 + (part + 1))
                                at = big_b[:, ds(q * GTP + (h * NP + half * HGT), HGT)]
                                nc.vector.tensor_tensor(at, at, banks[:, 4 + part, 0:HGT], ALU.add).then_inc(agg_done, 1)
        ph.close()
        prep.close()

        big_d = sb("big_d", [P, NT * D])
        in_scale = sb("in_scale", [P, NT])
        deg_inv = sb("deg_inv", [P, NT])
        has = sb("has", [P, NT])
        amp = sb("amp", [P, NT])
        att = sb("att", [P, NT])
        late = ExitStack()
        h1 = maker(late)("h1", [P, NT * HID1])
        ph = ExitStack()
        psb2 = maker(ph)
        w1 = psb2("w1", [P, 2, HID0])
        w2 = psb2("w2", [P, HID0 // P, D])
        wc = psb2("wc", [P, 2, HID1])
        b1 = psb2("b1", [P, HID0 // P])
        b2 = psb2("b2", [P, D])
        hid = psb2("hid", [P, HID0 // P, GT * P])
        yg = psb2("yg", [P, GT, D])
        x1g = psb2("x1g", [P, GT, D])
        x1t = psb2("x1t", [P, 2, GT * P])
        w_in2, x_in2, hid_psum, hid_ready, out_psum, y_ready, step2, stored = (sem(n) for n in (
            "w_in2", "x_in2", "hid_psum", "hid_ready", "out_psum", "y_ready", "step2", "stored"))
        x1_ready, x1_out, t_psum, t_ready, h_psum, h1_ready, pna_step = (sem(n) for n in (
            "x1_ready", "x1_out", "t_psum", "t_ready", "h_psum", "h1_ready", "pna_step"))
        var2, dev2 = sem("var2"), sem("dev2")
        five = flat[:, 6 * 512:6 * 512 + GTP]
        STEP2 = 7

        with nc.Block() as block:
            @block.sync
            def _(sp):
                sp.dma_start(w1[:, :, :], L0_W1.rearrange("(k p) m -> p k m", p=P)).then_inc(w_in2, 16)
                sp.dma_start(w2[:, :, :], L0_W2.rearrange("(k p) m -> p k m", p=P)).then_inc(w_in2, 16)
                sp.dma_start(wc[:, :, :], L1_Wc.rearrange("(k p) m -> p k m", p=P)).then_inc(w_in2, 16)
                sp.dma_start(b1[:, :], L0_b1).then_inc(w_in2, 16)
                sp.dma_start(b2[:, :], L0_b2.to_broadcast([P, D])).then_inc(w_in2, 16)
                sp.dma_start(big_c[:, :].rearrange("p (t d) -> p t d", t=NT), x.rearrange("(t p) d -> p t d", p=P)
                             ).then_inc(x_in2, 16)
                x1_rows = x1_dram.rearrange("(g t p) d -> g p t d", t=GT, p=P)
                sp.sem_inc(stored, 1)
                with sp.Fori(0, NG) as g:
                    hold(sp, x1_ready, g * GT + GT)
                    sp.dma_start(x1_rows[ds(g, 1), :, :, :].rearrange("o p t d -> p (o t) d"), x1g[:, :, :]
                                 ).then_inc(x1_out, 16)
                    hold(sp, x1_out, g * 16 + 16)
                    sp.sem_inc(stored, 1)
                sp.wait_ge(x_in2, 16)
                sp.wait_ge(x1_out, 16 * NG)

            @block.gpsimd
            def _(pool):
                s = Steps(pool, pna_step)
                s(nc.gpsimd.tensor_tensor(tab_pna[:, :, :, 1].bitcast(F32),
                                          deg_rank[:, :, None].to_broadcast([P, NT, K]),
                                          slot_k[:, None, :].to_broadcast([P, NT, K]), ALU.subtract))
                s.settle()
                s(nc.gpsimd.tensor_scalar(tab_pna[:, :, :, 1].bitcast(F32), tab_pna[:, :, :, 1].bitcast(F32),
                                          0.0, 1.0, ALU.max, ALU.min))
                s.settle()
                s(nc.gpsimd.tensor_scalar(tab_pna[:, :, :, 1].bitcast(F32), tab_pna[:, :, :, 1].bitcast(F32),
                                          2 * LOW, -2 * LOW, ALU.mult, ALU.add))

            @block.tensor
            def _(pe):
                pe.wait_ge(w_in2, 16 * 5)
                pe.sem_inc(out_psum, 1)

                def hidden(g):
                    for c in range(HID0 // P):
                        pair = 2 * (c % 2)
                        hold(pe, hid_ready, g * 4 + (c + 1))
                        for h in range(2):
                            for k in range(2):
                                last = nc.tensor.matmul(banks[:, pair + h, 0:HGT], w1[:, k, c * P:(c + 1) * P],
                                                        big_b[:, ds(g * GTP + (k * NP + h * HGT), HGT)],
                                                        start=k == 0, stop=k == 1)
                        last.then_inc(hid_psum, 1)

                def out(g):
                    hold(pe, hid_ready, g * 4 + 6)
                    for i in range(GT):
                        hold(pe, y_ready, g * GT + (i + (2 if i == 0 else 1)))
                        for c in range(4):
                            last = nc.tensor.matmul(banks[:, 4 + i % 2, 0:D], hid[:, c, i * P:(i + 1) * P], w2[:, c, :],
                                                    start=c == 0, stop=c == 3)
                        last.then_inc(out_psum, 1)

                def gcn_input(g):
                    hold(pe, x1_ready, g * GT + GT)
                    hold(pe, h1_ready, g * GT + 1)
                    for k in range(2):
                        hold(pe, t_ready, g * 2 + (1 + k))
                        for i in range(GT):
                            last = nc.tensor.transpose(five[:, i * P:(i + 1) * P], x1g[:, i, k * P:(k + 1) * P], ident[:, :])
                        last.then_inc(t_psum, 1)
                    hold(pe, t_ready, g * 2 + 3)
                    for i in range(GT):
                        for k in range(2):
                            last = nc.tensor.matmul(five[:, i * P:(i + 1) * P], x1t[:, k, i * P:(i + 1) * P], wc[:, k, :],
                                                    start=k == 0, stop=k == 1)
                    last.then_inc(h_psum, 1)

                hidden(0)
                out(0)
                with pe.Fori(0, NG - 1) as g:
                    hidden(g + 1)
                    gcn_input(g)
                    out(g + 1)
                gcn_input(NG - 1)

            @block.scalar
            def _(act):
                act.wait_ge(w_in2, 16 * 5)
                act.sem_inc(hid_ready, 2)
                act.sem_inc(t_ready, 1)
                act.sem_inc(h1_ready, 1)

                def hidden(g, blocks_c):
                    hold(act, out_psum, g * GT + 1)
                    for c in blocks_c:
                        pair = 2 * (c % 2)
                        hold(act, hid_psum, g * 4 + (c + 1))
                        nc.scalar.activation(hid[:, c, :].rearrange("p (h n) -> p h n", h=2), banks[:, pair:pair + 2, 0:HGT],
                                             ACT.Relu, bias=b1[:, c:c + 1]).then_inc(hid_ready, 1)

                def gcn_input(g):
                    for k in range(2):
                        hold(act, t_psum, g * 2 + (k + 1))
                        nc.scalar.activation(x1t[:, k, :], five, ACT.Copy).then_inc(t_ready, 1)
                    hold(act, h_psum, g + 1)
                    for i in range(GT):
                        nc.scalar.activation(h1[:, ds(g * (GT * HID1) + i * HID1, HID1)], five[:, i * P:(i + 1) * P], ACT.Copy,
                                             scale=out_scale[:, ds(g * GT + i, 1)]).then_inc(h1_ready, 1)

                hidden(0, range(4))
                with act.Fori(0, NG - 1) as g:
                    hidden(g + 1, range(3))
                    deviation(act, g, var2, dev2)
                    hidden(g + 1, range(3, 4))
                    gcn_input(g)
                deviation(act, NG - 1, var2, dev2)
                gcn_input(NG - 1)

            @block.vector
            def _(dve):
                dve.wait_ge(w_in2, 16 * 5)
                dve.wait_ge(x_in2, 16)
                dve.sem_inc(y_ready, 2)
                with dve.Fori(0, NG) as g:
                    s = Steps(dve, step2, g * STEP2, (const_step, CONSTS))
                    for i in range(GT):
                        hold(dve, out_psum, g * GT + (i + 2))
                        nc.vector.tensor_tensor(yg[:, i, :], banks[:, 4 + i % 2, 0:D],
                                                big_c[:, ds(g * GW + i * D, D)], ALU.add).then_inc(y_ready, 1)
                    hold(dve, y_ready, g * GT + (GT + 2))
                    s(nc.vector.tensor_tensor(yg[:, :, :], yg[:, :, :], b2[:, None, :].to_broadcast([P, GT, D]), ALU.add))
                    hold(dve, stored, g + 1)
                    hold(dve, h1_ready, g * GT + 1)
                    layer_norm(dve, s, lambda i: yg[:, i, :], lambda i: x1g[:, i, :],
                               lambda i, ins: ins.then_inc(x1_ready, 1), g, var2, dev2)
                    assert s.n == STEP2, s.n
        ph.close()

        recycle_sems()

        ph = ExitStack()
        psb3 = maker(ph)
        wt3 = psb3("wt3", [P, WR, GTP, 2])
        w1t = psb3("w1t", [P, HID1])
        w2t = psb3("w2t", [P, D])
        wp = psb3("wp", [P, 2, D])
        whq = psb3("whq", [P, 2, 2 * D])
        bc, b1c, b2c, bq, bp = (psb3(n, [P, m]) for n, m in (("bc", 1), ("b1c", 1), ("b2c", D), ("bq", D), ("bp", D)))
        ones3 = psb3("ones3", [P, P])
        diag = psb3("diag", [P, GTP])
        scale_row = psb3("scale_row", [P, GTP])
        hmt = psb3("hmt", [P, GTP])
        h2t = psb3("h2t", [P, GTP])
        y4 = psb3("y4", [P, GT, D])
        x2t = psb3("x2t", [P, 2, GTP])
        block3_in = [sem(f"block3_in{i}") for i in range(WR)]
        x1rank_in, step3, log_done, in_deg_ready, ones_set, diag_ready, scale_psum, scale_ready = (sem(n) for n in (
            "x1rank_in", "step3", "log_done", "in_deg_ready", "ones_set", "diag_ready", "scale_psum", "scale_ready"))
        block_used, sum_read, w_in4, hmt_ready, h2_psum, h2_ready, out4_psum, y4_ready = (sem(n) for n in (
            "block_used", "sum_read", "w_in4", "hmt_ready", "h2_psum", "h2_ready", "out4_psum", "y4_ready"))
        x2_ready, x2t_psum, x2t_ready, pq_psum, p_ready, q_ready, step4, p_out = (sem(n) for n in (
            "x2_ready", "x2t_psum", "x2t_ready", "pq_psum", "p_ready", "q_ready", "step4", "p_out"))
        var4, dev4 = sem("var4"), sem("dev4")
        STEP4 = 7
        halves = banks[:, 0:2, 0:HGT]

        def load_blocks(sp, ring, landed, used_sem):
            with sp.Fori(0, NT) as q:
                for j in range(WR):
                    hold(sp, used_sem, q * WR + (j + 1))
                    sp.dma_start(ring[:, j, :, :].rearrange("p n two -> p (n two)"),
                                 blocks[ds(q * WR + j, 1), :, :].rearrange("o p n -> (o p) n")).then_inc(landed[j], 16)
            for j in range(WR):
                sp.wait_ge(landed[j], 16 * NT)

        with nc.Block() as block:
            @block.sync
            def _(sp):
                sp.sem_inc(block_used, WR)
                load_blocks(sp, wt3, block3_in, block_used)

            @block.gpsimd
            def _(pool):
                nc.gpsimd.memset(ones3[:, :], 1.0).then_inc(ones_set, 1)
                pool.dma_start(w1t[:, :], L1_W1T).then_inc(w_in4, 16)
                pool.dma_start(w2t[:, :], L1_W2T).then_inc(w_in4, 16)
                pre = L2_preW.rearrange("(h k p) m -> h p k m", h=2, p=P)
                pool.dma_start(wp[:, :, :], pre[0]).then_inc(w_in4, 16)
                pool.dma_start(whq[:, :, D:2 * D], pre[1]).then_inc(w_in4, 16)
                pool.dma_start(whq[:, :, 0:D], L2_postW[0:D, :].rearrange("(k p) m -> p k m", p=P)).then_inc(w_in4, 16)
                pool.dma_start(bc[:, :], L1_bc).then_inc(w_in4, 16)
                pool.dma_start(b1c[:, :], L1_b1).then_inc(w_in4, 16)
                for a, b in ((b2c, L1_b2), (bq, L2_preb), (bp, L2_postb)):
                    pool.dma_start(a[:, :], b.to_broadcast([P, D])).then_inc(w_in4, 16)
                for t in range(NT):
                    gather(big_a[:, t * D:(t + 1) * D], x1_dram, node_of_rank[:, t, 0:1]).then_inc(x1rank_in, 16)
                pool.wait_ge(x1rank_in, 16 * NT)
                for t in range(NT):
                    pool.wait_ge(p_ready, t + 2)
                    scatter(p2_dram, node_of_rank[:, t, 0:1], big_a[:, t * D:(t + 1) * D]).then_inc(p_out, 16)
                pool.wait_ge(p_out, 16 * NT)

            @block.tensor
            def _(pe):
                def scales(g):
                    pe.wait_ge(x2t_ready, g * 2 + 1)
                    pe.wait_ge(diag_ready, g + 1)
                    for i in range(GT):
                        last = nc.tensor.matmul(five[:, i * P:(i + 1) * P], ones3[:, :], diag[:, i * P:(i + 1) * P],
                                                start=True, stop=True)
                    last.then_inc(scale_psum, 1)

                def first_product(g):
                    pe.wait_ge(hmt_ready, g + 1)
                    pe.wait_ge(q_ready, g * GT + 2)
                    for h in range(2):
                        last = nc.tensor.matmul(banks[:, 2 + h, 0:HGT], w1t[:, :], hmt[:, h * HGT:(h + 1) * HGT],
                                                start=True, stop=True)
                    last.then_inc(h2_psum, 1)

                def second_product(g):
                    pe.wait_ge(h2_ready, g + 1)
                    pe.wait_ge(p_ready, g * GT + 1)
                    for i in range(GT):
                        pe.wait_ge(y4_ready, g * GT + i + (2 if i == 0 else 1))
                        nc.tensor.matmul(banks[:, 4 + i % 2, 0:D], h2t[:, i * P:(i + 1) * P], w2t[:, :],
                                         start=True, stop=True).then_inc(out4_psum, 1)

                def turn_x2(g, k):
                    pe.wait_ge(x2_ready, g * GT + GT)
                    pe.wait_ge(scale_ready, g + 1)
                    pe.wait_ge(x2t_ready, g * 2 + 1 + k)
                    for i in range(GT):
                        last = nc.tensor.transpose(five[:, i * P:(i + 1) * P],
                                                   big_c[:, g * GW + i * D + k * P:g * GW + i * D + (k + 1) * P], ident[:, :])
                    last.then_inc(x2t_psum, 1)

                def pna_products(g, i):
                    pe.wait_ge(x2t_ready, g * 2 + 3)
                    pe.wait_ge(y4_ready, g * GT + GT + 2)
                    if i > 0:
                        pe.wait_ge(p_ready, g * GT + i)
                        pe.wait_ge(q_ready, g * GT + (i + 1))
                    for k in range(2):
                        nc.tensor.matmul(banks[:, 4 + i % 2, 0:D], x2t[:, k, i * P:(i + 1) * P], wp[:, k, :],
                                         start=k == 0, stop=k == 1)
                    for k in range(2):
                        last = nc.tensor.matmul(banks[:, 2 + i % 2, :], x2t[:, k, i * P:(i + 1) * P], whq[:, k, :],
                                                start=k == 0, stop=k == 1)
                    last.then_inc(pq_psum, 1)

                between = {1: lambda g: first_product(g), 3: lambda g: second_product(g),
                           11: lambda g: turn_x2(g, 0), 12: lambda g: turn_x2(g, 1)}
                for i in range(GT):
                    between[13 + 2 * i] = lambda g, i=i: pna_products(g, i)
                pe.wait_ge(ones_set, 1)
                for g in range(NG):
                    pe.wait_ge(sum_read, g + 1)
                    for b in range(NT):
                        if g > 0 and b in between:
                            between[b](g - 1)
                        pe.wait_ge(block3_in[b % WR], g * (16 * NT // WR) + 16 * (b // WR + 1))
                        for h in range(2):
                            last = nc.tensor.matmul(banks[:, h, 0:HGT], h1[:, b * HID1:(b + 1) * HID1],
                                                    wt3[:, b % WR, h * HGT:(h + 1) * HGT, 1],
                                                    start=b == 0, stop=b == NT - 1)
                        last.then_inc(block_used, 1)
                    scales(g)
                    pe.wait_ge(w_in4, 160)
                for b in sorted(between):
                    between[b](NG - 1)

            @block.scalar
            def _(act):
                nc.scalar.activation(amp[:, :], deg_rank[:, :], ACT.Ln, bias=1.0).then_inc(log_done, 1)
                act.wait_ge(in_deg_ready, 1)
                nc.scalar.activation(in_scale[:, :], in_scale[:, :], ACT.Sqrt).then_inc(log_done, 1)
                act.wait_ge(w_in4, 160)
                act.wait_ge(x1rank_in, 16 * NT)
                act.sem_inc(p_ready, 1)
                act.sem_inc(x2t_ready, 1)

                with act.Fori(0, NG) as g:
                    hold(act, scale_psum, g + 1)
                    hold(act, sum_read, g + 1)
                    nc.scalar.activation(scale_row[:, :], five, ACT.Copy).then_inc(scale_ready, 1)
                    hold(act, sum_read, g + 2)
                    nc.scalar.activation(hmt[:, :], hmt[:, :], ACT.Relu, bias=bc[:, :]).then_inc(hmt_ready, 1)
                    hold(act, h2_psum, g + 1)
                    nc.scalar.activation(h2t[:, :].rearrange("p (h n) -> p h n", h=2), banks[:, 2:4, 0:HGT],
                                         ACT.Relu, bias=b1c[:, :]).then_inc(h2_ready, 1)
                    deviation(act, g, var4, dev4)
                    for k in range(2):
                        hold(act, x2t_psum, g * 2 + (k + 1))
                        nc.scalar.activation(x2t[:, k, :], five, ACT.Copy).then_inc(x2t_ready, 1)
                    for i in range(GT):
                        hold(act, pq_psum, g * GT + (i + 1))
                        nc.scalar.activation(big_a[:, ds(g * GW + i * D, D)], banks[:, 4 + i % 2, 0:D], ACT.Copy
                                             ).then_inc(p_ready, 1)

            @block.vector
            def _(dve):
                s = Steps(dve, step3)
                nc.vector.tensor_scalar(in_scale[:, :], deg_rank[:, :], 1.0, None, ALU.max).then_inc(in_deg_ready, 1)
                s(nc.vector.tensor_scalar(deg_inv[:, :], deg_rank[:, :], 1.0, None, ALU.max))
                s(nc.vector.tensor_scalar(has[:, :], deg_rank[:, :], 1.0, None, ALU.min))
                dve.wait_ge(log_done, 2)
                s(nc.vector.tensor_scalar(att[:, :], amp[:, :], EPS, None, ALU.max))
                s.settle()
                s(nc.vector.reciprocal(att[:, :], att[:, :]))
                s(nc.vector.reciprocal(in_scale[:, :], in_scale[:, :]))
                s(nc.vector.reciprocal(deg_inv[:, :], deg_inv[:, :]))
                s.settle()
                s(nc.vector.tensor_scalar(att[:, :], att[:, :], AVG_D, None, ALU.mult))
                s(nc.vector.tensor_scalar(amp[:, :], amp[:, :], 1.0 / AVG_D, None, ALU.mult))
                dve.sem_inc(sum_read, 1)
                dve.sem_inc(y4_ready, 2)
                dve.sem_inc(q_ready, 2)

                dve.wait_ge(w_in4, 160)
                dve.wait_ge(x1rank_in, 16 * NT)
                with dve.Fori(0, NG) as g:
                    s = Steps(dve, step4, g * STEP4, (const_step, CONSTS))
                    nc.vector.tensor_tensor(diag[:, :].rearrange("p (t n) -> p t n", t=GT),
                                            ident[:, None, :].to_broadcast([P, GT, P]),
                                            in_scale[:, ds(g * GT, GT), None].to_broadcast([P, GT, P]), ALU.mult
                                            ).then_inc(diag_ready, 1)
                    hold(dve, block_used, g * NT + (NT + WR))
                    hold(dve, scale_ready, g + 1)
                    nc.vector.tensor_tensor(hmt[:, :].rearrange("p (h n) -> p h n", h=2), halves,
                                            scale_row[:, :].rearrange("p (h n) -> p h n", h=2), ALU.mult
                                            ).then_inc(sum_read, 1)
                    for i in range(GT):
                        hold(dve, out4_psum, g * GT + (i + 1))
                        nc.vector.tensor_tensor(y4[:, i, :], banks[:, 4 + i % 2, 0:D],
                                                big_a[:, ds(g * GW + i * D, D)], ALU.add).then_inc(y4_ready, 1)
                    hold(dve, y4_ready, g * GT + (GT + 2))
                    s(nc.vector.tensor_tensor(y4[:, :, :], y4[:, :, :], b2c[:, None, :].to_broadcast([P, GT, D]), ALU.add))
                    layer_norm(dve, s, lambda i: y4[:, i, :], lambda i: big_c[:, ds(g * GW + i * D, D)],
                               lambda i, ins: ins.then_inc(x2_ready, 1), g, var4, dev4)
                    for i in range(GT):
                        hold(dve, pq_psum, g * GT + (i + 1))
                        at = ds(g * GW + i * D, D)
                        nc.vector.tensor_tensor(big_d[:, at], banks[:, 2 + i % 2, 0:D], bp[:, :], ALU.add)
                        nc.vector.tensor_tensor(big_b[:, at], banks[:, 2 + i % 2, D:2 * D], bq[:, :], ALU.add
                                                ).then_inc(q_ready, 1)
                    assert s.n == STEP4, s.n
        ph.close()
        late.close()

        recycle_sems()

        late = ExitStack()
        psb5 = maker(late)
        gath = psb5("gath", [P, RND, GT, D])
        z = psb5("z", [P, RND, GW])
        VT = 2
        MP = (GT - VT) * D
        summed = psb5("summed", [P, RND, MP + GW])
        run = psb5("run", [P, GW + VT * D])
        mx, part_sum = run[:, 0:GW], run[:, GW:]
        mn = psb5("mn", [P, GW])
        nothing = psb5("nothing", [1, 512], BF16)
        wpost = psb5("wpost", [P, 8, 3 * D])
        wmix = psb5("wmix", [P, 2, D])
        bmix = psb5("bmix", [P, D])
        quant = psb5("quant", [P, 4, D])
        aggt = psb5("aggt", [P, 8, P])
        ht = psb5("ht", [P, D])
        htt = psb5("htt", [P, D])
        y5 = psb5("y5", [P, D])
        saved = big_a[:, 0:4 * GW].rearrange("p (q n) -> p q n", q=4)
        mean, mx_all, mn_all, var_all, mean_sq = (big_a[:, n * GW:(n + 1) * GW] for n in range(5))
        land = [[sem(f"land_{r}{i}") for i in range(GT)] for r in range(RND)]
        w_in5, used, z_ready, m_ready, run_done, sq_ready, sums_done = (sem(n) for n in (
            "w_in5", "used", "z_ready", "m_ready", "run_done", "sq_ready", "sums_done"))
        sums_final, evac_done, x3_ready, nothing_set, step5, step_ht, step_y, step_fin, saved_ready = (sem(n) for n in (
            "sums_final", "evac_done", "x3_ready", "nothing_set", "step5", "step_ht", "step_y", "step_fin", "saved_ready"))
        quant_ready, t5_psum, t5_read, mix_read, abc_psum, ht_ready, htt_psum, htt_ready, mix_psum, x3_out = (sem(n) for n in (
            "quant_ready", "t5_psum", "t5_read", "mix_read", "abc_psum", "ht_ready", "htt_psum", "htt_ready", "mix_psum", "x3_out"))
        var5, dev5 = sem("var5"), sem("dev5")
        STEP5, STEP_HT, STEP_Y, STEP_FIN = 4, 2, 3, 2
        SB = (MP + GW) // 512
        mixed = banks[:, 5, 0:D]

        def pna_steps(engine, name, step):
            n_reg, *lag_regs = (engine.alloc_register(f"{name}_{r}") for r in ("n", "n1", "n2"))
            for reg in (n_reg, *lag_regs):
                engine.reg_mov(reg, 0)

            def between(g):
                n = engine.snap(n_reg, min_val=0, max_val=NT)
                with engine.If(n < g * GT):
                    def lagging(lag, part):
                        with engine.If(n > lag - 1):
                            part(engine.snap(lag_regs[lag - 1], min_val=0, max_val=NT - 1 - lag))

                    tile = bounded(engine, n - g * GT + GT, 0, GT - 1)
                    step(bounded(engine, n, 0, NT - GT - 1), lagging, bounded(engine, g - 1, 0, NG - 2), tile)
                    engine.reg_mov(lag_regs[1], lag_regs[0])
                    engine.reg_mov(lag_regs[0], n_reg)
                    engine.reg_add(n_reg, n_reg, 1)

            def last_group():
                with engine.Fori(0, GT) as k:
                    step(k + (NT - GT), lambda lag, part: part(k + (NT - GT - lag)), NG - 1, k)

            return between, last_group

        with nc.Block() as block:
            @block.sync
            def _(sp):
                post = L2_postW[D:, :].rearrange("(s c p) m -> s p c m", s=3, p=P)
                for n in range(3):
                    sp.dma_start(wpost[:, :, n * D:(n + 1) * D], post[n]).then_inc(w_in5, 16)
                sp.dma_start(wmix[:, :, :], L2_mixW.rearrange("(k p) m -> p k m", p=P)).then_inc(w_in5, 16)
                sp.dma_start(bmix[:, :], L2_mixb.to_broadcast([P, D])).then_inc(w_in5, 16)
                sp.wait_ge(w_in5, 80)

            @block.gpsimd
            def _(pool):
                nc.gpsimd.memset(nothing[:, :], 0.0).then_inc(nothing_set, 1)

                def before_round(it, r):
                    hold(pool, used, it * SLOTS + (r + 1) * GT)

                def issue(it, r, i):
                    gather(gath[:, r, i, :], p2_dram, stage[:, r, i, 0:1]).then_inc(land[r][i], 16)

                pool_rounds(pool, "pna", tab_pna, "pna", before_round, issue)
                for t in range(NT):
                    pool.wait_ge(x3_ready, t + 1)
                    scatter(x3_dram, node_of_rank[:, t, 0:1], big_c[:, t * D:(t + 1) * D]).then_inc(x3_out, 16)
                pool.wait_ge(x3_out, 16 * NT)

            @block.vector
            def _(dve):
                dve.sem_inc(used, SLOTS)
                dve.sem_inc(run_done, RND)
                dve.sem_inc(ht_ready, 1)
                dve.sem_inc(mix_read, 2)
                dve.sem_inc(step_fin, STEP_FIN)
                dve.wait_ge(w_in5, 80)

                def norm(n):
                    s = Steps(dve, step_y, n * STEP_Y, (const_step, CONSTS))
                    tile = big_c[:, ds(n * D, D)]
                    hold(dve, mix_psum, n + 1)
                    nc.vector.tensor_tensor(y5[:, :], mixed, bmix[:, :], ALU.add).then_inc(mix_read, 1)
                    hold(dve, mix_read, n + 3)
                    s(nc.vector.scalar_tensor_tensor(y5[:, :], y5[:, :], 0.0, tile, ALU.max, ALU.add))
                    s.settle()
                    s(nc.vector.bn_stats(bn[:, 0, :], y5[:, :]))
                    s.settle()
                    nc.vector.bn_aggr(mv[:, 0, :], bn[:, 0, :]).then_inc(var5, 1)
                    hold(dve, dev5, n + 1)
                    s(nc.vector.reciprocal(rstd[:, 0:1], dev[:, 0:1]))
                    s.settle()
                    nc.vector.tensor_scalar(tile, y5[:, :], mv[:, 0, 0:1], rstd[:, 0:1], ALU.subtract, ALU.mult
                                            ).then_inc(x3_ready, 1)
                    assert s.n == STEP_Y, s.n

                def second_input(n):
                    s = Steps(dve, step_ht, n * STEP_HT, (const_step, CONSTS))
                    hold(dve, abc_psum, n + 1)
                    s(nc.vector.tensor_tensor(ht[:, :], banks[:, 6, 0:D], big_d[:, ds(n * D, D)], ALU.add))
                    s.settle()
                    s(nc.vector.scalar_tensor_tensor(ht[:, :], banks[:, 6, D:2 * D], amp[:, ds(n, 1)], ht[:, :],
                                                     ALU.mult, ALU.add))
                    s.settle()
                    nc.vector.scalar_tensor_tensor(ht[:, :], banks[:, 7, 0:D], att[:, ds(n, 1)], ht[:, :],
                                                   ALU.mult, ALU.add).then_inc(ht_ready, 1)
                    assert s.n == STEP_HT, s.n

                def finish(g):
                    s = Steps(dve, step_fin, g * STEP_FIN + STEP_FIN, (const_step, CONSTS))
                    hold(dve, evac_done, g + 2)
                    s(nc.vector.tensor_tensor(mean_sq, mean, mean, ALU.mult))
                    for i in range(GT):
                        at = mn_all[:, i * D:(i + 1) * D]
                        nc.vector.tensor_scalar(at, at, 0.0, has[:, ds(g * GT + i, 1)], ALU.max, ALU.mult)
                    s.settle()
                    s(nc.vector.tensor_tensor(var_all, var_all, mean_sq, ALU.subtract))
                    s.settle()
                    nc.vector.tensor_scalar(var_all, var_all, 0.0, EPS, ALU.max, ALU.add).then_inc(saved_ready, 1)
                    assert s.n == STEP_FIN, s.n

                def step(n, lagging, group, tile):
                    with dve.If(tile == 0):
                        finish(group)
                    lagging(2, norm)
                    lagging(1, second_input)

                between, last_group = pna_steps(dve, "pna_dve", step)

                def before(g, it):
                    s = Steps(dve, step5, g * STEP5, (const_step, CONSTS))
                    s(nc.vector.memset(run[:, :], 0.0))
                    s(nc.vector.memset(mn[:, :], -LOW))
                    s.settle()

                def body(g, it):
                    for r in range(RND):
                        hold(dve, m_ready, it * RND + (r + 1))
                        hold(dve, run_done, it * RND + (r + 1))
                        for i in range(GT):
                            hold(dve, land[r][i], it * 16 + 16)
                            last = nc.vector.tensor_tensor(z[:, r, i * D:(i + 1) * D], gath[:, r, i, :],
                                                           big_b[:, ds(g * GW + i * D, D)], ALU.add)
                        last.then_inc(z_ready, 1)
                        hold(dve, used, it * SLOTS + (r + 1) * GT + GT)
                        for i in range(GT):
                            at = mn[:, i * D:(i + 1) * D]
                            nc.vector.scalar_tensor_tensor(at, gath[:, r, i, :], stage[:, r, i, 1:2].bitcast(F32), at,
                                                           ALU.add, ALU.min).then_inc(used, 1)
                        hold(dve, z_ready, it * RND + (r + 1))
                        hold(dve, run_done, it * RND + (r + 2))
                        nc.vector.tensor_tensor(mx, mx, z[:, r, :], ALU.max)
                        nc.vector.scalar_tensor_tensor(part_sum, z[:, r, MP:GW], 0.0, part_sum, ALU.max, ALU.add
                                                       ).then_inc(run_done, 1)
                    between(g)

                def after(g, it):
                    s = Steps(dve, step5, g * STEP5, (const_step, CONSTS))
                    s.n = 2
                    hold(dve, used, it * SLOTS + SLOTS)
                    hold(dve, run_done, it * RND + RND)
                    hold(dve, quant_ready, g * GT + 1)
                    s(nc.vector.tensor_copy(mx_all, mx))
                    for i in range(GT - VT, GT):
                        nc.vector.tensor_scalar(mean[:, i * D:(i + 1) * D], part_sum[:, i * D - MP:(i + 1) * D - MP],
                                                deg_inv[:, ds(g * GT + i, 1)], None, ALU.mult)
                    s(nc.vector.tensor_tensor(mn_all, mn[:, :], big_b[:, ds(g * GW, GW)], ALU.add))
                    s.settle()
                    assert s.n == STEP5, s.n

                rounds(dve, "pna_dve", body, before, after)
                last_group()
                norm(NT - 2)
                second_input(NT - 1)
                norm(NT - 1)

            @block.scalar
            def _(act):
                act.sem_inc(m_ready, RND)
                act.sem_inc(evac_done, 1)
                act.sem_inc(quant_ready, 1)

                def norm(n):
                    hold(act, var5, n + 1)
                    nc.scalar.activation(dev[:, 0:1], mv[:, 0, 1:2], ACT.Sqrt, bias=eps[:, :]).then_inc(dev5, 1)

                def second_turned(n):
                    hold(act, htt_psum, n + 1)
                    nc.scalar.activation(htt[:, :], mixed, ACT.Relu).then_inc(htt_ready, 1)

                def step(n, lagging, group, tile):
                    hold(act, saved_ready, group + 1)
                    hold(act, t5_psum, n * 2 + 1)
                    nc.scalar.activation(quant[:, 0:3, :], saved[:, 0:3, ds(tile * D, D)], ACT.Copy)
                    nc.scalar.activation(quant[:, 3, :], saved[:, 3, ds(tile * D, D)], ACT.Sqrt).then_inc(quant_ready, 1)
                    lagging(2, norm)
                    for q in range(2):
                        hold(act, t5_psum, n * 2 + (q + 2))
                        nc.scalar.activation(aggt[:, 4 * q:4 * q + 4, :].rearrange("p c n -> p (c n)"), banks[:, 4 + q, :],
                                             ACT.Copy).then_inc(t5_read, 1)
                    lagging(1, second_turned)

                between, last_group = pna_steps(act, "pna_act", step)

                def body(g, it):
                    for r in range(RND):
                        hold(act, z_ready, it * RND + (r + 1))
                        hold(act, sums_done, it * RND + (r + 1))
                        m, sq, last_sq = summed[:, r, 0:MP], summed[:, r, MP:2 * MP], summed[:, r, 2 * MP:]
                        nc.scalar.activation(m, z[:, r, 0:MP], ACT.Relu)
                        nc.scalar.activation(last_sq, z[:, r, MP:GW], ACT.Relu).then_inc(m_ready, 1)
                        hold(act, m_ready, it * RND + (r + 3))
                        nc.scalar.activation(sq, m, ACT.Square)
                        nc.scalar.activation(last_sq, last_sq, ACT.Square).then_inc(sq_ready, 1)
                    between(g)

                def after(g, it):
                    hold(act, sums_final, g + 1)
                    hold(act, quant_ready, g * GT + 1)
                    for to, at, tiles in ((mean, 0, GT - VT), (var_all, MP, GT)):
                        for i in range(tiles):
                            last = nc.scalar.activation(to[:, i * D:(i + 1) * D], flat[:, at + i * D:at + (i + 1) * D],
                                                        ACT.Copy, scale=deg_inv[:, ds(g * GT + i, 1)])
                    last.then_inc(evac_done, 1)

                rounds(act, "pna_act", body, None, after)
                last_group()
                norm(NT - 2)
                second_turned(NT - 1)
                norm(NT - 1)

            @block.tensor
            def _(pe):
                pe.sem_inc(sums_done, RND)
                pe.sem_inc(t5_psum, 1)
                pe.wait_ge(w_in5, 80)
                pe.wait_ge(nothing_set, 1)

                def turn_second(n):
                    hold(pe, ht_ready, n + 2)
                    for k in range(2):
                        last = nc.tensor.transpose(banks[:, 5, k * P:(k + 1) * P], ht[:, k * P:(k + 1) * P], ident[:, :])
                    last.then_inc(htt_psum, 1)

                def second_product(n):
                    hold(pe, htt_ready, n + 1)
                    for k in range(2):
                        last = nc.tensor.matmul(mixed, htt[:, k * P:(k + 1) * P], wmix[:, k, :], start=k == 0, stop=k == 1)
                    last.then_inc(mix_psum, 1)

                def turn_aggregates(q):
                    for c in range(4):
                        last = nc.tensor.transpose(banks[:, 4 + q, c * P:(c + 1) * P],
                                                   quant[:, 2 * q + c // 2, (c % 2) * P:(c % 2 + 1) * P], ident[:, :])
                    last.then_inc(t5_psum, 1)

                def products(chunks):
                    for c in chunks:
                        nc.tensor.matmul(banks[:, 6, :], aggt[:, c, :], wpost[:, c, 0:2 * D], start=c == 0, stop=c == 7)
                        last = nc.tensor.matmul(banks[:, 7, 0:D], aggt[:, c, :], wpost[:, c, 2 * D:3 * D],
                                                start=c == 0, stop=c == 7)
                    return last

                def step(n, lagging, group, tile):
                    hold(pe, quant_ready, n + 2)
                    turn_aggregates(0)
                    hold(pe, mix_read, n + 1)
                    turn_aggregates(1)
                    hold(pe, ht_ready, n + 1)
                    hold(pe, t5_read, n * 2 + 1)
                    products(range(4))
                    hold(pe, t5_read, n * 2 + 2)
                    lagging(1, turn_second)
                    products(range(4, 6))
                    lagging(1, second_product)
                    products(range(6, 8)).then_inc(abc_psum, 1)

                between, last_group = pna_steps(pe, "pna_pe", step)

                def before(g, it):
                    hold(pe, evac_done, g + 1)
                    for b in range(SB):
                        nc.tensor.matmul(banks[:, b, :], nothing[:, 0:P], nothing[:, :], start=True, stop=False)

                def body(g, it):
                    for r in range(RND):
                        hold(pe, sq_ready, it * RND + (r + 1))
                        for b in range(SB):
                            last = nc.tensor.matmul(banks[:, b, :], ident[:, :], summed[:, r, b * 512:(b + 1) * 512],
                                                    start=False, stop=False)
                        last.then_inc(sums_done, 1)
                    between(g)

                def after(g, it):
                    for b in range(SB):
                        last = nc.tensor.matmul(banks[:, b, :], nothing[:, 0:P], nothing[:, :], start=False, stop=True)
                    last.then_inc(sums_final, 1)

                rounds(pe, "pna_pe", body, before, after)
                last_group()
                turn_second(NT - 1)
                second_product(NT - 1)
        late.close()

        late = ExitStack()
        psb6 = maker(late)
        wt6 = psb6("wt6", [P, WR, GTP, 2])
        w6 = psb6("w6", [P, 2, D])
        b6 = psb6("b6", [P, D])
        st = psb6("st", [P, 2, GTP])
        y6 = psb6("y6", [P, GT, D])
        block6_in = [sem(f"block6_in{i}") for i in range(WR)]
        x3_in = [sem(f"x3_in{n}") for n in range(NG)]
        w_in6, block_used6, st_ready, out6_psum, y6_ready, x4_ready, x4_out, step6 = (sem(n) for n in (
            "w_in6", "block_used6", "st_ready", "out6_psum", "y6_ready", "x4_ready", "x4_out", "step6"))
        var6, dev6 = sem("var6"), sem("dev6")
        STEP6 = 7

        with nc.Block() as block:
            @block.sync
            def _(sp):
                sp.sem_inc(block_used6, WR)
                load_blocks(sp, wt6, block6_in, block_used6)

            @block.tensor
            def _(pe):
                with pe.Fori(0, NG) as g:
                    hold(pe, st_ready, g * 4 + 4)
                    for b in range(NT):
                        if b % GT == 0:
                            pe.wait_ge(x3_in[b // GT], 16)
                        hold(pe, block6_in[b % WR], g * (16 * NT // WR) + 16 * (b // WR + 1))
                        for k in range(2):
                            for h in range(2):
                                last = nc.tensor.matmul(banks[:, 2 * k + h, 0:HGT], big_b[:, b * D + k * P:b * D + (k + 1) * P],
                                                        wt6[:, b % WR, h * HGT:(h + 1) * HGT, 0],
                                                        start=b == 0, stop=b == NT - 1)
                        last.then_inc(block_used6, 1)
                    pe.wait_ge(w_in6, 32)
                    hold(pe, st_ready, g * 4 + 8)
                    for i in range(GT):
                        hold(pe, y6_ready, g * GT + (i + (2 if i == 0 else 1)))
                        for k in range(2):
                            last = nc.tensor.matmul(banks[:, 4 + i % 2, 0:D], st[:, k, i * P:(i + 1) * P], w6[:, k, :],
                                                    start=k == 0, stop=k == 1)
                        last.then_inc(out6_psum, 1)

            @block.scalar
            def _(act):
                act.sem_inc(st_ready, 4)
                act.sem_inc(out6_psum, 1)
                with act.Fori(0, NG) as g:
                    hold(act, block_used6, g * NT + (NT + WR))
                    hold(act, out6_psum, g * GT + 1)
                    for k in range(2):
                        for h in range(2):
                            nc.scalar.activation(st[:, k, h * HGT:(h + 1) * HGT], banks[:, 2 * k + h, 0:HGT], ACT.Copy
                                                 ).then_inc(st_ready, 1)
                    deviation(act, g, var6, dev6)

            @block.vector
            def _(dve):
                dve.wait_ge(w_in6, 32)
                dve.sem_inc(y6_ready, 2)
                dve.sem_inc(x4_ready, 1)
                with dve.Fori(0, NG) as g:
                    s = Steps(dve, step6, g * STEP6, (const_step, CONSTS))
                    hold(dve, x4_ready, g * GT + 1)
                    for i in range(GT):
                        hold(dve, out6_psum, g * GT + (i + 2))
                        nc.vector.tensor_tensor(y6[:, i, :], banks[:, 4 + i % 2, 0:D], b6[:, :], ALU.add
                                                ).then_inc(y6_ready, 1)
                    hold(dve, y6_ready, g * GT + (GT + 2))
                    s(nc.vector.scalar_tensor_tensor(y6[:, :, :].rearrange("p t d -> p (t d)"),
                                                     y6[:, :, :].rearrange("p t d -> p (t d)"), 0.0,
                                                     big_c[:, ds(g * GW, GW)], ALU.max, ALU.add))
                    layer_norm(dve, s, lambda i: y6[:, i, :], lambda i: big_d[:, ds(g * GW + i * D, D)],
                               lambda i, ins: ins.then_inc(x4_ready, 1), g, var6, dev6)
                    assert s.n == STEP6, s.n

            @block.gpsimd
            def _(pool):
                for n in range(NG):
                    pool.dma_start(big_b[:, n * GW:(n + 1) * GW].rearrange("p (t d) -> p t d", t=GT),
                                   x3_dram[n * GTP:(n + 1) * GTP, :].rearrange("(t p) d -> p t d", p=P)).then_inc(x3_in[n], 16)
                pool.dma_start(w6[:, :, :], L3_W.rearrange("(k p) m -> p k m", p=P)).then_inc(w_in6, 16)
                pool.dma_start(b6[:, :], L3_b.to_broadcast([P, D])).then_inc(w_in6, 16)
                for t in range(NT):
                    pool.wait_ge(x4_ready, t + 2)
                    scatter(out, node_of_rank[:, t, 0:1], big_d[:, t * D:(t + 1) * D], bounds_check=N - 1,
                            oob_is_err=False).then_inc(x4_out, 16)
                pool.wait_ge(x4_out, 16 * NT)
        late.close()


def kernel(x, src, dst, edge_weight, L0_gnn_W1, L0_gnn_b1, L0_gnn_W2, L0_gnn_b2, L1_gnn_W_conv, L1_gnn_b_conv,
           L1_gnn_W1, L1_gnn_b1, L1_gnn_W2, L1_gnn_b2, L2_gnn_pre_W, L2_gnn_pre_b, L2_gnn_post_W, L2_gnn_post_b,
           L2_gnn_mix_W, L2_gnn_mix_b, L3_gnn_W, L3_gnn_b):
    import numpy as np
    from concourse import bacc
    from concourse.bass_utils import run_bass_kernel_spmd

    def rows(a, n, fill):
        a = np.asarray(a)
        return np.concatenate([a, np.full((n - a.shape[0],) + a.shape[1:], fill, a.dtype)])

    xp = rows(x, NP, 0)
    line = lambda a: np.asarray(a).reshape(1, -1)
    arrays = {
        "x": xp, "xT": np.ascontiguousarray(xp.T),
        "src": rows(src, EP, NP).reshape(P, EC), "dst": rows(dst, EP, NP).reshape(P, EC),
        "w": rows(edge_weight, EP, 0).reshape(P, EC),
        "L0_W1": L0_gnn_W1, "L0_b1": np.ascontiguousarray(np.asarray(L0_gnn_b1).reshape(-1, P).T),
        "L0_W2": L0_gnn_W2, "L0_b2": line(L0_gnn_b2),
        "L1_Wc": L1_gnn_W_conv, "L1_bc": np.asarray(L1_gnn_b_conv).reshape(-1, 1),
        "L1_W1T": np.ascontiguousarray(np.asarray(L1_gnn_W1).T), "L1_b1": np.asarray(L1_gnn_b1).reshape(-1, 1),
        "L1_W2T": np.ascontiguousarray(np.asarray(L1_gnn_W2).T), "L1_b2": line(L1_gnn_b2),
        "L2_preW": L2_gnn_pre_W, "L2_preb": line(L2_gnn_pre_b), "L2_postW": L2_gnn_post_W,
        "L2_postb": line(L2_gnn_post_b), "L2_mixW": L2_gnn_mix_W, "L2_mixb": line(L2_gnn_mix_b),
        "L3_W": L3_gnn_W, "L3_b": line(L3_gnn_b),
    }
    arrays = {f"in_{k}": np.ascontiguousarray(v) for k, v in arrays.items()}
    nc = bacc.Bacc("TRN2", target_bir_lowering=False, num_devices=1)
    args = [nc.dram_tensor(k, v.shape, mybir.dt.from_np(v.dtype), kind="ExternalInput").ap() for k, v in arrays.items()]
    out = nc.dram_tensor("out", (N, D), F32, kind="ExternalOutput").ap()
    build(nc, *args, out)
    result = run_bass_kernel_spmd(nc, [arrays], core_ids=[0])
    return result.results[0]["out"]
```
